# Optimizing a Trainium2 kernel written in Bass

```python
import numpy as np
import jax
import jax.numpy as jnp

def _softmax(x, axis=-1):
    return jax.nn.softmax(x, axis=axis)

def _gelu(x):
    return jax.nn.gelu(x, approximate=True)

def _silu(x):
    return jax.nn.silu(x)

def _sigmoid(x):
    return jax.nn.sigmoid(x)

def _layernorm(x, axis=-1, eps=1e-05):
    m = jnp.mean(x, axis=axis, keepdims=True)
    v = jnp.var(x, axis=axis, keepdims=True)
    return (x - m) / jnp.sqrt(v + eps)

def _scatter_add(tgt, idx, src, axis=0):
    return tgt.at[idx].add(src)

def _segment_sum(src, seg, n):
    return jax.ops.segment_sum(src, seg, n)
kernel_name = 'mk_adaln_d1_jaxref_r8_15ef0c'

def setup_inputs(seed: int=0):
    np.random.seed(seed)
    _w = jnp.asarray

    def _L0_attn_setup():
        import jax, jax.numpy as jnp
        import numpy as np
        B, L, E = (4, 256, 128)
        H, DK = (16, 64)
        key = jax.random.key(seed)
        k1, k2, k3, k4, k5 = jax.random.split(key, 5)
        s_in = 1.0 / np.sqrt(E)
        s_fc = 1.0 / np.sqrt(H * DK)
        return {'X': jax.random.normal(k1, (B, L, E), dtype=jnp.float32), 'W_qkv': jax.random.uniform(k2, (E, 3 * H * DK), minval=-s_in, maxval=s_in, dtype=jnp.float32), 'b_qkv': jax.random.uniform(k3, (3 * H * DK,), minval=-s_in, maxval=s_in, dtype=jnp.float32), 'W_fc': jax.random.uniform(k4, (H * DK, E), minval=-s_fc, maxval=s_fc, dtype=jnp.float32), 'b_fc': jax.random.uniform(k5, (E,), minval=-s_fc, maxval=s_fc, dtype=jnp.float32)}
    _L0_attn_in = _L0_attn_setup()

    def _L0_ffn_setup():
        import jax, jax.numpy as jnp
        import numpy as np
        EPS_LN = 1e-05
        EPS_GATE = 1e-08

        def layer_norm(x, gamma, beta):
            mu = jnp.mean(x, axis=-1, keepdims=True)
            var = jnp.mean(jnp.square(x - mu), axis=-1, keepdims=True)
            return (x - mu) * jax.lax.rsqrt(var + EPS_LN) * gamma + beta
        key = jax.random.key(seed)
        ks = jax.random.split(key, 8)
        B, S, D, E, H = (4, 512, 128, 4, 256)
        s_in = 1.0 / np.sqrt(D)
        s_h = 1.0 / np.sqrt(H)
        return {'h': jax.random.normal(ks[0], (B, S, D), dtype=jnp.float32), 'router_w': jax.random.uniform(ks[1], (E, D), jnp.float32, -s_in, s_in), 'rn_g': jnp.ones((D,), jnp.float32), 'rn_b': jnp.zeros((D,), jnp.float32), 'w1': jax.random.uniform(ks[2], (E, D, H), jnp.float32, -s_in, s_in), 'ln_g': jnp.ones((E, H), jnp.float32), 'ln_b': jnp.zeros((E, H), jnp.float32), 'w2': jax.random.uniform(ks[3], (E, H, D), jnp.float32, -s_h, s_h), 'on_g': jnp.ones((D,), jnp.float32), 'on_b': jnp.zeros((D,), jnp.float32)}
    _L0_ffn_in = _L0_ffn_setup()
    _L0_c = _w((lambda *s: np.random.randn(*s).astype(np.float32) * 0.05)(4, 128))
    _L0_wmod = _w((lambda *s: np.random.randn(*s).astype(np.float32) * 0.05)(128, 6 * 128) * 128 ** (-0.5))
    _d = {'L0_attn_X': _L0_attn_in['X'], 'L0_attn_W_qkv': _L0_attn_in['W_qkv'], 'L0_attn_b_qkv': _L0_attn_in['b_qkv'], 'L0_attn_W_fc': _L0_attn_in['W_fc'], 'L0_attn_b_fc': _L0_attn_in['b_fc'], 'L0_ffn_router_w': _L0_ffn_in['router_w'], 'L0_ffn_rn_g': _L0_ffn_in['rn_g'], 'L0_ffn_rn_b': _L0_ffn_in['rn_b'], 'L0_ffn_w1': _L0_ffn_in['w1'], 'L0_ffn_ln_g': _L0_ffn_in['ln_g'], 'L0_ffn_ln_b': _L0_ffn_in['ln_b'], 'L0_ffn_w2': _L0_ffn_in['w2'], 'L0_ffn_on_g': _L0_ffn_in['on_g'], 'L0_ffn_on_b': _L0_ffn_in['on_b'], 'L0_c': _L0_c, 'L0_wmod': _L0_wmod}
    _x0 = _d['L0_attn_X']
    _d['L0_attn_X'] = jax.random.normal(jax.random.fold_in(jax.random.key(seed), 1), (4, 1024, 128), dtype=_x0.dtype)
    del _x0
    return _d

def reference(L0_attn_X, L0_attn_W_qkv, L0_attn_b_qkv, L0_attn_W_fc, L0_attn_b_fc, L0_ffn_router_w, L0_ffn_rn_g, L0_ffn_rn_b, L0_ffn_w1, L0_ffn_ln_g, L0_ffn_ln_b, L0_ffn_w2, L0_ffn_on_g, L0_ffn_on_b, L0_c, L0_wmod):

    def _L0_attn_ref(X, W_qkv, b_qkv, W_fc, b_fc):
        import jax, jax.numpy as jnp
        import numpy as np
        B, L, E = (4, 256, 128)
        H, DK = (16, 64)
        b, l, _ = X.shape
        qkv = X @ W_qkv + b_qkv
        qkv = qkv.reshape(b, l, H, 3 * DK).transpose(0, 2, 1, 3)
        Q, K, V = jnp.split(qkv, 3, axis=-1)
        scores = jnp.einsum('bhqd,bhkd->bhqk', Q, K) / np.sqrt(DK).astype(np.float32)
        attn = jax.nn.softmax(scores, axis=-1)
        out = jnp.einsum('bhqk,bhkv->bhqv', attn, V)
        out = out.transpose(0, 2, 1, 3).reshape(b, l, H * DK)
        return out @ W_fc + b_fc

    def _L0_ffn_ref(h, router_w, rn_g, rn_b, w1, ln_g, ln_b, w2, on_g, on_b):
        import jax, jax.numpy as jnp
        import numpy as np
        EPS_LN = 1e-05
        EPS_GATE = 1e-08

        def layer_norm(x, gamma, beta):
            mu = jnp.mean(x, axis=-1, keepdims=True)
            var = jnp.mean(jnp.square(x - mu), axis=-1, keepdims=True)
            return (x - mu) * jax.lax.rsqrt(var + EPS_LN) * gamma + beta
        D = h.shape[-1]
        h_norm = layer_norm(h, rn_g, rn_b)
        g = jax.nn.softmax(jnp.einsum('bsd,ed->bse', h_norm, router_w), axis=-1)
        top2_w, top2_idx = jax.lax.top_k(g, 2)
        top2_w = top2_w / (jnp.sum(top2_w, axis=-1, keepdims=True) + EPS_GATE)
        hid = jnp.einsum('bsd,edh->bseh', h, w1)
        hid = jax.nn.relu(layer_norm(hid, ln_g, ln_b))
        expert_out = jnp.einsum('bseh,ehd->bsed', hid, w2)
        idx = jnp.broadcast_to(top2_idx[..., None], top2_idx.shape + (D,))
        top2_out = jnp.take_along_axis(expert_out, idx, axis=-2)
        out = jnp.sum(top2_out * top2_w[..., None], axis=-2)
        return layer_norm(out, on_g, on_b)
    x = L0_attn_X
    mod = (_silu(L0_c) @ L0_wmod).reshape(L0_c.shape[0], 6, 1, -1)
    sa, ca, ga, sb, cb, gb = (mod[:, 0], mod[:, 1], mod[:, 2], mod[:, 3], mod[:, 4], mod[:, 5])
    ga = (2 * (ga >= 0) - 1) * jnp.maximum(jnp.abs(ga), 0.25)
    gb = (2 * (gb >= 0) - 1) * jnp.maximum(jnp.abs(gb), 0.25)
    h = _layernorm(x, axis=-1) * (1 + ca) + sa
    x = x + ga * _L0_attn_ref(h, L0_attn_W_qkv, L0_attn_b_qkv, L0_attn_W_fc, L0_attn_b_fc)
    h = _layernorm(x, axis=-1) * (1 + cb) + sb
    x = x + gb * _L0_ffn_ref(h, L0_ffn_router_w, L0_ffn_rn_g, L0_ffn_rn_b, L0_ffn_w1, L0_ffn_ln_g, L0_ffn_ln_b, L0_ffn_w2, L0_ffn_on_g, L0_ffn_on_b)
    return x

_drawn_inputs = setup_inputs


def setup_inputs(seed=0):
    import zlib

    import numpy as np

    out = dict(_drawn_inputs(seed))
    spreads = {'L0_ffn_rn_g': (1.0, 0.542),
     'L0_ffn_rn_b': (0.0, 0.306),
     'L0_ffn_ln_g': (1.0, 0.6),
     'L0_ffn_ln_b': (0.0, 1.017),
     'L0_ffn_on_g': (1.0, 0.6),
     'L0_ffn_on_b': (0.0, 0.963)}
    factors = {'L0_attn_W_qkv': 8.0,
     'L0_attn_b_qkv': 3.848,
     'L0_attn_W_fc': 4.353,
     'L0_attn_b_fc': 29.484}
    for name, (base, spread) in spreads.items():
        noise = np.random.default_rng([zlib.crc32(name.encode()), seed]).standard_normal(out[name].shape)
        drawn = base * np.exp(spread * noise) if base else spread * noise
        out[name] = jnp.asarray(drawn.astype(out[name].dtype))
    for name, factor in factors.items():
        out[name] = (out[name] * factor).astype(out[name].dtype)
    return out
```

```python
from contextlib import ExitStack

import concourse.bass as bass
from concourse import mybir

F32 = mybir.dt.float32
F32R = mybir.dt.float32r
ACT = mybir.ActivationFunctionType
ALU = mybir.AluOpType
AX = mybir.AxisListType.X

P = 128
EPS = 1e-5
EPS_GATE = 1e-8
GUARD = 0.25
ds = bass.ds


def flat(ap):
    return ap.rearrange("p a b -> p (a b)")


def wait(eng, sem, value):
    if not isinstance(value, int) or value > 0:
        eng.wait_ge(sem, value)


def wait_first(eng, sem, value, vector, spot):
    wait(eng, sem, value)
    vector.tensor_copy(spot[0:1, 0:1], spot[0:1, 1:2])


class Shared:
    pass


def build(nc, X, W_qkv, b_qkv, W_fc, b_fc, router_w, rn_g, rn_b, w1, ln_g, ln_b, w2, on_g, on_b, c, wmod, out):
    B, L, E = X.shape
    HD = W_fc.shape[0]
    DK = 64
    H = HD // DK
    assert E == P and L == 1024 and H == 16 and B == 4
    with ExitStack() as ctx:
        g = Shared()
        g.X, g.W_qkv, g.W_fc, g.out = X, W_qkv, W_fc, out
        g.small = (b_qkv, b_fc, router_w, rn_g, rn_b, ln_g, ln_b, on_g, on_b, c, wmod)
        g.w1, g.w2 = w1, w2
        g.B, g.L, g.E, g.H = B, L, E, H

        def sb(name, shape, dt=F32):
            return ctx.enter_context(nc.sbuf_tensor(name, shape, dt))

        g.ident = sb("ident", [P, P])
        g.ones = sb("ones", [P, P])
        g.eps = sb("eps", [P, 1])
        g.attnT = sb("attnT", [P, B * L])
        g.vecT = sb("vecT", [P, 64])
        g.modT = sb("modT", [P, 6, B])
        g.gaT = sb("gaT", [P, B])
        g.gacT = sb("gacT", [P, B])
        g.mod_rep = sb("mod_rep", [P, 4, B, P])
        g.rw = sb("rw", [P, 8])
        g.rw_sum = sb("rw_sum", [P, 8])
        with ExitStack() as two:
            g.hT = two.enter_context(nc.sbuf_tensor("hT", [P, B * L], F32))
            g.hT_hi = two.enter_context(nc.sbuf_tensor("hT_hi", [P, B * L], F32R))
            g.hT_lo = two.enter_context(nc.sbuf_tensor("hT_lo", [P, B * L], F32R))
            setup_stage(nc, g)
            attention_stage(nc, g)
        ffn_stage(nc, g)


C_LNG, C_LNB, C_RNG, C_RNB, C_BFC, C_RW, C_C, C_BQ, C_BK, C_BV = 0, 8, 16, 17, 18, 19, 23, 27, 35, 43
N_VEC = 51


def setup_stage(nc, g):
    b_qkv, b_fc, router_w, rn_g, rn_b, ln_g, ln_b, on_g, on_b, c, wmod = g.small
    B, L = g.B, g.L
    GROUPS = B * L // 512
    with ExitStack() as ctx:
        def sb(name, shape, dt=F32):
            return ctx.enter_context(nc.sbuf_tensor(name, shape, dt))

        def sem(name):
            return ctx.enter_context(nc.semaphore(name))

        rows = sb("rows", [64, P])
        on_row = sb("on_row", [1, 2 * P])
        wm = sb("wm", [P, 6 * P])
        wfc = sb("wfc_all", [P, 8, P])
        on_rep = sb("on_rep", [P, 2, P])
        spot = sb("spot", [1, 2])
        silu = sb("silu", [P, 4, B])
        silu_rep = sb("silu_rep", [P, B, P])
        tmp = sb("tmp", [P, 3, B, P])
        tmpT = sb("tmpT", [P, 4, B])
        xg = sb("xg", [P, 2, 4, P])
        xn = sb("xn", [P, 4, P])
        st = sb("st", [P, 4, 6])
        mv = sb("mv", [P, 4, 2])
        sd = sb("sd", [P, 4])
        rs = sb("rs", [P, 4])
        ps_a = ctx.enter_context(nc.psum_tensor("ps_a", [P, 512], F32))
        ps_m = ctx.enter_context(nc.psum_tensor("ps_m", [P, B, 512], F32))
        ps_x = ctx.enter_context(nc.psum_tensor("ps_x", [P, 512], F32))
        ps_c = ctx.enter_context(nc.psum_tensor("ps_c", [P, 512], F32))
        ps_b = ctx.enter_context(nc.psum_tensor("ps_b", [P, 512], F32))

        s_rows, s_on, s_wm, s_wfc = sem("s_rows"), sem("s_on"), sem("s_wm"), sem("s_wfc")
        s_x = [sem("s_x0"), sem("s_x1")]
        s_id, s_const = sem("s_id"), sem("s_const")
        s_vec, s_vecT, s_exp = sem("s_vec"), sem("s_vecT"), sem("s_exp")
        s_v = sem("s_v")
        s_mod, s_modrep, s_onrep, s_bv, s_rwsum = (sem("s_mod"), sem("s_modrep"), sem("s_onrep"),
                                                   sem("s_bv"), sem("s_rwsum"))
        s_st, s_mv, s_sd, s_rs, s_xn, s_xt = sem("s_st"), sem("s_mv"), sem("s_sd"), sem("s_rs"), sem("s_xn"), sem("s_xt")
        s_h, s_hi, s_lo = sem("s_h"), sem("s_hi"), sem("s_lo")

        xv = g.X.rearrange("b l e -> (b l) e").rearrange("(t p) e -> p t e", p=P)
        N_ROW_DMAS = 13
        SETUP_V = 26

        block = ctx.enter_context(nc.Block())

        @block.sync
        def _(sp):
            sp.dma_start(rows[C_LNG:C_LNG + 8, :], ln_g.rearrange("e (a h) -> (e a) h", h=P)).then_inc(s_rows, 16)
            sp.dma_start(rows[C_LNB:C_LNB + 8, :], ln_b.rearrange("e (a h) -> (e a) h", h=P)).then_inc(s_rows, 16)
            sp.dma_start(rows[C_RNG:C_RNG + 1, :], rn_g.rearrange("(a h) -> a h", a=1)).then_inc(s_rows, 16)
            sp.dma_start(rows[C_RNB:C_RNB + 1, :], rn_b.rearrange("(a h) -> a h", a=1)).then_inc(s_rows, 16)
            sp.dma_start(rows[C_BFC:C_BFC + 1, :], b_fc.rearrange("(a h) -> a h", a=1)).then_inc(s_rows, 16)
            sp.dma_start(rows[C_RW:C_RW + 4, :], router_w).then_inc(s_rows, 16)
            sp.dma_start(rows[C_C:C_C + 4, :], c).then_inc(s_rows, 16)
            bv = b_qkv.rearrange("(p h t d) -> t p h d", h=2, t=3, d=64)
            for col, t in ((C_BQ, 0), (C_BK, 1), (C_BV, 2)):
                for hh in range(2):
                    sp.dma_start(rows[col:col + 8, 64 * hh:64 * hh + 64], bv[t, :, hh, :]).then_inc(s_rows, 16)
            sp.dma_start(on_row[0:1, 0:P], on_g.rearrange("(a h) -> a h", a=1)).then_inc(s_on, 16)
            sp.dma_start(on_row[0:1, P:2 * P], on_b.rearrange("(a h) -> a h", a=1)).then_inc(s_on, 16)
            sp.dma_start(wm[:, :], wmod).then_inc(s_wm, 16)
            sp.dma_start(wfc[:, :, :], g.W_fc.rearrange("(k p) e -> p k e", p=P)).then_inc(s_wfc, 16)
            with sp.Fori(0, GROUPS // 2) as j:
                for u in range(2):
                    wait(sp, s_xn, 2 * j)
                    sp.dma_start(xg[:, u, :, :], xv[:, ds(j * 8 + 4 * u, 4), :]).then_inc(s_x[u], 16)

        @block.gpsimd
        def _(pool):
            nc.gpsimd.memset(g.ident[:, :], 0.0).then_inc(s_id, 1)
            nc.gpsimd.memset(g.ones[:, :], 1.0).then_inc(s_const, 1)
            nc.gpsimd.memset(g.eps[:, :], EPS).then_inc(s_const, 1)
            pool.wait_ge(s_id, 1)
            nc.gpsimd.affine_select(out=g.ident[:, :], in_=g.ident[:, :], compare_op=ALU.not_equal, fill=1.0,
                                    base=0, pattern=[[-1, P]], channel_multiplier=1).then_inc(s_id, 1)
            nc.gpsimd.memset(g.attnT[:, :], 0.0)

        @block.scalar
        def _(act):
            act.wait_ge(s_vecT, 1)
            nc.scalar.activation(silu[:, 0, :], g.vecT[:, C_C:C_C + 4], ACT.Exp, scale=-1.0).then_inc(s_exp, 1)
            with act.Fori(0, GROUPS) as n:
                act.wait_ge(s_mv, n + 1)
                act.wait_ge(s_const, 2)
                nc.scalar.activation(sd[:, :], mv[:, :, 1], ACT.Sqrt, bias=g.eps[:, 0:1]).then_inc(s_sd, 1)

        @block.vector
        def _(dve):
            done = [0]

            def link(ins):
                done[0] += 1
                ins.then_inc(s_v, 1)
                dve.wait_ge(s_v, done[0])

            V = nc.vector
            link(V.memset(spot[:, :], 0.0))
            dve.wait_ge(s_vec, 1)
            V.tensor_copy(g.vecT[:, 0:N_VEC], ps_a[:, 0:N_VEC]).then_inc(s_vecT, 1)
            dve.wait_ge(s_vecT, 1)
            dve.wait_ge(s_exp, 1)
            link(V.tensor_scalar_add(silu[:, 1, :], silu[:, 0, :], 1.0))
            link(V.reciprocal(silu[:, 2, :], silu[:, 1, :]))
            link(V.tensor_tensor(silu[:, 3, :], silu[:, 2, :], g.vecT[:, C_C:C_C + 4], ALU.mult))
            link(V.tensor_copy(silu_rep[:, :, :], silu[:, 3, :].unsqueeze(2).to_broadcast([P, B, P])))
            link(V.tensor_scalar(g.rw[:, 0:4], g.vecT[:, C_RW:C_RW + 4], g.vecT[:, C_RNG:C_RNG + 1], None, ALU.mult))
            link(V.tensor_scalar(g.rw[:, 4:8], g.vecT[:, C_RW:C_RW + 4], g.vecT[:, C_RNB:C_RNB + 1], None, ALU.mult))
            dve.wait_ge(s_mod, 1)
            link(V.tensor_copy(g.modT[:, :, :], ps_c[:, 0:24].rearrange("p (a b) -> p a b", a=6)))
            link(V.tensor_scalar_add(g.modT[:, 1, :], g.modT[:, 1, :], 1.0))
            ga = g.modT[:, 2, :]
            link(V.scalar_tensor_tensor(tmpT[:, 0, :], ga, -1.0, ga, op0=ALU.mult, op1=ALU.max))
            link(V.tensor_scalar_max(tmpT[:, 1, :], tmpT[:, 0, :], GUARD))
            link(V.tensor_scalar(tmpT[:, 2, :], ga, 0.0, 2.0, ALU.is_ge, ALU.mult))
            link(V.scalar_tensor_tensor(g.gaT[:, :], tmpT[:, 2, :], 1.0, tmpT[:, 1, :], op0=ALU.subtract, op1=ALU.mult))
            dve.wait_ge(s_bv, 1)
            dve.wait_ge(s_rwsum, 1)
            link(V.tensor_tensor(tmpT[:, 3, 0:1], ps_b[:, 0:1], g.vecT[:, C_BFC:C_BFC + 1], ALU.add))
            link(V.tensor_scalar(g.gacT[:, :], g.gaT[:, :], tmpT[:, 3, 0:1], None, ALU.mult))
            link(V.tensor_copy(g.rw_sum[:, :], ps_b[:, 8:16]))
            dve.wait_ge(s_onrep, 1)
            link(V.tensor_copy(flat(on_rep[:, :, :]), ps_x[:, 0:2 * P]))
            dve.wait_ge(s_modrep, 1)
            link(V.tensor_copy(g.mod_rep[:, 1, :, :], ps_m[:, :, 0:P]))
            link(V.tensor_scalar_add(g.mod_rep[:, 0, :, :], ps_m[:, :, P:2 * P], 1.0))
            link(V.tensor_copy(tmp[:, 0, :, :], ps_m[:, :, 2 * P:3 * P]))
            gb = tmp[:, 0, :, :]
            link(V.scalar_tensor_tensor(tmp[:, 1, :, :], gb, -1.0, gb, op0=ALU.mult, op1=ALU.max))
            link(V.tensor_scalar_max(tmp[:, 1, :, :], tmp[:, 1, :, :], GUARD))
            link(V.tensor_scalar(tmp[:, 2, :, :], gb, 0.0, 2.0, ALU.is_ge, ALU.mult))
            link(V.scalar_tensor_tensor(tmp[:, 0, :, :], tmp[:, 2, :, :], 1.0, tmp[:, 1, :, :], op0=ALU.subtract, op1=ALU.mult))
            link(V.tensor_tensor(g.mod_rep[:, 2, :, :], tmp[:, 0, :, :], on_rep[:, 0:1, :].to_broadcast([P, B, P]), ALU.mult))
            V.tensor_tensor(g.mod_rep[:, 3, :, :], tmp[:, 0, :, :], on_rep[:, 1:2, :].to_broadcast([P, B, P]), ALU.mult).then_inc(s_v, 1)

            with dve.Fori(0, GROUPS // 2) as j:
                for u in range(2):
                    n = 2 * j + u
                    b = j
                    cols = ds(n * 512, 512)
                    dve.wait_ge(s_x[u], 16 * (j + 1))
                    for i in range(4):
                        last = V.bn_stats(st[:, i, :], xg[:, u, i, :])
                    last.then_inc(s_st, 1)
                    wait_first(dve, s_st, n + 1, V, spot)
                    for i in range(4):
                        last = V.bn_aggr(mv[:, i, :], st[:, i, :])
                    last.then_inc(s_mv, 1)
                    dve.wait_ge(s_sd, n + 1)
                    V.reciprocal(rs[:, :], sd[:, :]).then_inc(s_rs, 1)
                    dve.wait_ge(s_rs, n + 1)
                    dve.wait_ge(s_mv, n + 1)
                    wait(dve, s_xt, n)
                    for i in range(4):
                        last = V.tensor_scalar(xn[:, i, :], xg[:, u, i, :], mv[:, i, 0:1], rs[:, i:i + 1],
                                               ALU.subtract, ALU.mult)
                    last.then_inc(s_xn, 1)
                    dve.wait_ge(s_xt, n + 1)
                    V.tensor_scalar(g.hT[:, cols], ps_x[:, :], g.modT[:, 1, ds(b, 1)], g.modT[:, 0, ds(b, 1)],
                                    ALU.mult, ALU.add).then_inc(s_h, 1)
                    dve.wait_ge(s_h, n + 1)
                    V.tensor_scalar(g.hT_hi[:, cols], g.hT[:, cols], 1.0, None, ALU.mult).then_inc(s_hi, 1)
                    dve.wait_ge(s_hi, n + 1)
                    V.tensor_tensor(g.hT_lo[:, cols], g.hT[:, cols], g.hT_hi[:, cols].bitcast(F32), ALU.subtract).then_inc(s_lo, 1)

        @block.tensor
        def _(pe):
            T = nc.tensor
            pe.wait_ge(s_id, 2)
            pe.wait_ge(s_const, 2)
            pe.wait_ge(s_rows, 16 * N_ROW_DMAS)
            T.transpose(ps_a[:, 0:N_VEC], rows[0:N_VEC, :], g.ident[0:N_VEC, 0:N_VEC]).then_inc(s_vec, 1)
            pe.wait_ge(s_on, 32)
            T.matmul(ps_x[:, 0:2 * P], g.ones[0:1, :], on_row[0:1, :], start=True, stop=True).then_inc(s_onrep, 1)
            pe.wait_ge(s_vecT, 1)
            pe.wait_ge(s_wfc, 16)
            for k in range(8):
                last = T.matmul(ps_b[:, 0:1], wfc[:, k, :], g.vecT[:, C_BV + k:C_BV + k + 1],
                                start=(k == 0), stop=(k == 7))
            last.then_inc(s_bv, 1)
            pe.wait_ge(s_wm, 16)
            pe.wait_ge(s_v, 4)
            for k in range(6):
                last = T.matmul(ps_c[:, 4 * k:4 * k + 4], wm[:, k * P:(k + 1) * P], silu[:, 3, :], start=True, stop=True)
            last.then_inc(s_mod, 1)
            pe.wait_ge(s_v, 7)
            T.matmul(ps_b[:, 8:16], g.ones[:, :], g.rw[:, :], start=True, stop=True).then_inc(s_rwsum, 1)
            for b in range(B):
                last = T.matmul(ps_m[:, b, 0:3 * P], silu_rep[:, b, :], wm[:, 3 * P:6 * P], start=True, stop=True)
            last.then_inc(s_modrep, 1)
            pe.wait_ge(s_v, SETUP_V)
            with pe.Fori(0, GROUPS) as n:
                pe.wait_ge(s_xn, n + 1)
                wait(pe, s_h, n)
                for i in range(4):
                    last = T.transpose(ps_x[:, i * P:(i + 1) * P], xn[:, i, :], g.ident[:, :])
                last.then_inc(s_xt, 1)


def attention_stage(nc, g):
    B, L, H = g.B, g.L, g.H
    NP = B * H // 2
    PAIRS = H // 2
    SCALE = 0.125
    with ExitStack() as ctx:
        def sb(name, shape, dt=F32):
            return ctx.enter_context(nc.sbuf_tensor(name, shape, dt))

        def psum(name, shape):
            return ctx.enter_context(nc.psum_tensor(name, shape, F32))

        def sem(name):
            return ctx.enter_context(nc.semaphore(name))

        QA = sb("QA", [P, 2, 2, L], F32R)
        QB = sb("QB", [P, 2, 2, L], F32R)
        KA = sb("KA", [P, 2, 2, L], F32R)
        KB = sb("KB", [P, 2, 2, L], F32R)
        V = sb("V", [P, 2, 8, P])
        PR = sb("PR", [P, 8, 2, 512])
        ACC = sb("ACC", [P, 2, 2, 512])
        Wraw = sb("Wraw", [P, 2, 2, 3, 64])
        Whi = sb("Whi", [P, 2, 2, 64], F32R)
        Wlo = sb("Wlo", [P, 2, 2, 64], F32R)
        bias = sb("bias", [P, 2, 2])
        Wfc = sb("Wfc", [P, 2, P])
        hcur = sb("hcur", [P, L])
        Oraw = sb("Oraw", [P, 512])
        R = sb("R", [P, 512])
        On = sb("On", [P, 512])
        NM = sb("NM", [P, 2, 2, 4])
        mask = sb("mask", [P, 4, P])

        ps_s = psum("ps_s", [P, 2, 2, 512])
        ps_mx = psum("ps_mx", [P, 2 * 512])
        ps_o = psum("ps_o", [P, 512])
        ps_w = psum("ps_w", [P, 512])

        s_init = sem("a_init")
        s_mask = sem("a_mask")
        wraw_in, hcur_in, wfc_in = [sem("wraw_in0"), sem("wraw_in1")], sem("hcur_in"), [sem("wfc_in0"), sem("wfc_in1")]
        kdup, qdup = [sem("kdup0"), sem("kdup1")], [[sem(f"qdup{u}{ch}") for ch in range(2)] for u in range(2)]
        scored, pv_done, mx_done = sem("scored"), sem("pv_done"), sem("mx_done")
        k_proj, q_proj, v_proj = sem("k_proj"), sem("q_proj"), sem("v_proj")
        rows_t, sums_mm, fc_mm = sem("rows_t"), sem("sums_mm"), sem("fc_mm")
        exp_done, k_hi, q_hi, v_copied, o_copied, w_hi = (sem("exp_done"), sem("k_hi"), sem("q_hi"),
                                                          sem("v_copied"), sem("o_copied"), sem("w_hi"))
        mx_red, k_lo, q_lo, neg_rows, recip, o_norm, fc_added, w_lo = (
            sem("mx_red"), sem("k_lo"), sem("q_lo"), sem("neg_rows"), sem("recip"), sem("o_norm"),
            sem("fc_added"), sem("w_lo"))
        added = sem("added")

        wqkv = g.W_qkv.rearrange("e (p h t d) -> e p h t d", h=2, t=3, d=64)
        wfc_v = g.W_fc.rearrange("(k p) e -> p k e", p=P)

        def place(s):
            if s < 6:
                i = s + 2
                return 0, 1, i // 4, i % 4
            if s < 14:
                i = s - 6
                return 1, 0, i // 4, i % 4
            i = s - 14
            return 1, 1, i // 4, i % 4

        UNITS = {0: ("k", 1, 0), 1: ("k", 1, 1), 2: ("q", 1, 0), 3: ("sums", -1, 1), 5: ("fc", -1, 1),
                 6: ("rows", 0, 1), 7: ("q", 1, 1), 8: ("v", 1, 0), 9: ("v", 1, 1),
                 11: ("sums", 0, 0), 13: ("fc", 0, 0), 14: ("rows", 1, 0)}

        def unit_at(n, s):
            if s not in UNITS:
                return None
            kind, d, ch = UNITS[s]
            if isinstance(n, int) and not 0 <= n + d < NP:
                return None
            return kind, n + d, ch

        def has(n):
            return not isinstance(n, int) or 0 <= n < NP

        def batch_cols(m, ch):
            b = m // PAIRS
            return ds(b * L + ch * 512, 512) if not isinstance(b, int) else slice(b * L + ch * 512, b * L + ch * 512 + 512)

        def col(base, m):
            p = m % PAIRS
            return ds(p + base, 1) if not isinstance(p, int) else slice(base + p, base + p + 1)

        def half(h):
            return slice(64 * h, 64 * h + 64)

        def other(h):
            return slice(64 - 64 * h, 128 - 64 * h)

        def run(eng, pair, first, last):
            first()
            pair(0, 0)
            pair(1, 1)
            with eng.Fori(1, NP // 2 - 1) as j:
                pair(2 * j, 0)
                pair(2 * j + 1, 1)
            pair(NP - 2, 0)
            pair(NP - 1, 1)
            last()

        block = ctx.enter_context(nc.Block())

        @block.sync
        def _(sp):
            def load_w(m, u):
                wait(sp, v_proj, 2 * m - 2)
                p = m % PAIRS
                src = wqkv[:, p:p + 1, :, :, :] if isinstance(p, int) else wqkv[:, ds(p, 1), :, :, :]
                sp.dma_start(Wraw[:, u, :, :, :], src).then_inc(wraw_in[u], 16)

            def load_h(m):
                wait(sp, v_proj, 2 * m)
                b = m // PAIRS
                src = g.hT[:, b * L:(b + 1) * L] if isinstance(b, int) else g.hT[:, ds(b * L, L)]
                sp.dma_start(hcur[:, :], src).then_inc(hcur_in, 16)

            def load_fc(m, u):
                wait(sp, fc_mm, 2 * m - 2)
                p = m % PAIRS
                src = wfc_v[:, p:p + 1, :] if isinstance(p, int) else wfc_v[:, ds(p, 1), :]
                sp.dma_start(Wfc[:, u:u + 1, :], src).then_inc(wfc_in[u], 16)

            def dup_k(m, u, ch):
                q = slice(ch * 512, ch * 512 + 512)
                sp.wait_ge(k_hi, 2 * m + ch + 1)
                for h in range(2):
                    sp.dma_start(KA[other(h), u, h, q].bitcast(F32), KA[half(h), u, h, q].bitcast(F32)).then_inc(kdup[u], 16)

            def dup_q(m, u, ch):
                q = slice(ch * 512, ch * 512 + 512)
                sp.wait_ge(q_hi, 2 * m + ch + 1)
                for h in range(2):
                    sp.dma_start(QB[half(h), u, h, q].bitcast(F32), QA[half(h), u, h, q].bitcast(F32)).then_inc(qdup[u][ch], 16)

            def first():
                load_w(0, 0)
                load_h(0)
                load_w(1, 1)
                load_fc(0, 0)
                dup_k(0, 0, 0)
                dup_k(0, 0, 1)
                dup_q(0, 0, 0)
                dup_q(0, 0, 1)
                load_h(1)

            def pair(n, u):
                if has(n + 1):
                    dup_k(n + 1, 1 - u, 0)
                    dup_k(n + 1, 1 - u, 1)
                    dup_q(n + 1, 1 - u, 0)
                    load_fc(n + 1, 1 - u)
                    dup_q(n + 1, 1 - u, 1)
                if has(n + 2):
                    load_w(n + 2, u)
                    load_h(n + 2)

            run(sp, pair, first, lambda: None)

        @block.gpsimd
        def _(pool):
            G = nc.gpsimd

            def first():
                G.memset(mask[:, :, :], 1.0).then_inc(s_mask, 1)
                pool.wait_ge(s_mask, 1)
                G.affine_select(out=mask[0:64, :, :], in_=mask[0:64, :, :], compare_op=ALU.is_equal, fill=0.0,
                                base=0, pattern=[[-1, 4], [0, P]], channel_multiplier=1).then_inc(s_mask, 1)
                G.affine_select(out=mask[64:128, :, :], in_=mask[64:128, :, :], compare_op=ALU.is_equal, fill=0.0,
                                base=0, pattern=[[-1, 4], [0, P]], channel_multiplier=1).then_inc(s_mask, 1)

            def pair(n, u):
                for ch in range(2):
                    chunk = 2 * n + ch
                    wait(pool, sums_mm, chunk - 1)
                    for t in range(1, 8):
                        pool.wait_ge(exp_done, 16 * n + 8 * ch + t + 1)
                        a = PR[:, 0, :, :] if t == 1 else ACC[:, ch, :, :]
                        if t > 1:
                            pool.wait_ge(added, 7 * chunk + t - 1)
                        G.tensor_tensor(ACC[:, ch, :, :], a, PR[:, t, :, :], ALU.add).then_inc(added, 1)

            run(pool, pair, first, lambda: None)

        @block.scalar
        def _(act):
            A = nc.scalar

            def split_w(m, u):
                A.activation(bias[:, u, 0:1], g.vecT[:, col(C_BQ, m)], ACT.Copy)
                A.activation(bias[:, u, 1:2], g.vecT[:, col(C_BK, m)], ACT.Copy)
                wait(act, wraw_in[u], (m // 2 + 1) * 16)
                wait(act, q_proj, 2 * m)
                for h in range(2):
                    last = A.activation(Whi[:, :, h, :], Wraw[:, u, h, 0:2, :], ACT.Copy)
                last.then_inc(w_hi, 1)

            def unit(kind, m, u, ch):
                q = slice(ch * 512, ch * 512 + 512)
                if kind == "k":
                    act.wait_ge(k_proj, 2 * m + ch + 1)
                    for h in range(2):
                        last = A.activation(KA[half(h), u, h, q], ps_w[half(h), :], ACT.Identity,
                                            bias=bias[half(h), u, 1:2])
                    last.then_inc(k_hi, 1)
                elif kind == "q":
                    act.wait_ge(q_proj, 2 * m + ch + 1)
                    for h in range(2):
                        last = A.activation(QA[half(h), u, h, q], ps_w[half(h), :], ACT.Identity,
                                            bias=bias[half(h), u, 0:1])
                    last.then_inc(q_hi, 1)
                elif kind == "v":
                    act.wait_ge(v_proj, 2 * m + ch + 1)
                    A.activation(flat(V[:, u, 4 * ch:4 * ch + 4, :]), ps_w[:, :], ACT.Copy).then_inc(v_copied, 1)

            def first():
                split_w(0, 0)
                unit("k", 0, 0, 0)
                unit("k", 0, 0, 1)
                unit("q", 0, 0, 0)
                unit("q", 0, 0, 1)
                unit("v", 0, 0, 0)
                unit("v", 0, 0, 1)
                split_w(1, 1)

            def copy_o(n, ch):
                act.wait_ge(pv_done, 16 * n + 8 * ch + 8)
                wait(act, o_norm, 2 * n + ch)
                A.activation(Oraw[:, :], ps_o[:, :], ACT.Copy).then_inc(o_copied, 1)

            def pair(n, u):
                for s in range(16):
                    ch, t = divmod(s, 8)
                    chunk = 2 * n + ch
                    act.wait_ge(scored, 16 * n + s + 1)
                    wait(act, pv_done, 16 * n + s - 7)
                    wait(act, added, 7 * (chunk - 1) + max(t, 1))
                    A.activation(PR[:, t, :, :], ps_s[:, s % 2, :, :], ACT.Exp, scale=SCALE).then_inc(exp_done, 1)
                    x = unit_at(n, s)
                    if x and x[0] in "kqv":
                        unit(x[0], x[1], 1 - u, x[2])
                    if s == 8:
                        copy_o(n, 0)
                    if s == 0 and has(n - 1):
                        copy_o(n - 1, 1)
                    if s == 12 and has(n + 2):
                        split_w(n + 2, u)

            run(act, pair, first, lambda: copy_o(NP - 1, 1))

        @block.vector
        def _(dve):
            D = nc.vector

            def split_w(m, u):
                dve.wait_ge(w_hi, m + 1)
                for h in range(2):
                    last = D.tensor_tensor(Wlo[:, :, h, :], Wraw[:, u, h, 0:2, :], Whi[:, :, h, :].bitcast(F32), ALU.subtract)
                last.then_inc(w_lo, 1)

            def reduce_max(m, ch, h, i, count):
                dve.wait_ge(mx_done, count)
                if h == 0 and i == 0:
                    wait(dve, rows_t, 2 * m + ch - 1)
                D.tensor_reduce(NM[:, ch, h, i:i + 1], ps_mx[:, :], AX, ALU.max, negate=True).then_inc(mx_red, 1)

            def unit(kind, m, u, ch):
                q = slice(ch * 512, ch * 512 + 512)
                if kind == "k":
                    dve.wait_ge(k_hi, 2 * m + ch + 1)
                    for h in range(2):
                        last = D.scalar_tensor_tensor(KB[half(h), u, h, q], ps_w[half(h), :], bias[half(h), u, 1:2],
                                                      KA[half(h), u, h, q].bitcast(F32), op0=ALU.add, op1=ALU.subtract)
                    last.then_inc(k_lo, 1)
                elif kind == "q":
                    dve.wait_ge(q_hi, 2 * m + ch + 1)
                    for h in range(2):
                        last = D.scalar_tensor_tensor(QA[other(h), u, h, q], ps_w[half(h), :], bias[half(h), u, 0:1],
                                                      QA[half(h), u, h, q].bitcast(F32), op0=ALU.add, op1=ALU.subtract)
                    last.then_inc(q_lo, 1)
                elif kind == "rows":
                    dve.wait_ge(rows_t, 2 * m + ch + 1)
                    for h in range(2):
                        at = slice(64 - 64 * h, 68 - 64 * h)
                        rows = ps_w[at, h * P:(h + 1) * P].unsqueeze(1).to_broadcast([4, 4, P])
                        last = D.tensor_tensor(QB[at, u, h, q].rearrange("p (i q) -> p i q", i=4), rows, mask[at, :, :], ALU.mult)
                    last.then_inc(neg_rows, 1)
                elif kind == "sums":
                    dve.wait_ge(sums_mm, 2 * m + ch + 1)
                    D.reciprocal(R[:, :], ps_w[:, :]).then_inc(recip, 1)
                    dve.wait_ge(recip, 2 * m + ch + 1)
                    dve.wait_ge(o_copied, 2 * m + ch + 1)
                    wait(dve, fc_mm, 2 * m + ch)
                    D.tensor_tensor(On[:, :], Oraw[:, :], R[:, :], ALU.mult).then_inc(o_norm, 1)
                elif kind == "fc":
                    dve.wait_ge(fc_mm, 2 * m + ch + 1)
                    wait(dve, fc_added, 2 * m + ch)
                    cols = batch_cols(m, ch)
                    D.tensor_tensor(g.attnT[:, cols], g.attnT[:, cols], ps_w[:, :], ALU.add).then_inc(fc_added, 1)

            def first():
                for h in range(2):
                    at = other(h)
                    D.memset(QB[at, :, h, :].bitcast(F32), 0.0)
                    D.memset(KB[at, :, h, :].bitcast(F32), 0.0).then_inc(s_init, 1)
                dve.wait_ge(s_init, 2)
                for h in range(2):
                    at = slice(64 - 64 * h, 68 - 64 * h)
                    D.memset(KB[at, :, h, :].bitcast(F32), 1.0).then_inc(s_init, 1)
                split_w(0, 0)
                unit("k", 0, 0, 0)
                unit("k", 0, 0, 1)
                unit("q", 0, 0, 0)
                unit("q", 0, 0, 1)
                for i in range(8):
                    reduce_max(0, 0, i // 4, i % 4, i + 1)
                dve.wait_ge(s_mask, 3)
                unit("rows", 0, 0, 0)
                for i in range(2):
                    reduce_max(0, 1, i // 4, i % 4, i + 9)
                split_w(1, 1)

            def pair(n, u):
                for s in range(16):
                    d, ch, h, i = place(s)
                    if has(n + d):
                        reduce_max(n + d, ch, h, i, 16 * n + s + 11)
                    x = unit_at(n, s)
                    if x:
                        unit(x[0], x[1], u if UNITS[s][1] == 0 else 1 - u, x[2])
                    if s == 12 and has(n + 2):
                        split_w(n + 2, u)

            def last():
                unit("sums", NP - 1, 1, 1)
                unit("fc", NP - 1, 1, 1)

            run(dve, pair, first, last)

        @block.tensor
        def _(pe):
            T = nc.tensor

            def unit(kind, m, u, ch):
                q = slice(ch * 512, ch * 512 + 512)
                if kind in "qk":
                    ty = 0 if kind == "q" else 1
                    pe.wait_ge(w_lo, m + 1)
                    if kind == "q" and ch == 1:
                        wait(pe, neg_rows, 2 * m if not (isinstance(m, int) and m == 0) else 0)
                    hi, lo = g.hT_hi[:, batch_cols(m, ch)], g.hT_lo[:, batch_cols(m, ch)]
                    wh, wl = flat(Whi[:, ty, :, :]), flat(Wlo[:, ty, :, :])
                    T.matmul(ps_w[:, :], wh, hi, start=True, stop=False)
                    T.matmul(ps_w[:, :], wl, hi, start=False, stop=False)
                    T.matmul(ps_w[:, :], wh, lo, start=False, stop=True).then_inc(q_proj if kind == "q" else k_proj, 1)
                elif kind == "v":
                    pe.wait_ge(hcur_in, 16 * (m + 1))
                    pe.wait_ge(wraw_in[u], 16 * (m // 2 + 1))
                    for i in range(4):
                        t = 4 * ch + i
                        last = T.matmul(ps_w[:, i * P:(i + 1) * P], hcur[:, t * P:(t + 1) * P], Wraw[:, u, :, 2, :],
                                        start=True, stop=True)
                    last.then_inc(v_proj, 1)
                elif kind == "rows":
                    for h in range(2):
                        last = T.matmul(ps_w[64 - 64 * h:68 - 64 * h, h * P:(h + 1) * P], NM[:, ch, h, :], g.ident[:, :],
                                        start=True, stop=True)
                    last.then_inc(rows_t, 1)
                elif kind == "sums":
                    pe.wait_ge(added, 14 * m + 7 * ch + 7)
                    for h in range(2):
                        last = T.matmul(ps_w[half(h), :], g.ones[:, 0:64], ACC[:, ch, h, :], start=True, stop=True)
                    last.then_inc(sums_mm, 1)
                elif kind == "fc":
                    pe.wait_ge(o_norm, 2 * m + ch + 1)
                    pe.wait_ge(wfc_in[u], 16 * (m // 2 + 1))
                    T.matmul(ps_w[:, :], Wfc[:, u, :], On[:, :], start=True, stop=True).then_inc(fc_mm, 1)

            FREED = {"k": k_lo, "q": q_lo, "v": v_copied, "rows": neg_rows, "sums": recip, "fc": fc_added}

            def freed(kind, m, ch):
                pe.wait_ge(FREED[kind], 2 * m + ch + 1)

            def max_group(m, u, ch, h, i, count):
                wait(pe, mx_red, count)
                if h == 0 and i == 0:
                    pe.wait_ge(q_lo, 2 * m + ch + 1)
                    if ch == 0:
                        pe.wait_ge(k_hi, 2 * m + 2)
                        pe.wait_ge(kdup[u], 64 * (m // 2 + 1))
                q = ch * 512 + i * P
                for kc in range(2):
                    last = T.matmul(ps_mx[:, kc * 512:(kc + 1) * 512], QA[:, u, h, q:q + P], KA[:, u, h, kc * 512:(kc + 1) * 512],
                                    start=True, stop=True)
                last.then_inc(mx_done, 1)

            def scores(n, u, s):
                ch, t = divmod(s, 8)
                q, k = slice(ch * 512, ch * 512 + 512), slice(t * P, (t + 1) * P)
                wait(pe, exp_done, 16 * n + s - 1)
                if t == 0:
                    pe.wait_ge(neg_rows, 2 * n + ch + 1)
                    pe.wait_ge(qdup[u][ch], 32 * (n // 2) + 32)
                    if ch == 0:
                        pe.wait_ge(k_lo, 2 * n + 2)
                for h in range(2):
                    T.matmul(ps_s[:, s % 2, h, :], KA[:, u, h, k], QA[:, u, h, q], start=True, stop=False)
                    last = T.matmul(ps_s[:, s % 2, h, :], KB[:, u, h, k], QB[:, u, h, q], start=False, stop=True)
                last.then_inc(scored, 1)

            def times_v(n, u, s):
                ch, t = divmod(s, 8)
                pe.wait_ge(exp_done, 16 * n + s + 1)
                if t == 0:
                    wait(pe, o_copied, 2 * n + ch)
                    pe.wait_ge(v_copied, 2 * n + 2)
                for h in range(2):
                    last = T.matmul(ps_o[half(h), :], V[:, u, t, half(h)], PR[:, t, h, :], start=(t == 0), stop=(t == 7))
                last.then_inc(pv_done, 1)

            def first():
                pe.wait_ge(s_init, 4)
                unit("k", 0, 0, 0)
                freed("k", 0, 0)
                unit("k", 0, 0, 1)
                freed("k", 0, 1)
                unit("q", 0, 0, 0)
                freed("q", 0, 0)
                unit("q", 0, 0, 1)
                freed("q", 0, 1)
                unit("v", 0, 0, 0)
                freed("v", 0, 0)
                unit("v", 0, 0, 1)
                freed("v", 0, 1)
                for i in range(8):
                    max_group(0, 0, 0, i // 4, i % 4, i)
                pe.wait_ge(mx_red, 8)
                unit("rows", 0, 0, 0)
                for i in range(2):
                    max_group(0, 0, 1, i // 4, i % 4, i + 8)

            ORDER = sorted(UNITS)

            def pair(n, u):
                for s in range(16):
                    d, ch, h, i = place(s)
                    if has(n + d):
                        max_group(n + d, u if d == 0 else 1 - u, ch, h, i, 16 * n + s + 10)
                    scores(n, u, s)
                    x = unit_at(n, s)
                    if x:
                        k = ORDER.index(s) - 1
                        while k >= 0 and not unit_at(n, ORDER[k]):
                            k -= 1
                        if k >= 0:
                            freed(*unit_at(n, ORDER[k]))
                        else:
                            freed("rows", n, 0)
                        if x[0] == "rows":
                            pe.wait_ge(mx_red, 16 * n + s + 10)
                        unit(x[0], x[1], u if UNITS[s][1] == 0 else 1 - u, x[2])
                    if s > 0:
                        times_v(n, u, s - 1)
                    elif has(n - 1):
                        times_v(n - 1, 1 - u, 15)

            def last():
                times_v(NP - 1, 1, 15)
                freed("fc", NP - 1, 0)
                unit("sums", NP - 1, 1, 1)
                freed("sums", NP - 1, 1)
                unit("fc", NP - 1, 1, 1)

            run(pe, pair, first, last)


def ffn_stage(nc, g):
    B, L = g.B, g.L
    GROUPS = B * L // 512
    GPB = L // 512
    with ExitStack() as ctx:
        def sb(name, shape, dt=F32):
            return ctx.enter_context(nc.sbuf_tensor(name, shape, dt))

        def psum(name, shape):
            return ctx.enter_context(nc.psum_tensor(name, shape, F32))

        def sem(name):
            return ctx.enter_context(nc.semaphore(name))

        spot = sb("f_spot", [1, 2])
        w1 = sb("w1s", [P, 4, 256])
        w2 = sb("w2s", [P, 8, P])
        xg = sb("f_x", [P, 4, P])
        yT = sb("f_yT", [P, 512])
        x2 = sb("f_x2", [P, 2, 4, P])
        st = sb("f_st", [P, 4, 6])
        mv = sb("f_mv", [P, 4, 2])
        sd = sb("f_sd", [P, 4])
        rs = sb("f_rs", [P, 4])
        n2 = sb("f_n2", [P, 4, P])
        hm = sb("f_hm", [P, 4, P])
        hh = sb("f_h", [P, 4, P])
        st2 = sb("f_st2", [P, 4, 6])
        mv2 = sb("f_mv2", [P, 4, 2])
        sd2 = sb("f_sd2", [P, 4])
        rs2 = sb("f_rs2", [P, 4])
        hT2 = sb("f_hT2", [P, 512])
        lg = sb("f_lg", [P, 6, 4, 4])
        lt = sb("f_lt", [P, 4, 4])
        cmp_ = sb("f_cmp", [P, 3, 4, 4, 4])
        tri = sb("f_tri", [P, 2, 4, 4])
        gate = sb("f_gate", [P, 4, 4])
        st3 = sb("f_st3", [P, 4, 4, 6])
        mv3 = sb("f_mv3", [P, 4, 4, 2])
        sd3 = sb("f_sd3", [P, 4, 4])
        rs3 = sb("f_rs3", [P, 4, 4])
        hn = sb("f_hn", [P, 4, 8, P])
        rT = sb("f_rT", [P, 8, 512])
        o = sb("f_o", [P, 4, P])
        st4 = sb("f_st4", [P, 4, 6])
        mv4 = sb("f_mv4", [P, 4, 2])
        sd4 = sb("f_sd4", [P, 4])
        rs4 = sb("f_rs4", [P, 4])
        n4 = sb("f_n4", [P, 4, P])
        t4 = sb("f_t4", [P, 4, P])
        t5 = sb("f_t5", [P, 4, P])
        res = sb("f_res", [P, 4, P])

        ps_h = psum("ps_h", [P, 2, 4, 256])
        ps_t = psum("ps_t", [P, 2, 512])
        ps_e = psum("ps_e", [P, 4, P])
        ps_f = psum("ps_f", [P, 512])

        names = ("w x y yt x2 st1 mv1 sd1 rs1 n2 hm h st2 mv2 sd2 rs2 ht hT2 logit hid st3 mv3 sd3 rs3 hn "
                 "tp relu eo gacc g1 g2 g3 g4 ge gs gr gp gc gm gw gsum grs gate st4 mv4 sd4 rs4 n4 t4 t5 res out tri spot").split()
        s = {k: sem("f_" + k) for k in names}

        xv = g.X.rearrange("b l e -> (b l) e").rearrange("(t p) e -> p t e", p=P)
        ov = g.out.rearrange("b l e -> (b l) e").rearrange("(t p) e -> p t e", p=P)

        def tiles(n):
            return ds(n * 4, 4) if not isinstance(n, int) else slice(4 * n, 4 * n + 4)

        def one(b):
            return ds(b, 1) if not isinstance(b, int) else slice(b, b + 1)

        def parity(n):
            return one(n % 2)

        def run(eng, front, back):
            front(0)
            with eng.Fori(0, GROUPS - 1) as n:
                back(n, True)
            back(GROUPS - 1, False)

        block = ctx.enter_context(nc.Block())

        @block.sync
        def _(sp):
            sp.dma_start(w1[:, :, :], g.w1.rearrange("e d h -> d e h")).then_inc(s["w"], 16)
            sp.dma_start(w2[:, :, :], g.w2.rearrange("e (a p) d -> p (e a) d", p=P)).then_inc(s["w"], 16)

            def front(n):
                wait(sp, s["x2"], n)
                sp.dma_start(xg[:, :, :], xv[:, tiles(n), :]).then_inc(s["x"], 16)

            def back(n, more):
                if more:
                    front(n + 1)
                sp.wait_ge(s["res"], n + 1)
                sp.dma_start(ov[:, tiles(n), :], res[:, :, :]).then_inc(s["out"], 16)

            run(sp, front, back)
            sp.wait_ge(s["out"], 16 * GROUPS)

        @block.gpsimd
        def _(pool):
            G = nc.gpsimd
            G.memset(tri[:, :, :, :], 1.0).then_inc(s["tri"], 1)
            pool.wait_ge(s["tri"], 1)
            G.affine_select(out=tri[:, 0, :, :], in_=tri[:, 0, :, :], compare_op=ALU.is_gt, fill=0.0, base=0,
                            pattern=[[1, 4], [-1, 4]], channel_multiplier=0).then_inc(s["tri"], 1)
            G.affine_select(out=tri[:, 1, :, :], in_=tri[:, 1, :, :], compare_op=ALU.is_gt, fill=0.0, base=0,
                            pattern=[[-1, 4], [1, 4]], channel_multiplier=0).then_inc(s["tri"], 1)

            def front(n):
                b = n // GPB
                pool.wait_ge(s["n2"], n + 1)
                wait(pool, s["h"], n)
                G.tensor_tensor(hm[:, :, :], n2[:, :, :], g.mod_rep[:, 0, one(b), :].to_broadcast([P, 4, P]), ALU.mult).then_inc(s["hm"], 1)
                pool.wait_ge(s["hm"], n + 1)
                wait(pool, s["st2"], n)
                wait(pool, s["ht"], n)
                G.tensor_tensor(hh[:, :, :], hm[:, :, :], g.mod_rep[:, 1, one(b), :].to_broadcast([P, 4, P]), ALU.add).then_inc(s["h"], 1)

            def back(n, more):
                if more:
                    front(n + 1)
                b = n // GPB
                pool.wait_ge(s["n4"], n + 1)
                G.tensor_tensor(t4[:, :, :], n4[:, :, :], g.mod_rep[:, 2, one(b), :].to_broadcast([P, 4, P]), ALU.mult).then_inc(s["t4"], 1)
                pool.wait_ge(s["t4"], n + 1)
                G.tensor_tensor(t5[:, :, :], t4[:, :, :], g.mod_rep[:, 3, one(b), :].to_broadcast([P, 4, P]), ALU.add).then_inc(s["t5"], 1)
                pool.wait_ge(s["t5"], n + 1)
                wait(pool, s["out"], 16 * n)
                G.tensor_tensor(res[:, :, :], t5[:, :, :], x2[:, parity(n), :, :].rearrange("p a b c -> p (a b) c"), ALU.add).then_inc(s["res"], 1)

            run(pool, front, back)

        @block.scalar
        def _(act):
            A = nc.scalar

            def sqrt(out, var, need, to, count, freed):
                act.wait_ge(need, count)
                wait(act, *freed)
                A.activation(out, var, ACT.Sqrt, bias=g.eps[:, 0:1]).then_inc(to, 1)

            def front(n):
                sqrt(sd[:, :], mv[:, :, 1], s["mv1"], s["sd1"], n + 1, (s["rs1"], n))
                sqrt(sd2[:, :], mv2[:, :, 1], s["mv2"], s["sd2"], n + 1, (s["rs2"], n))
                act.wait_ge(s["ht"], n + 1)
                wait(act, s["hid"], 4 * n)
                A.activation(hT2[:, :], ps_f[:, :], ACT.Copy).then_inc(s["hT2"], 1)

            def back(n, more):
                for i in range(4):
                    sqrt(sd3[:, i, :], mv3[:, i, :, 1], s["mv3"], s["sd3"], 4 * n + i + 1, (s["rs3"], 4 * n))
                for k in range(8):
                    act.wait_ge(s["tp"], 8 * n + k + 1)
                    wait(act, s["eo"], 4 * n)
                    A.activation(rT[:, k, :], ps_t[:, k % 2, :], ACT.Relu, bias=g.vecT[:, C_LNB + k:C_LNB + k + 1],
                                 scale=g.vecT[:, C_LNG + k:C_LNG + k + 1]).then_inc(s["relu"], 1)
                if more:
                    front(n + 1)
                act.wait_ge(s["g4"], n + 1)
                wait(act, s["gp"], n)
                A.activation(lg[:, 3, :, :], lg[:, 2, :, :], ACT.Exp).then_inc(s["ge"], 1)
                sqrt(sd4[:, :], mv4[:, :, 1], s["mv4"], s["sd4"], n + 1, (s["rs4"], n))

            run(act, front, back)

        @block.vector
        def _(dve):
            D = nc.vector

            def after(ins, name, value):
                ins.then_inc(s[name], 1)
                dve.wait_ge(s[name], value)

            def layer_stats(src, st, mv, sd, rs, k, n):
                D.tensor_copy(spot[0:1, 0:1], spot[0:1, 1:2])
                for i in range(4):
                    last = D.bn_stats(st[:, i, :], src[i])
                after(last, "st" + k, n + 1)
                D.tensor_copy(spot[0:1, 0:1], spot[0:1, 1:2])
                for i in range(4):
                    last = D.bn_aggr(mv[:, i, :], st[:, i, :])
                after(last, "mv" + k, n + 1)
                dve.wait_ge(s["sd" + k], n + 1)
                after(D.reciprocal(rs[:, :], sd[:, :]), "rs" + k, n + 1)

            def front(n):
                b = n // GPB
                cols = ds(n * 512, 512) if not isinstance(n, int) else slice(n * 512, n * 512 + 512)
                wait(dve, s["yt"], n)
                D.tensor_scalar(yT[:, :], g.attnT[:, cols], g.gaT[:, one(b)], g.gacT[:, one(b)], ALU.mult, ALU.add).then_inc(s["y"], 1)
                dve.wait_ge(s["x"], 16 * (n + 1))
                dve.wait_ge(s["yt"], n + 1)
                xd = x2[:, parity(n), :, :].rearrange("p a b c -> p (a b) c")
                after(D.tensor_tensor(xd, xg[:, :, :], ps_f[:, :].rearrange("p (a b) -> p a b", a=4), ALU.add), "x2", n + 1)
                src = [x2[:, parity(n), i, :].rearrange("p a b -> p (a b)") for i in range(4)]
                layer_stats(src, st, mv, sd, rs, "1", n)
                wait(dve, s["hm"], n)
                for i in range(4):
                    last = D.tensor_scalar(n2[:, i, :], src[i], mv[:, i, 0:1], rs[:, i:i + 1], ALU.subtract, ALU.mult)
                last.then_inc(s["n2"], 1)
                dve.wait_ge(s["h"], n + 1)
                for i in range(4):
                    last = D.bn_stats(st2[:, i, :], hh[:, i, :])
                after(last, "st2", n + 1)
                D.tensor_copy(spot[0:1, 0:1], spot[0:1, 1:2])
                for i in range(4):
                    last = D.bn_aggr(mv2[:, i, :], st2[:, i, :])
                after(last, "mv2", n + 1)
                dve.wait_ge(s["sd2"], n + 1)
                after(D.reciprocal(rs2[:, :], sd2[:, :]), "rs2", n + 1)

            def experts(n):
                for i in range(4):
                    dve.wait_ge(s["hid"], 4 * n + i + 1)
                    for e in range(4):
                        last = D.bn_stats(st3[:, i, e, :], ps_h[:, i % 2, e, :])
                    after(last, "st3", 4 * n + i + 1)
                    D.tensor_copy(spot[0:1, 0:1], spot[0:1, 1:2])
                    for e in range(4):
                        last = D.bn_aggr(mv3[:, i, e, :], st3[:, i, e, :])
                    after(last, "mv3", 4 * n + i + 1)
                    dve.wait_ge(s["sd3"], 4 * n + i + 1)
                    after(D.reciprocal(rs3[:, i, :], sd3[:, i, :]), "rs3", 4 * n + i + 1)
                    wait(dve, s["tp"], 8 * n)
                    for e in range(4):
                        last = D.tensor_scalar(flat(hn[:, i, 2 * e:2 * e + 2, :]), ps_h[:, i % 2, e, :], mv3[:, i, e, 0:1],
                                               rs3[:, i, e:e + 1], ALU.subtract, ALU.mult)
                    last.then_inc(s["hn"], 1)

            def gates(n):
                def per_e(ap):
                    return ap.unsqueeze(1).to_broadcast([P, 4, 4])

                def per_t(ap):
                    return ap.unsqueeze(2).to_broadcast([P, 4, 4])

                dve.wait_ge(s["logit"], n + 1)
                after(D.tensor_tensor(lg[:, 0, :, :], per_t(mv2[:, :, 0]), per_e(g.rw_sum[:, 0:4]), ALU.mult), "g1", n + 1)
                after(D.tensor_tensor(lg[:, 1, :, :], ps_f[:, 0:16].rearrange("p (a b) -> p a b", a=4), lg[:, 0, :, :], ALU.subtract), "g2", n + 1)
                dve.wait_ge(s["rs2"], n + 1)
                D.tensor_tensor(lg[:, 4, :, :], lg[:, 1, :, :], per_t(rs2[:, :]), ALU.mult).then_inc(s["g3"], 1)
                dve.wait_ge(s["g3"], n + 1)
                after(D.tensor_tensor(lg[:, 5, :, :], lg[:, 4, :, :], per_e(g.rw_sum[:, 4:8]), ALU.add), "gs", n + 1)
                after(D.tensor_reduce(lt[:, 0, :], lg[:, 5, :, :], AX, ALU.max), "gr", n + 1)
                after(D.tensor_tensor(lg[:, 2, :, :], lg[:, 5, :, :], per_t(lt[:, 0, :]), ALU.subtract), "g4", n + 1)

            def top_two(n):
                def per_t(ap):
                    return ap.unsqueeze(2).to_broadcast([P, 4, 4])

                dve.wait_ge(s["ge"], n + 1)
                after(D.tensor_reduce(lt[:, 1, :], lg[:, 3, :, :], AX, ALU.add), "gp", n + 1)
                after(D.reciprocal(lt[:, 2, :], lt[:, 1, :]), "gc", n + 1)
                after(D.tensor_tensor(lg[:, 1, :, :], lg[:, 3, :, :], per_t(lt[:, 2, :]), ALU.mult), "gm", n + 1)
                dve.wait_ge(s["tri"], 3)
                pr = lg[:, 1, :, :]
                for i in range(4):
                    pj = pr[:, i:i + 1, :].to_broadcast([P, 4, 4])
                    pe_ = pr[:, i, :].unsqueeze(2).to_broadcast([P, 4, 4])
                    D.tensor_tensor(cmp_[:, 0, i, :, :], pj, pe_, ALU.is_ge)
                    last = D.tensor_tensor(cmp_[:, 1, i, :, :], pj, pe_, ALU.is_gt)
                after(last, "gw", 4 * n + 1)
                for i in range(4):
                    D.tensor_tensor(cmp_[:, 0, i, :, :], cmp_[:, 0, i, :, :], tri[:, 0, :, :], ALU.mult)
                    last = D.tensor_tensor(cmp_[:, 1, i, :, :], cmp_[:, 1, i, :, :], tri[:, 1, :, :], ALU.mult)
                after(last, "gw", 4 * n + 2)
                flat4 = "p a b c -> p (a b c)"
                after(D.tensor_tensor(cmp_[:, 2, :, :, :].rearrange(flat4), cmp_[:, 0, :, :, :].rearrange(flat4),
                                      cmp_[:, 1, :, :, :].rearrange(flat4), ALU.add), "gw", 4 * n + 3)
                after(D.tensor_reduce(lg[:, 0, :, :], cmp_[:, 2, :, :, :], AX, ALU.add), "gw", 4 * n + 4)
                after(D.scalar_tensor_tensor(flat(lg[:, 4, :, :]), flat(lg[:, 0, :, :]), 2.0, flat(pr), op0=ALU.is_lt, op1=ALU.mult), "gsum", 3 * n + 1)
                after(D.tensor_reduce(lt[:, 3, :], lg[:, 4, :, :], AX, ALU.add), "gsum", 3 * n + 2)
                after(D.tensor_scalar_add(lt[:, 0, :], lt[:, 3, :], EPS_GATE), "gsum", 3 * n + 3)
                after(D.reciprocal(lt[:, 1, :], lt[:, 0, :]), "grs", n + 1)
                after(D.tensor_tensor(gate[:, :, :], lg[:, 4, :, :], per_t(lt[:, 1, :]), ALU.mult), "gate", n + 1)

            def back(n, more):
                experts(n)
                gates(n)
                if more:
                    front(n + 1)
                top_two(n)
                for i in range(4):
                    dve.wait_ge(s["eo"], 4 * n + i + 1)
                    after(D.tensor_scalar(o[:, i, :], ps_e[:, 0, :], gate[:, i, 0:1], None, ALU.mult), "gacc", 16 * n + 4 * i + 1)
                    for e in range(1, 4):
                        after(D.scalar_tensor_tensor(o[:, i, :], ps_e[:, e, :], gate[:, i, e:e + 1], o[:, i, :], op0=ALU.mult, op1=ALU.add),
                              "gacc", 16 * n + 4 * i + e + 1)
                layer_stats([o[:, i, :] for i in range(4)], st4, mv4, sd4, rs4, "4", n)
                wait(dve, s["t4"], n)
                for i in range(4):
                    last = D.tensor_scalar(n4[:, i, :], o[:, i, :], mv4[:, i, 0:1], rs4[:, i:i + 1], ALU.subtract, ALU.mult)
                last.then_inc(s["n4"], 1)

            after(D.memset(spot[:, :], 0.0), "spot", 1)
            run(dve, front, back)

        @block.tensor
        def _(pe):
            T = nc.tensor
            pe.wait_ge(s["w"], 32)

            def front(n):
                pe.wait_ge(s["y"], n + 1)
                wait(pe, s["g2"], n)
                for i in range(4):
                    last = T.transpose(ps_f[:, i * P:(i + 1) * P], yT[:, i * P:(i + 1) * P], g.ident[:, :])
                last.then_inc(s["yt"], 1)
                pe.wait_ge(s["h"], n + 1)
                pe.wait_ge(s["x2"], n + 1)
                for i in range(4):
                    last = T.transpose(ps_f[:, i * P:(i + 1) * P], hh[:, i, :], g.ident[:, :])
                last.then_inc(s["ht"], 1)

            def back(n, more):
                pe.wait_ge(s["hT2"], n + 1)
                for i in range(4):
                    last = T.matmul(ps_f[:, 4 * i:4 * i + 4], hT2[:, i * P:(i + 1) * P], g.rw[:, 0:4], start=True, stop=True)
                last.then_inc(s["logit"], 1)
                for i in range(4):
                    wait(pe, s["hn"], 4 * n + i - 1 if i > 0 else 4 * n)
                    for k in range(2):
                        last = T.matmul(flat(ps_h[:, i % 2, 2 * k:2 * k + 2, :]), hT2[:, i * P:(i + 1) * P],
                                        flat(w1[:, 2 * k:2 * k + 2, :]), start=True, stop=True)
                    last.then_inc(s["hid"], 1)
                pe.wait_ge(s["hn"], 4 * n + 4)
                for k in range(8):
                    wait(pe, s["relu"], 8 * n + k - 1 if k > 0 else 8 * n)
                    for i in range(4):
                        last = T.transpose(ps_t[:, k % 2, i * P:(i + 1) * P], hn[:, i, k, :], g.ident[:, :])
                    last.then_inc(s["tp"], 1)
                if more:
                    front(n + 1)
                pe.wait_ge(s["relu"], 8 * n + 8)
                for i in range(4):
                    wait(pe, s["gacc"], 16 * n + 4 * i)
                    for e in range(4):
                        for a in range(2):
                            last = T.matmul(ps_e[:, e, :], rT[:, 2 * e + a, i * P:(i + 1) * P], w2[:, 2 * e + a, :],
                                            start=(a == 0), stop=(a == 1))
                    last.then_inc(s["eo"], 1)

            run(pe, front, back)


_INS = ['L0_attn_X', 'L0_attn_W_qkv', 'L0_attn_b_qkv', 'L0_attn_W_fc', 'L0_attn_b_fc', 'L0_ffn_router_w', 'L0_ffn_rn_g',
        'L0_ffn_rn_b', 'L0_ffn_w1', 'L0_ffn_ln_g', 'L0_ffn_ln_b', 'L0_ffn_w2', 'L0_ffn_on_g', 'L0_ffn_on_b', 'L0_c', 'L0_wmod']


def kernel(**inputs):
    import numpy as np
    import concourse.bacc as bacc
    from concourse.bass_utils import run_bass_kernel_spmd

    nc = bacc.Bacc("TRN2", target_bir_lowering=False, num_devices=1)
    arrays, args = {}, []
    for name in _INS:
        a = np.ascontiguousarray(inputs[name])
        arrays[f"in_{name}"] = a
        args.append(nc.dram_tensor(f"in_{name}", a.shape, mybir.dt.from_np(a.dtype), kind="ExternalInput").ap())
    args.append(nc.dram_tensor("out_0", inputs['L0_attn_X'].shape, F32, kind="ExternalOutput").ap())
    build(nc, *args)
    r = run_bass_kernel_spmd(nc, [arrays], core_ids=[0])
    return r.results[0]["out_0"]
```

```python
from contextlib import ExitStack

import concourse.bass as bass
from concourse import mybir

F32 = mybir.dt.float32
F32R = mybir.dt.float32r
ACT = mybir.ActivationFunctionType
ALU = mybir.AluOpType
AX = mybir.AxisListType.X

P = 128
EPS = 1e-5
EPS_GATE = 1e-8
GUARD = 0.25
ds = bass.ds


def flat(ap):
    return ap.rearrange("p a b -> p (a b)")


def wait(eng, sem, value):
    if not isinstance(value, int) or value > 0:
        eng.wait_ge(sem, value)


def run_pairs(eng, count, body, first=None, last=None):
    if first:
        first()
    body(0, 0)
    body(1, 1)
    with eng.Fori(1, count // 2 - 1) as j:
        body(2 * j, 0)
        body(2 * j + 1, 1)
    body(count - 2, 0)
    body(count - 1, 1)
    if last:
        last()


def at(index, size):
    return slice(index, index + size) if isinstance(index, int) else ds(index, size)


def carry(eng, spot, zero, kind, index):
    eng.tensor_tensor(spot[0:1, kind, at(index, 1)], zero[0:1, 0:1], zero[0:1, 0:1], ALU.mult)


class Shared:
    pass


def build(nc, X, W_qkv, b_qkv, W_fc, b_fc, router_w, rn_g, rn_b, w1, ln_g, ln_b, w2, on_g, on_b, c, wmod, out):
    B, L, E = X.shape
    HD = W_fc.shape[0]
    DK = 64
    H = HD // DK
    assert E == P and L == 1024 and H == 16 and B == 4
    with ExitStack() as ctx:
        g = Shared()
        g.X, g.W_qkv, g.W_fc, g.out = X, W_qkv, W_fc, out
        g.small = (b_qkv, b_fc, router_w, rn_g, rn_b, ln_g, ln_b, on_g, on_b, c, wmod)
        g.w1, g.w2 = w1, w2
        g.B, g.L, g.E, g.H = B, L, E, H

        def sb(name, shape, dt=F32):
            return ctx.enter_context(nc.sbuf_tensor(name, shape, dt))

        g.ident = sb("ident", [P, P])
        g.ones = sb("ones", [P, P])
        g.eps = sb("eps", [P, 1])
        g.attnT = sb("attnT", [P, B * L])
        g.vecT = sb("vecT", [P, 64])
        g.modT = sb("modT", [P, 6, B])
        g.gaT = sb("gaT", [P, B])
        g.gacT = sb("gacT", [P, B])
        g.mod_rep = sb("mod_rep", [P, 4, B, P])
        g.on_rep = sb("on_rep", [P, 2, P])
        g.rw = sb("rw", [P, 8])
        g.rw_sum = sb("rw_sum", [P, 4])
        with ExitStack() as two:
            g.hT = two.enter_context(nc.sbuf_tensor("hT", [P, B * L], F32))
            g.hT_hi = two.enter_context(nc.sbuf_tensor("hT_hi", [P, B * L], F32R))
            g.hT_lo = two.enter_context(nc.sbuf_tensor("hT_lo", [P, B * L], F32R))
            setup_stage(nc, g)
            attention_stage(nc, g)
        ffn_stage(nc, g)


C_LNG, C_LNB, C_RNG, C_RNB, C_BFC, C_RW, C_C, C_BQ, C_BK, C_BV = 0, 8, 16, 17, 18, 19, 23, 27, 35, 43
N_VEC = 51


def setup_stage(nc, g):
    b_qkv, b_fc, router_w, rn_g, rn_b, ln_g, ln_b, on_g, on_b, c, wmod = g.small
    B, L = g.B, g.L
    GROUPS = B * L // 512
    with ExitStack() as ctx:
        def sb(name, shape, dt=F32):
            return ctx.enter_context(nc.sbuf_tensor(name, shape, dt))

        def sem(name):
            return ctx.enter_context(nc.semaphore(name))

        rows = sb("rows", [64, P])
        on_row = sb("on_row", [1, 2 * P])
        wm = sb("wm", [P, 6 * P])
        wfc = sb("wfc_all", [P, 8, P])
        silu = sb("silu", [P, 4, B])
        silu_rep = sb("silu_rep", [P, B, P])
        tmpT = sb("tmpT", [P, 4, B])
        TILES = 4 * GROUPS
        x = sb("x", [P, TILES, P])
        xn = sb("xn", [P, 2, 4, P])
        st = sb("st", [P, TILES, 6])
        mv = sb("mv", [P, TILES, 2])
        sd = sb("sd", [P, TILES])
        rs = sb("rs", [P, TILES])
        ps_a = ctx.enter_context(nc.psum_tensor("ps_a", [P, 512], F32))
        ps_m = ctx.enter_context(nc.psum_tensor("ps_m", [P, B, 512], F32))
        ps_x = ctx.enter_context(nc.psum_tensor("ps_x", [P, 2, 512], F32))
        ps_b = ctx.enter_context(nc.psum_tensor("ps_b", [P, 512], F32))

        s_rows, s_wm, s_wfc = sem("s_rows"), sem("s_wm"), sem("s_wfc")
        s_x = [sem(f"s_x{b}") for b in range(B)]
        s_id, s_const = sem("s_id"), sem("s_const")
        s_vec, s_vecT, s_exp = sem("s_vec"), sem("s_vecT"), sem("s_exp")
        s_v = sem("s_v")
        s_mod, s_modrep, s_onrep, s_bv, s_silu, s_modT = (sem("s_mod"), sem("s_modrep"), sem("s_onrep"), sem("s_bv"),
                                                          sem("s_silu"), sem("s_modT"))
        s_st, s_mv, s_sd, s_rs, s_xn, s_xt = sem("s_st"), sem("s_mv"), sem("s_sd"), sem("s_rs"), sem("s_xn"), sem("s_xt")
        s_h, s_hi, s_lo = sem("s_h"), sem("s_hi"), sem("s_lo")

        xv = g.X.rearrange("b l e -> (b l) e").rearrange("(t p) e -> p t e", p=P)
        N_ROW_DMAS = 15

        block = ctx.enter_context(nc.Block())

        @block.sync
        def _(sp):
            for b in range(B):
                sp.dma_start(x[:, 8 * b:8 * b + 8, :], xv[:, 8 * b:8 * b + 8, :]).then_inc(s_x[b], 16)
            sp.dma_start(wm[:, :], wmod).then_inc(s_wm, 16)
            sp.dma_start(wfc[:, :, :], g.W_fc.rearrange("(k p) e -> p k e", p=P)).then_inc(s_wfc, 16)

        @block.gpsimd
        def _(pool):
            nc.gpsimd.memset(g.ident[:, :], 0.0).then_inc(s_id, 1)
            nc.gpsimd.memset(g.ones[:, :], 1.0).then_inc(s_const, 1)
            nc.gpsimd.memset(g.eps[:, :], EPS).then_inc(s_const, 1)
            pool.wait_ge(s_id, 1)
            nc.gpsimd.affine_select(out=g.ident[:, :], in_=g.ident[:, :], compare_op=ALU.not_equal, fill=1.0,
                                    base=0, pattern=[[-1, P]], channel_multiplier=1).then_inc(s_id, 1)
            nc.gpsimd.memset(g.attnT[:, :], 0.0)

            def body(n, u):
                cols = at(n * 512, 512)
                pool.wait_ge(s_hi, n + 1)
                nc.gpsimd.tensor_tensor(g.hT_lo[:, cols], g.hT[:, cols], g.hT_hi[:, cols].bitcast(F32), ALU.subtract)

            run_pairs(pool, GROUPS, body)

        @block.scalar
        def _(act):
            A = nc.scalar
            act.dma_start(rows[C_LNG:C_LNG + 8, :], ln_g.rearrange("e (a h) -> (e a) h", h=P)).then_inc(s_rows, 16)
            act.dma_start(rows[C_LNB:C_LNB + 8, :], ln_b.rearrange("e (a h) -> (e a) h", h=P)).then_inc(s_rows, 16)
            act.dma_start(rows[C_RNG:C_RNG + 1, :], rn_g.rearrange("(a h) -> a h", a=1)).then_inc(s_rows, 16)
            act.dma_start(rows[C_RNB:C_RNB + 1, :], rn_b.rearrange("(a h) -> a h", a=1)).then_inc(s_rows, 16)
            act.dma_start(rows[C_BFC:C_BFC + 1, :], b_fc.rearrange("(a h) -> a h", a=1)).then_inc(s_rows, 16)
            act.dma_start(rows[C_RW:C_RW + 4, :], router_w).then_inc(s_rows, 16)
            act.dma_start(rows[C_C:C_C + 4, :], c).then_inc(s_rows, 16)
            bv = b_qkv.rearrange("(p h t d) -> t p h d", h=2, t=3, d=64)
            for col, t in ((C_BQ, 0), (C_BK, 1), (C_BV, 2)):
                for hh in range(2):
                    act.dma_start(rows[col:col + 8, 64 * hh:64 * hh + 64], bv[t, :, hh, :]).then_inc(s_rows, 16)
            act.dma_start(on_row[0:1, 0:P], on_g.rearrange("(a h) -> a h", a=1)).then_inc(s_rows, 16)
            act.dma_start(on_row[0:1, P:2 * P], on_b.rearrange("(a h) -> a h", a=1)).then_inc(s_rows, 16)

            act.wait_ge(s_vecT, 1)
            A.activation(silu[:, 0, :], g.vecT[:, C_C:C_C + 4], ACT.Exp, scale=-1.0).then_inc(s_exp, 1)
            A.activation(flat(g.on_rep[:, :, :]), ps_a[:, 256:512], ACT.Copy).then_inc(s_onrep, 1)
            act.wait_ge(s_modrep, 1)
            act.wait_ge(s_const, 2)
            A.activation(g.mod_rep[:, 1, :, :], ps_m[:, :, 0:P], ACT.Copy)
            A.activation(g.mod_rep[:, 0, :, :], ps_m[:, :, P:2 * P], ACT.Identity, bias=g.ones[:, 0:1])
            A.activation(g.mod_rep[:, 2, :, :], ps_m[:, :, 2 * P:3 * P], ACT.Copy)
            act.wait_ge(s_mv, 1)
            A.activation(sd[:, :], mv[:, :, 1], ACT.Sqrt, bias=g.eps[:, 0:1]).then_inc(s_sd, 1)
            act.wait_ge(s_modT, 1)
            for n in range(GROUPS):
                cols, b = slice(n * 512, n * 512 + 512), n * 512 // L
                act.wait_ge(s_xt, n + 1)
                A.activation(g.hT[:, cols], ps_x[:, n % 2, :], ACT.Identity, scale=g.modT[:, 1, b:b + 1],
                             bias=g.modT[:, 0, b:b + 1]).then_inc(s_h, 1)
                act.wait_ge(s_h, n + 1)
                A.activation(g.hT_hi[:, cols], g.hT[:, cols], ACT.Copy).then_inc(s_hi, 1)

        @block.vector
        def _(dve):
            done = [0]

            def link(ins):
                done[0] += 1
                ins.then_inc(s_v, 1)
                dve.wait_ge(s_v, done[0])

            V = nc.vector

            def token_stats(b):
                dve.wait_ge(s_x[b], 16)
                for t in range(8 * b, 8 * b + 8):
                    last = V.bn_stats(st[:, t, :], x[:, t, :])
                last.then_inc(s_st, 1)

            token_stats(0)
            token_stats(1)
            dve.wait_ge(s_vec, 1)
            V.tensor_copy(g.vecT[:, 0:N_VEC], ps_a[:, 0:N_VEC]).then_inc(s_vecT, 1)
            token_stats(2)
            dve.wait_ge(s_vecT, 1)
            dve.wait_ge(s_exp, 1)
            link(V.tensor_scalar_add(silu[:, 1, :], silu[:, 0, :], 1.0))
            link(V.reciprocal(silu[:, 2, :], silu[:, 1, :]))
            link(V.tensor_tensor(silu[:, 3, :], silu[:, 2, :], g.vecT[:, C_C:C_C + 4], ALU.mult))
            V.tensor_copy(silu_rep[:, :, :], silu[:, 3, :].unsqueeze(2).to_broadcast([P, B, P])).then_inc(s_silu, 1)
            token_stats(3)
            dve.wait_ge(s_st, B)
            for t in range(TILES):
                last = V.bn_aggr(mv[:, t, :], st[:, t, :])
            last.then_inc(s_mv, 1)
            dve.wait_ge(s_mod, 1)
            link(V.tensor_copy(g.modT[:, :, :], ps_b[:, 0:24].rearrange("p (a b) -> p a b", a=6)))
            V.tensor_scalar_add(g.modT[:, 1, :], g.modT[:, 1, :], 1.0).then_inc(s_modT, 1)

            dve.wait_ge(s_sd, 1)
            V.reciprocal(rs[:, :], sd[:, :]).then_inc(s_rs, 1)
            dve.wait_ge(s_rs, 1)
            dve.wait_ge(s_mv, 1)

            def body(n, u):
                wait(dve, s_xt, n - 1)
                for i in range(4):
                    last = V.tensor_scalar(xn[:, u, i:i + 1, :], x[:, at(4 * n + i, 1), :], mv[:, at(4 * n + i, 1), 0],
                                           rs[:, at(4 * n + i, 1)], ALU.subtract, ALU.mult)
                last.then_inc(s_xn, 1)

            run_pairs(dve, GROUPS, body)

            link(V.tensor_scalar_add(g.modT[:, 4, :], g.modT[:, 4, :], 1.0))
            ga = g.modT[:, 2, :]
            link(V.scalar_tensor_tensor(tmpT[:, 0, :], ga, -1.0, ga, op0=ALU.mult, op1=ALU.max))
            link(V.tensor_scalar_max(tmpT[:, 1, :], tmpT[:, 0, :], GUARD))
            link(V.tensor_scalar(tmpT[:, 2, :], ga, 0.0, 2.0, ALU.is_ge, ALU.mult))
            link(V.scalar_tensor_tensor(g.gaT[:, :], tmpT[:, 2, :], 1.0, tmpT[:, 1, :], op0=ALU.subtract, op1=ALU.mult))
            dve.wait_ge(s_bv, 1)
            link(V.tensor_tensor(tmpT[:, 3, 0:1], ps_b[:, 64:65], g.vecT[:, C_BFC:C_BFC + 1], ALU.add))
            V.tensor_scalar(g.gacT[:, :], g.gaT[:, :], tmpT[:, 3, 0:1], None, ALU.mult)

        @block.tensor
        def _(pe):
            T = nc.tensor
            pe.wait_ge(s_id, 2)
            pe.wait_ge(s_const, 2)
            pe.wait_ge(s_rows, 16 * N_ROW_DMAS)
            T.matmul(ps_a[:, 256:512], g.ones[0:1, :], on_row[0:1, :], start=True, stop=True)
            T.transpose(ps_a[:, 0:N_VEC], rows[0:N_VEC, :], g.ident[0:N_VEC, 0:N_VEC]).then_inc(s_vec, 1)
            pe.wait_ge(s_wm, 16)
            pe.wait_ge(s_silu, 1)
            for k in range(6):
                last = T.matmul(ps_b[:, 4 * k:4 * k + 4], wm[:, k * P:(k + 1) * P], silu[:, 3, :], start=True, stop=True)
            last.then_inc(s_mod, 1)
            for b in range(B):
                last = T.matmul(ps_m[:, b, 0:3 * P], silu_rep[:, b, :], wm[:, 3 * P:6 * P], start=True, stop=True)
            last.then_inc(s_modrep, 1)

            def body(n, u):
                pe.wait_ge(s_xn, n + 1)
                wait(pe, s_h, n - 1)
                for i in range(4):
                    last = T.transpose(ps_x[:, u, i * P:(i + 1) * P], xn[:, u, i, :], g.ident[:, :])
                last.then_inc(s_xt, 1)

            run_pairs(pe, GROUPS, body)
            pe.wait_ge(s_wfc, 16)
            pe.wait_ge(s_modT, 1)
            for k in range(8):
                last = T.matmul(ps_b[:, 64:65], wfc[:, k, :], g.vecT[:, C_BV + k:C_BV + k + 1],
                                start=(k == 0), stop=(k == 7))
            last.then_inc(s_bv, 1)


def attention_stage(nc, g):
    B, L, H = g.B, g.L, g.H
    NP = B * H // 2
    PAIRS = H // 2
    SCALE = 0.125
    with ExitStack() as ctx:
        def sb(name, shape, dt=F32):
            return ctx.enter_context(nc.sbuf_tensor(name, shape, dt))

        def psum(name, shape):
            return ctx.enter_context(nc.psum_tensor(name, shape, F32))

        def sem(name):
            return ctx.enter_context(nc.semaphore(name))

        QA = sb("QA", [P, 2, 2, L], F32R)
        QB = sb("QB", [P, 2, 2, L], F32R)
        KA = sb("KA", [P, 2, 2, L], F32R)
        KB = sb("KB", [P, 2, 2, L], F32R)
        V = sb("V", [P, 2, 8, P])
        PR = sb("PR", [P, 8, 2, 512])
        ACC = sb("ACC", [P, 2, 2, 512])
        Wraw = sb("Wraw", [P, 2, 2, 3, 64])
        Whi = sb("Whi", [P, 2, 2, 64], F32R)
        Wlo = sb("Wlo", [P, 2, 2, 64], F32R)
        bias = sb("bias", [P, 2, 2])
        Wfc = sb("Wfc", [P, 2, P])
        hcur = sb("hcur", [P, L])
        raw = sb("raw", [P, 2, 512])
        SUM = sb("SUM", [P, 512])
        O = sb("O", [P, 512])
        NMH = sb("NMH", [P, 2, 2, 4, 2])
        NM = sb("NM", [P, 2, 2, 4])
        mask = sb("mask", [P, 4, P])

        ps_s = psum("ps_s", [P, 2, 512])
        ps_mx = psum("ps_mx", [P, 2, 512])
        ps_o = psum("ps_o", [P, 2, 512])
        ps_w2 = psum("ps_w2", [P, 2, 512])

        s_init = sem("a_init")
        s_gb = sem("a_gate_rows")
        s_mask = sem("a_mask")
        wraw_in, hcur_in, wfc_in = [sem("wraw_in0"), sem("wraw_in1")], sem("hcur_in"), [sem("wfc_in0"), sem("wfc_in1")]
        kdup, qdup = [sem("kdup0"), sem("kdup1")], [[sem(f"qdup{u}{ch}") for ch in range(2)] for u in range(2)]
        scored, pv_done, mx_done = sem("scored"), sem("pv_done"), sem("mx_done")
        k_proj, q_proj, v_proj = sem("k_proj"), sem("q_proj"), sem("v_proj")
        rows_t, sums_mm, fc_mm = sem("rows_t"), sem("sums_mm"), sem("fc_mm")
        exp_done, k_hi, q_hi, v_copied, o_copied, w_hi = (sem("exp_done"), sem("k_hi"), sem("q_hi"),
                                                          sem("v_copied"), sem("o_copied"), sem("w_hi"))
        mx_red, k_lo, q_lo, neg_rows, recip, o_norm, fc_added, w_lo = (
            sem("mx_red"), sem("k_lo"), sem("q_lo"), sem("neg_rows"), sem("recip"), sem("o_norm"),
            sem("fc_added"), sem("w_lo"))
        added, raw_in, sums_in, mx_both = sem("added"), sem("raw_in"), sem("sums_in"), sem("mx_both")

        wqkv = g.W_qkv.rearrange("e (p h t d) -> e p h t d", h=2, t=3, d=64)
        wfc_v = g.W_fc.rearrange("(k p) e -> p k e", p=P)

        def place(s):
            if s < 6:
                i = s + 2
                return 0, 1, i // 4, i % 4
            if s < 14:
                i = s - 6
                return 1, 0, i // 4, i % 4
            i = s - 14
            return 1, 1, i // 4, i % 4

        UNITS = {0: ("k", 1, 0), 1: ("k", 1, 1), 2: ("sums", -1, 1), 3: ("q", 1, 0),
                 6: ("rows", 0, 1), 7: ("fc", -1, 1), 8: ("q", 1, 1), 9: ("v", 1, 0),
                 10: ("sums", 0, 0), 11: ("v", 1, 1), 14: ("rows", 1, 0), 15: ("fc", 0, 0)}
        INVERT = {2: (-1, 1, (0,)), 4: (-1, 1, (1, 2)), 5: (-1, 1, (3,)),
                  10: (0, 0, (0,)), 11: (0, 0, (1,)), 12: (0, 0, (2,)), 13: (0, 0, (3,))}
        ORDER = sorted(UNITS)

        def unit_at(n, s):
            if s not in UNITS:
                return None
            kind, d, ch = UNITS[s]
            if isinstance(n, int) and not 0 <= n + d < NP:
                return None
            return kind, n + d, ch

        FIRST_UNITS = [("k", 0), ("k", 1), ("q", 0), ("rows", 0), ("q", 1), ("v", 0), ("v", 1)]

        def unit_u(s, u):
            return u if UNITS[s][1] == 0 else 1 - u

        def raw_count(kind, m, ch):
            return 4 * m + (2 if kind == "q" else 0) + ch + 1

        def has(n):
            return not isinstance(n, int) or 0 <= n < NP

        def batch_cols(m, ch):
            b = m // PAIRS
            return ds(b * L + ch * 512, 512) if not isinstance(b, int) else slice(b * L + ch * 512, b * L + ch * 512 + 512)

        def col(base, m):
            p = m % PAIRS
            return ds(p + base, 1) if not isinstance(p, int) else slice(base + p, base + p + 1)

        def half(h):
            return slice(64 * h, 64 * h + 64)

        def other(h):
            return slice(64 - 64 * h, 128 - 64 * h)

        def run(eng, pair, first, last=None):
            run_pairs(eng, NP, pair, first, last)

        block = ctx.enter_context(nc.Block())

        @block.sync
        def _(sp):
            def load_w(m, u):
                wait(sp, v_proj, 2 * m - 2)
                p = m % PAIRS
                src = wqkv[:, p:p + 1, :, :, :] if isinstance(p, int) else wqkv[:, ds(p, 1), :, :, :]
                sp.dma_start(Wraw[:, u, :, :, :], src).then_inc(wraw_in[u], 16)

            def load_h(m):
                wait(sp, v_proj, 2 * m)
                b = m // PAIRS
                src = g.hT[:, b * L:(b + 1) * L] if isinstance(b, int) else g.hT[:, ds(b * L, L)]
                sp.dma_start(hcur[:, :], src).then_inc(hcur_in, 16)

            def load_fc(m, u):
                wait(sp, fc_mm, 2 * m - 2)
                p = m % PAIRS
                src = wfc_v[:, p:p + 1, :] if isinstance(p, int) else wfc_v[:, ds(p, 1), :]
                sp.dma_start(Wfc[:, u:u + 1, :], src).then_inc(wfc_in[u], 16)

            def dup_k(m, u, ch):
                q = slice(ch * 512, ch * 512 + 512)
                sp.wait_ge(k_hi, 2 * m + ch + 1)
                for h in range(2):
                    sp.dma_start(KA[other(h), u, h, q].bitcast(F32), KA[half(h), u, h, q].bitcast(F32)).then_inc(kdup[u], 16)

            def dup_q(m, u, ch):
                q = slice(ch * 512, ch * 512 + 512)
                sp.wait_ge(q_hi, 2 * m + ch + 1)
                for h in range(2):
                    sp.dma_start(QB[half(h), u, h, q].bitcast(F32), QA[half(h), u, h, q].bitcast(F32)).then_inc(qdup[u][ch], 16)

            def first():
                load_w(0, 0)
                load_h(0)
                load_w(1, 1)
                load_fc(0, 0)
                dup_k(0, 0, 0)
                dup_k(0, 0, 1)
                dup_q(0, 0, 0)
                dup_q(0, 0, 1)
                load_h(1)

            def pair(n, u):
                if has(n + 1):
                    dup_k(n + 1, 1 - u, 0)
                    dup_k(n + 1, 1 - u, 1)
                    dup_q(n + 1, 1 - u, 0)
                    load_fc(n + 1, 1 - u)
                    dup_q(n + 1, 1 - u, 1)
                if has(n + 2):
                    load_w(n + 2, u)
                    load_h(n + 2)

            run(sp, pair, first)

        @block.gpsimd
        def _(pool):
            G = nc.gpsimd

            def first():
                for h in range(2):
                    rest = other(h)
                    G.memset(QB[rest, :, h, :].bitcast(F32), 0.0)
                    G.memset(KB[rest, :, h, :].bitcast(F32), 0.0).then_inc(s_init, 1)
                pool.wait_ge(s_init, 2)
                for h in range(2):
                    top = slice(64 - 64 * h, 68 - 64 * h)
                    G.memset(KB[top, :, h, :].bitcast(F32), 1.0).then_inc(s_init, 1)
                pool.wait_ge(s_init, 4)
                G.memset(mask[:, :, :], 1.0).then_inc(s_mask, 1)
                pool.wait_ge(s_mask, 1)
                G.affine_select(out=mask[0:64, :, :], in_=mask[0:64, :, :], compare_op=ALU.is_equal, fill=0.0,
                                base=0, pattern=[[-1, 4], [0, P]], channel_multiplier=1).then_inc(s_mask, 1)
                G.affine_select(out=mask[64:128, :, :], in_=mask[64:128, :, :], compare_op=ALU.is_equal, fill=0.0,
                                base=0, pattern=[[-1, 4], [0, P]], channel_multiplier=1).then_inc(s_mask, 1)

            def pair(n, u):
                for ch in range(2):
                    chunk = 2 * n + ch
                    wait(pool, sums_mm, chunk - 1)
                    for t in range(1, 8):
                        pool.wait_ge(exp_done, 2 * (16 * n + 8 * ch + t + 1))
                        a = PR[:, 0, :, :] if t == 1 else ACC[:, ch, :, :]
                        if t > 1:
                            pool.wait_ge(added, 7 * chunk + t - 1)
                        G.tensor_tensor(ACC[:, ch, :, :], a, PR[:, t, :, :], ALU.add).then_inc(added, 1)

            run(pool, pair, first)

        @block.scalar
        def _(act):
            A = nc.scalar

            def split_w(m, u):
                A.activation(bias[:, u, 0:1], g.vecT[:, col(C_BQ, m)], ACT.Copy)
                A.activation(bias[:, u, 1:2], g.vecT[:, col(C_BK, m)], ACT.Copy)
                wait(act, wraw_in[u], (m // 2 + 1) * 16)
                wait(act, q_proj, 2 * m)
                for h in range(2):
                    last = A.activation(Whi[:, :, h, :], Wraw[:, u, h, 0:2, :], ACT.Copy)
                last.then_inc(w_hi, 1)

            def unit(kind, m, u, ch, ps_w):
                q = slice(ch * 512, ch * 512 + 512)
                if kind in "qk":
                    X, proj, ty, hi, lo = (KA, k_proj, 1, k_hi, k_lo) if kind == "k" else (QA, q_proj, 0, q_hi, q_lo)
                    act.wait_ge(proj, 2 * m + ch + 1)
                    if kind == "k":
                        wait(act, q_lo, 2 * m + ch - 1)
                    else:
                        act.wait_ge(k_lo, 2 * m + ch + 1)
                    A.activation(raw[:, ch, :], ps_w, ACT.Identity, bias=bias[:, u, ty:ty + 1]).then_inc(raw_in, 1)
                    act.wait_ge(raw_in, raw_count(kind, m, ch))
                    for h in range(2):
                        last = A.activation(X[half(h), u, h, q], raw[half(h), ch, :], ACT.Copy)
                    last.then_inc(hi, 1)
                elif kind == "v":
                    act.wait_ge(v_proj, 2 * m + ch + 1)
                    A.activation(flat(V[:, u, 4 * ch:4 * ch + 4, :]), ps_w, ACT.Copy).then_inc(v_copied, 1)
                elif kind == "sums":
                    act.wait_ge(sums_mm, 2 * m + ch + 1)
                    wait(act, o_norm, 2 * m + ch)
                    A.activation(SUM[:, :], ps_w, ACT.Copy).then_inc(sums_in, 1)

            def first():
                split_w(0, 0)
                for k, (kind, ch) in enumerate(FIRST_UNITS):
                    if kind != "rows":
                        unit(kind, 0, 0, ch, ps_w2[:, k % 2, :])
                split_w(1, 1)

            def copy_o(n, ch):
                act.wait_ge(pv_done, 16 * n + 8 * ch + 8)
                wait(act, fc_mm, 2 * n + ch)
                A.activation(O[:, :], ps_o[:, ch, :], ACT.Copy).then_inc(o_copied, 1)

            def pair(n, u):
                for s in range(16):
                    ch, t = divmod(s, 8)
                    chunk = 2 * n + ch
                    wait(act, pv_done, 16 * n + s - 7)
                    wait(act, added, 7 * (chunk - 1) + max(t, 1))
                    for h in range(2):
                        act.wait_ge(scored, 32 * n + 2 * s + h + 1)
                        A.activation(PR[:, t, h, :], ps_s[:, h, :], ACT.Exp, scale=SCALE).then_inc(exp_done, 1)
                    x = unit_at(n, s)
                    if x and x[0] not in ("rows", "fc"):
                        unit(x[0], x[1], unit_u(s, u), x[2], ps_w2[:, ORDER.index(s) % 2, :])
                    if s == 8:
                        copy_o(n, 0)
                    if s == 0 and has(n - 1):
                        copy_o(n - 1, 1)
                    if s == 12 and has(n + 2):
                        split_w(n + 2, u)

            def last():
                copy_o(NP - 1, 1)
                unit("sums", NP - 1, 1, 1, ps_w2[:, 0, :])

            run(act, pair, first, last)

        @block.vector
        def _(dve):
            D = nc.vector

            def split_w(m, u):
                dve.wait_ge(w_hi, m + 1)
                for h in range(2):
                    last = D.tensor_tensor(Wlo[:, :, h, :], Wraw[:, u, h, 0:2, :], Whi[:, :, h, :].bitcast(F32), ALU.subtract)
                last.then_inc(w_lo, 1)

            def reduce_max(m, ch, h, i, count):
                if h == 0 and i == 0:
                    wait(dve, mx_both, 2 * m + ch - 1)
                for kc in range(2):
                    dve.wait_ge(mx_done, 2 * count - 1 + kc)
                    D.tensor_reduce(NMH[:, ch, h, i, kc:kc + 1], ps_mx[:, kc, :], AX, ALU.max, negate=True).then_inc(mx_red, 1)
                if h == 1 and i == 3:
                    dve.wait_ge(mx_red, 2 * count)
                    wait(dve, rows_t, 2 * m + ch - 1)
                    D.tensor_tensor(NM[:, ch, :, :], NMH[:, ch, :, :, 0], NMH[:, ch, :, :, 1], ALU.min).then_inc(mx_both, 1)

            def unit(kind, m, u, ch, ps_w):
                q = slice(ch * 512, ch * 512 + 512)
                if kind == "k":
                    dve.wait_ge(k_hi, 2 * m + ch + 1)
                    for h in range(2):
                        last = D.tensor_tensor(KB[half(h), u, h, q], raw[half(h), ch, :], KA[half(h), u, h, q].bitcast(F32), ALU.subtract)
                    last.then_inc(k_lo, 1)
                elif kind == "q":
                    dve.wait_ge(q_hi, 2 * m + ch + 1)
                    for h in range(2):
                        last = D.tensor_tensor(QA[other(h), u, h, q], raw[half(h), ch, :], QA[half(h), u, h, q].bitcast(F32), ALU.subtract)
                    last.then_inc(q_lo, 1)
                elif kind == "rows":
                    dve.wait_ge(rows_t, 2 * m + ch + 1)
                    for h in range(2):
                        top = slice(64 - 64 * h, 68 - 64 * h)
                        rows = ps_w[top, h * P:(h + 1) * P].unsqueeze(1).to_broadcast([4, 4, P])
                        last = D.tensor_tensor(QB[top, u, h, q].rearrange("p (i q) -> p i q", i=4), rows, mask[top, :, :], ALU.mult)
                    last.then_inc(neg_rows, 1)
                elif kind == "fc":
                    dve.wait_ge(fc_mm, 2 * m + ch + 1)
                    wait(dve, fc_added, 2 * m + ch)
                    cols = batch_cols(m, ch)
                    D.tensor_tensor(g.attnT[:, cols], g.attnT[:, cols], ps_w, ALU.add).then_inc(fc_added, 1)

            def invert(m, ch, part):
                q = slice(part * P, part * P + P)
                dve.wait_ge(sums_in, 2 * m + ch + 1)
                D.reciprocal(SUM[:, q], SUM[:, q]).then_inc(recip, 1)
                if part == 3:
                    dve.wait_ge(recip, 4 * (2 * m + ch + 1))
                    dve.wait_ge(o_copied, 2 * m + ch + 1)
                    D.tensor_tensor(O[:, :], O[:, :], SUM[:, :], ALU.mult).then_inc(o_norm, 1)

            def first():
                split_w(0, 0)
                for kind, ch in FIRST_UNITS[:3]:
                    unit(kind, 0, 0, ch, None)
                for i in range(8):
                    reduce_max(0, 0, i // 4, i % 4, i + 1)
                dve.wait_ge(s_mask, 3)
                dve.wait_ge(s_init, 4)
                unit("rows", 0, 0, 0, ps_w2[:, 1, :])
                unit("q", 0, 0, 1, None)
                for i in range(2):
                    reduce_max(0, 1, i // 4, i % 4, i + 9)
                split_w(1, 1)

            def pair(n, u):
                for s in range(16):
                    d, ch, h, i = place(s)
                    if has(n + d):
                        reduce_max(n + d, ch, h, i, 16 * n + s + 11)
                    x = unit_at(n, s)
                    if x:
                        unit(x[0], x[1], unit_u(s, u), x[2], ps_w2[:, ORDER.index(s) % 2, :])
                    if s in INVERT and has(n + INVERT[s][0]):
                        for part in INVERT[s][2]:
                            invert(n + INVERT[s][0], INVERT[s][1], part)
                    if s == 12 and has(n + 2):
                        split_w(n + 2, u)
                    if isinstance(n, int) and n == 1 and s in range(3, 9):
                        gate_rows(s - 3)

            def gate_rows(step):
                gb, t = g.mod_rep[:, 2, :, :], g.mod_rep[:, 3, :, :]
                if step:
                    dve.wait_ge(s_gb, step)
                if step == 0:
                    ins = D.scalar_tensor_tensor(t, gb, -1.0, gb, op0=ALU.mult, op1=ALU.max)
                elif step == 1:
                    ins = D.tensor_scalar_max(t, t, GUARD)
                elif step == 2:
                    ins = D.tensor_scalar(gb, gb, 0.0, 2.0, ALU.is_ge, ALU.mult)
                elif step == 3:
                    ins = D.scalar_tensor_tensor(t, gb, 1.0, t, op0=ALU.subtract, op1=ALU.mult)
                elif step == 4:
                    ins = D.tensor_tensor(gb, t, g.on_rep[:, 0:1, :].to_broadcast([P, B, P]), ALU.mult)
                else:
                    ins = D.tensor_tensor(t, t, g.on_rep[:, 1:2, :].to_broadcast([P, B, P]), ALU.mult)
                ins.then_inc(s_gb, 1)

            def last():
                for part in range(4):
                    invert(NP - 1, 1, part)
                unit("fc", NP - 1, 1, 1, ps_w2[:, 1, :])

            run(dve, pair, first, last)

        @block.tensor
        def _(pe):
            T = nc.tensor

            def unit(kind, m, u, ch, ps_w):
                q = slice(ch * 512, ch * 512 + 512)
                if kind in "qk":
                    ty = 0 if kind == "q" else 1
                    pe.wait_ge(w_lo, m + 1)
                    hi, lo = g.hT_hi[:, batch_cols(m, ch)], g.hT_lo[:, batch_cols(m, ch)]
                    wh, wl = flat(Whi[:, ty, :, :]), flat(Wlo[:, ty, :, :])
                    T.matmul(ps_w[:, :], wh, hi, start=True, stop=False)
                    T.matmul(ps_w[:, :], wl, hi, start=False, stop=False)
                    T.matmul(ps_w[:, :], wh, lo, start=False, stop=True).then_inc(q_proj if kind == "q" else k_proj, 1)
                elif kind == "v":
                    pe.wait_ge(hcur_in, 16 * (m + 1))
                    pe.wait_ge(wraw_in[u], 16 * (m // 2 + 1))
                    for i in range(4):
                        t = 4 * ch + i
                        last = T.matmul(ps_w[:, i * P:(i + 1) * P], hcur[:, t * P:(t + 1) * P], Wraw[:, u, :, 2, :],
                                        start=True, stop=True)
                    last.then_inc(v_proj, 1)
                elif kind == "rows":
                    for h in range(2):
                        last = T.matmul(ps_w[64 - 64 * h:68 - 64 * h, h * P:(h + 1) * P], NM[:, ch, h, :], g.ident[:, :],
                                        start=True, stop=True)
                    last.then_inc(rows_t, 1)
                elif kind == "sums":
                    pe.wait_ge(added, 14 * m + 7 * ch + 7)
                    for h in range(2):
                        last = T.matmul(ps_w[half(h), :], g.ones[:, 0:64], ACC[:, ch, h, :], start=True, stop=True)
                    last.then_inc(sums_mm, 1)
                elif kind == "fc":
                    pe.wait_ge(o_norm, 2 * m + ch + 1)
                    pe.wait_ge(wfc_in[u], 16 * (m // 2 + 1))
                    T.matmul(ps_w[:, :], Wfc[:, u, :], O[:, :], start=True, stop=True).then_inc(fc_mm, 1)

            def freed(kind, m, ch):
                if kind == "k" or kind == "q":
                    pe.wait_ge(raw_in, raw_count(kind, m, ch))
                else:
                    pe.wait_ge({"v": v_copied, "rows": neg_rows, "sums": sums_in, "fc": fc_added}[kind], 2 * m + ch + 1)

            def max_half(m, u, ch, h, i, kc, count):
                wait(pe, mx_red, 2 * count - 1 + kc)
                if h == 0 and i == 0 and kc == 0:
                    pe.wait_ge(q_lo, 2 * m + ch + 1)
                    if ch == 0:
                        pe.wait_ge(k_hi, 2 * m + 2)
                        pe.wait_ge(kdup[u], 64 * (m // 2 + 1))
                q = ch * 512 + i * P
                T.matmul(ps_mx[:, kc, :], QA[:, u, h, q:q + P], KA[:, u, h, kc * 512:(kc + 1) * 512],
                         start=True, stop=True).then_inc(mx_done, 1)

            def scores(n, u, s):
                ch, t = divmod(s, 8)
                q, k = slice(ch * 512, ch * 512 + 512), slice(t * P, (t + 1) * P)
                if t == 0:
                    pe.wait_ge(neg_rows, 2 * n + ch + 1)
                    pe.wait_ge(qdup[u][ch], 32 * (n // 2) + 32)
                    if ch == 0:
                        pe.wait_ge(k_lo, 2 * n + 2)
                for h in range(2):
                    wait(pe, exp_done, 32 * n + 2 * s + h - 1)
                    T.matmul(ps_s[:, h, :], KA[:, u, h, k], QA[:, u, h, q], start=True, stop=False)
                    T.matmul(ps_s[:, h, :], KB[:, u, h, k], QB[:, u, h, q], start=False, stop=True).then_inc(scored, 1)

            def times_v(n, u, s):
                ch, t = divmod(s, 8)
                pe.wait_ge(exp_done, 32 * n + 2 * s + 2)
                if t == 0:
                    wait(pe, o_copied, 2 * n + ch - 1)
                    pe.wait_ge(v_copied, 2 * n + 2)
                for h in range(2):
                    last = T.matmul(ps_o[half(h), ch, :], V[:, u, t, half(h)], PR[:, t, h, :], start=(t == 0), stop=(t == 7))
                last.then_inc(pv_done, 1)

            def first():
                for k, (kind, ch) in enumerate(FIRST_UNITS):
                    if k >= 2:
                        freed(FIRST_UNITS[k - 2][0], 0, FIRST_UNITS[k - 2][1])
                    if kind == "rows":
                        for i in range(8):
                            for kc in range(2):
                                max_half(0, 0, 0, i // 4, i % 4, kc, i)
                        pe.wait_ge(mx_both, 1)
                    unit(kind, 0, 0, ch, ps_w2[:, k % 2, :])
                for i in range(2):
                    for kc in range(2):
                        max_half(0, 0, 1, i // 4, i % 4, kc, i + 8)
                freed("v", 0, 0)
                freed("v", 0, 1)

            def v_of_last_step(n, u, s):
                if s > 0:
                    times_v(n, u, s - 1)
                elif has(n - 1):
                    times_v(n - 1, 1 - u, 15)

            def pair(n, u):
                for s in range(16):
                    d, ch, h, i = place(s)
                    grp = (n + d, u if d == 0 else 1 - u, ch, h, i)
                    scores(n, u, s)
                    if has(n + d):
                        max_half(*grp, 0, 16 * n + s + 10)
                    x = unit_at(n, s)
                    if not x or x[0] == "rows":
                        v_of_last_step(n, u, s)
                    if x:
                        k = ORDER.index(s) - 2
                        before = unit_at(n, ORDER[k]) if k >= 0 else has(n - 1) and unit_at(n - 1, ORDER[k])
                        if before:
                            freed(*before)
                        if x[0] == "rows":
                            pe.wait_ge(mx_both, 2 * x[1] + x[2] + 1)
                        unit(x[0], x[1], unit_u(s, u), x[2], ps_w2[:, ORDER.index(s) % 2, :])
                    if x and x[0] != "rows":
                        v_of_last_step(n, u, s)
                    if has(n + d):
                        max_half(*grp, 1, 16 * n + s + 10)

            def last():
                times_v(NP - 1, 1, 15)
                freed("sums", NP - 1, 0)
                unit("sums", NP - 1, 1, 1, ps_w2[:, 0, :])
                freed("fc", NP - 1, 0)
                unit("fc", NP - 1, 1, 1, ps_w2[:, 1, :])

            run(pe, pair, first, last)


def router_stage(nc, g, f):
    B, L = g.B, g.L
    GROUPS = B * L // 512
    TILES = 4 * GROUPS
    GPB = L // 512
    with ExitStack() as ctx:
        def sb(name, shape, dt=F32):
            return ctx.enter_context(nc.sbuf_tensor(name, shape, dt))

        def sem(name):
            return ctx.enter_context(nc.semaphore(name))

        yT = sb("r_yT", [P, 2, 512])
        st = sb("r_st", [P, TILES, 6])
        mv = sb("r_mv", [P, TILES, 2])
        sd = sb("r_sd", [P, TILES])
        rs = sb("r_rs", [P, TILES])
        n2 = sb("r_n2", [P, 2, 4, P])
        centre = sb("r_centre", [P, P])
        hc = sb("r_hc", [P, 2, 512])
        sq = sb("r_sq", [P, 2, 512])
        hT = sb("r_hT", [P, 2, 512])
        mean_col = sb("r_mean_col", [P, 1])
        sd2 = sb("r_sd2", [P, TILES])
        rs2 = sb("r_rs2", [P, TILES])
        lg = sb("r_lg", [P, 4, TILES, 4])
        lt = sb("r_lt", [P, 4, TILES])
        cmp_ = sb("r_cmp", [P, 2, TILES, 4, 4])
        zero = sb("r_zero", [1, 1])
        spot = sb("r_spot", [1, 1, GROUPS])
        tri = sb("r_tri", [P, 2, 4, 4])
        ps_y = ctx.enter_context(nc.psum_tensor("ps_y", [P, 2, 512], F32))
        ps_n = ctx.enter_context(nc.psum_tensor("ps_n", [P, 2, 512], F32))
        ps_c = ctx.enter_context(nc.psum_tensor("ps_c", [P, 2, 512], F32))
        ps_l = ctx.enter_context(nc.psum_tensor("ps_l", [P, 512], F32))
        ps_v = ctx.enter_context(nc.psum_tensor("ps_v", [P, 512], F32))
        logit = ps_l[:, 0:4 * TILES].rearrange("p (t e) -> p t e", e=4)

        s_x, s_y, s_yt, s_x2, s_st, s_mv, s_sd, s_rs = (sem("r_x"), sem("r_y"), sem("r_yt"), sem("r_x2"), sem("r_st_"),
                                                        sem("r_mv_"), sem("r_sd_"), sem("r_rs_"))
        s_n2, s_nt, s_hT, s_cm, s_hc, s_sq, s_sd2 = (sem("r_n2_"), sem("r_nt"), sem("r_hT_"), sem("r_cm"), sem("r_hc_"),
                                                     sem("r_sq_"), sem("r_sd2_"))
        s_logit, s_tri, s_ex, s_e, s_c, s_cen, s_rw, s_sum = (sem("r_logit"), sem("r_tri_"), sem("r_exp_in"), sem("r_exp"),
                                                              sem("r_chain"), sem("r_cen"), sem("r_rw"), sem("r_sum"))
        s_stored = [sem("r_stored0"), sem("r_stored1")]

        xv = g.X.rearrange("b l e -> (b l) e").rearrange("(t p) e -> p t e", p=P)
        block = ctx.enter_context(nc.Block())

        @block.sync
        def _(sp):
            for b in range(B):
                sp.dma_start(f.x2[:, 8 * b:8 * b + 8, :], xv[:, 8 * b:8 * b + 8, :]).then_inc(s_x, 16)
            sp.dma_start(f.w1[:, :, :], g.w1.rearrange("e d h -> d e h")).then_inc(f.s_w, 16)
            sp.dma_start(f.w2[:, :, :], g.w2.rearrange("e (a p) d -> p (e a) d", p=P)).then_inc(f.s_w, 16)

            def body(n, u):
                sp.wait_ge(s_hT, n + 1)
                sp.dma_start(f.hT2[:, at(512 * n, 512)], hT[:, u, :]).then_inc(s_stored[u], 16)

            run_pairs(sp, GROUPS, body)
            for u in range(2):
                sp.wait_ge(s_stored[u], 16 * GROUPS // 2)

        @block.gpsimd
        def _(pool):
            G = nc.gpsimd
            G.memset(mean_col[:, :], 1.0 / P).then_inc(s_cen, 1)
            G.memset(centre[:, :], -1.0 / P).then_inc(s_cen, 1)
            pool.wait_ge(s_cen, 2)
            G.affine_select(out=centre[:, :], in_=centre[:, :], compare_op=ALU.not_equal, fill=1.0 - 1.0 / P,
                            base=0, pattern=[[-1, P]], channel_multiplier=1).then_inc(s_cen, 1)
            G.memset(tri[:, :, :, :], 1.0).then_inc(s_tri, 1)
            pool.wait_ge(s_tri, 1)
            G.affine_select(out=tri[:, 0, :, :], in_=tri[:, 0, :, :], compare_op=ALU.is_gt, fill=0.0, base=0,
                            pattern=[[1, 4], [-1, 4]], channel_multiplier=0).then_inc(s_tri, 1)
            G.affine_select(out=tri[:, 1, :, :], in_=tri[:, 1, :, :], compare_op=ALU.is_gt, fill=0.0, base=0,
                            pattern=[[-1, 4], [1, 4]], channel_multiplier=0).then_inc(s_tri, 1)

        @block.scalar
        def _(act):
            A = nc.scalar
            act.wait_ge(s_mv, 1)
            A.activation(sd[:, :], mv[:, :, 1], ACT.Sqrt, bias=g.eps[:, 0:1]).then_inc(s_sd, 1)

            def centred(n):
                act.wait_ge(s_cm, n + 1)
                if n >= 2:
                    act.wait_ge(s_logit, n - 1)
                A.activation(hc[:, n % 2, :], ps_c[:, n % 2, :], ACT.Copy).then_inc(s_hc, 1)
                A.activation(sq[:, n % 2, :], ps_c[:, n % 2, :], ACT.Square).then_inc(s_sq, 1)

            for n in range(GROUPS):
                act.wait_ge(s_nt, n + 1)
                if n >= 2:
                    act.wait_ge(s_cm, n - 1)
                    act.wait_ge(s_stored[n % 2], 16 * (n // 2))
                A.activation(hT[:, n % 2, :], ps_n[:, n % 2, :], ACT.Identity, scale=g.modT[:, 4, n // GPB:n // GPB + 1],
                             bias=g.modT[:, 3, n // GPB:n // GPB + 1]).then_inc(s_hT, 1)
                if n >= 1:
                    centred(n - 1)
            centred(GROUPS - 1)
            act.wait_ge(s_logit, GROUPS)
            A.activation(sd2[:, :], ps_v[:, 0:TILES], ACT.Sqrt, bias=g.eps[:, 0:1]).then_inc(s_sd2, 1)
            act.wait_ge(s_ex, 1)
            A.activation(lg[:, 3, :, :], lg[:, 2, :, :], ACT.Exp).then_inc(s_e, 1)

        @block.vector
        def _(dve):
            D = nc.vector
            done = [0]

            def link(ins):
                done[0] += 1
                ins.then_inc(s_c, 1)
                dve.wait_ge(s_c, done[0])

            def one(ap):
                return ap.rearrange("p a b -> p (a b)")

            link(D.memset(zero[:, :], 0.0))
            D.tensor_scalar(g.rw[:, 0:4], g.vecT[:, C_RW:C_RW + 4], g.vecT[:, C_RNG:C_RNG + 1], None, ALU.mult)
            D.tensor_scalar(g.rw[:, 4:8], g.vecT[:, C_RW:C_RW + 4], g.vecT[:, C_RNB:C_RNB + 1], None, ALU.mult).then_inc(s_rw, 1)
            dve.wait_ge(s_sum, 1)
            link(D.tensor_copy(g.rw_sum[:, :], ps_v[:, 64:68]))

            def gated(n, u):
                b = n // GPB
                wait(dve, s_yt, n - 1)
                D.tensor_scalar(yT[:, u, :], g.attnT[:, at(512 * n, 512)], g.gaT[:, at(b, 1)], g.gacT[:, at(b, 1)], ALU.mult, ALU.add).then_inc(s_y, 1)

            def add_x(n, u):
                dve.wait_ge(s_yt, n + 1)
                x2 = f.x2[:, at(4 * n, 4), :]
                D.tensor_tensor(x2, x2, ps_y[:, u, :].rearrange("p (a b) -> p a b", a=4), ALU.add).then_inc(s_x2, 1)

            def stats(n):
                dve.wait_ge(s_x2, n + 1)
                carry(D, spot, zero, 0, n)
                for i in range(4):
                    last = D.bn_stats(one(st[:, at(4 * n + i, 1), :]), one(f.x2[:, at(4 * n + i, 1), :]))
                last.then_inc(s_st, 1)

            def body(n, u):
                if isinstance(n, int) and n == GROUPS - 1:
                    pass
                else:
                    gated(n + 1, 1 - u)
                add_x(n, u)
                if not isinstance(n, int) or n > 0:
                    stats(n - 1)

            def first():
                gated(0, 0)
                dve.wait_ge(s_x, 16 * B)

            run_pairs(dve, GROUPS, body, first, lambda: stats(GROUPS - 1))
            dve.wait_ge(s_st, GROUPS)
            for t in range(TILES):
                last = D.bn_aggr(mv[:, t, :], st[:, t, :])
            last.then_inc(s_mv, 1)
            dve.wait_ge(s_sd, 1)
            dve.wait_ge(s_mv, 1)
            D.reciprocal(rs[:, :], sd[:, :]).then_inc(s_rs, 1)
            dve.wait_ge(s_rs, 1)

            def body2(n, u):
                wait(dve, s_nt, n - 1)
                for i in range(4):
                    last = D.tensor_scalar(n2[:, u, i:i + 1, :], f.x2[:, at(4 * n + i, 1), :], mv[:, at(4 * n + i, 1), 0],
                                           rs[:, at(4 * n + i, 1)], ALU.subtract, ALU.mult)
                last.then_inc(s_n2, 1)

            run_pairs(dve, GROUPS, body2)

            def per_e(ap):
                return ap.unsqueeze(1).to_broadcast([P, TILES, 4])

            def per_t(ap):
                return ap.unsqueeze(2).to_broadcast([P, TILES, 4])

            dve.wait_ge(s_sd2, 1)
            link(D.reciprocal(rs2[:, :], sd2[:, :]))
            dve.wait_ge(s_logit, GROUPS)
            link(D.tensor_tensor(lg[:, 0, :, :], logit, per_t(rs2[:, :]), ALU.mult))
            link(D.tensor_tensor(lg[:, 1, :, :], lg[:, 0, :, :], per_e(g.rw_sum[:, :]), ALU.add))
            link(D.tensor_reduce(lt[:, 0, :], lg[:, 1, :, :], AX, ALU.max))
            D.tensor_tensor(lg[:, 2, :, :], lg[:, 1, :, :], per_t(lt[:, 0, :]), ALU.subtract).then_inc(s_ex, 1)
            dve.wait_ge(s_e, 1)
            link(D.tensor_reduce(lt[:, 1, :], lg[:, 3, :, :], AX, ALU.add))
            link(D.reciprocal(lt[:, 2, :], lt[:, 1, :]))
            pr = lg[:, 1, :, :]
            link(D.tensor_tensor(pr, lg[:, 3, :, :], per_t(lt[:, 2, :]), ALU.mult))
            dve.wait_ge(s_tri, 3)
            for e in range(4):
                pe_ = lg[:, 1, :, e:e + 1].to_broadcast([P, TILES, 4])
                D.tensor_tensor(cmp_[:, 0, :, e, :], pr, pe_, ALU.is_ge)
                last = D.tensor_tensor(cmp_[:, 1, :, e, :], pr, pe_, ALU.is_gt)
            link(last)
            for k in range(2):
                t = tri[:, k:k + 1, :, :].rearrange("p a e j -> p a (e j)").to_broadcast([P, TILES, 16])
                ck = cmp_[:, k, :, :, :].rearrange("p t e j -> p t (e j)")
                last = D.tensor_tensor(ck, ck, t, ALU.mult)
            link(last)
            c0, c1 = (cmp_[:, k, :, :, :].rearrange("p t e j -> p (t e j)") for k in range(2))
            link(D.tensor_tensor(c0, c0, c1, ALU.add))
            link(D.tensor_reduce(lg[:, 0, :, :], cmp_[:, 0, :, :, :], AX, ALU.add))
            link(D.scalar_tensor_tensor(flat(lg[:, 2, :, :]), flat(lg[:, 0, :, :]), 2.0, flat(pr), op0=ALU.is_lt, op1=ALU.mult))
            link(D.tensor_reduce(lt[:, 3, :], lg[:, 2, :, :], AX, ALU.add))
            link(D.tensor_scalar_add(lt[:, 0, :], lt[:, 3, :], EPS_GATE))
            link(D.reciprocal(lt[:, 1, :], lt[:, 0, :]))
            link(D.tensor_tensor(f.gate[:, :, :], lg[:, 2, :, :], per_t(lt[:, 1, :]), ALU.mult))

        @block.tensor
        def _(pe):
            T = nc.tensor

            def body(n, u):
                pe.wait_ge(s_y, n + 1)
                wait(pe, s_x2, n - 1)
                for i in range(4):
                    last = T.transpose(ps_y[:, u, i * P:(i + 1) * P], yT[:, u, i * P:(i + 1) * P], g.ident[:, :])
                last.then_inc(s_yt, 1)

            pe.wait_ge(s_rw, 1)
            T.matmul(ps_v[:, 64:68], g.ones[:, :], g.rw[:, 4:8], start=True, stop=True).then_inc(s_sum, 1)
            run_pairs(pe, GROUPS, body)
            pe.wait_ge(s_cen, 3)

            def centring(n, u):
                pe.wait_ge(s_hT, n + 1)
                wait(pe, s_sq, n - 1)
                T.matmul(ps_c[:, u, :], centre[:, :], hT[:, u, :], start=True, stop=True).then_inc(s_cm, 1)

            def logits(n, u):
                pe.wait_ge(s_hc, n + 1)
                pe.wait_ge(s_sq, n + 1)
                for i in range(4):
                    T.matmul(ps_l[:, at(16 * n + 4 * i, 4)], hc[:, u, i * P:(i + 1) * P], g.rw[:, 0:4], start=True, stop=True)
                    last = T.matmul(ps_v[:, at(4 * n + i, 1)], sq[:, u, i * P:(i + 1) * P], mean_col[:, :], start=True, stop=True)
                last.then_inc(s_logit, 1)

            def body2(n, u):
                pe.wait_ge(s_n2, n + 1)
                wait(pe, s_hT, n - 1)
                for i in range(4):
                    last = T.transpose(ps_n[:, u, i * P:(i + 1) * P], n2[:, u, i, :], g.ident[:, :])
                last.then_inc(s_nt, 1)
                if not isinstance(n, int) or n > 0:
                    centring(n - 1, 1 - u)
                if not isinstance(n, int) or n > 1:
                    logits(n - 2, u)

            def last():
                centring(GROUPS - 1, 1)
                logits(GROUPS - 2, 0)
                logits(GROUPS - 1, 1)

            run_pairs(pe, GROUPS, body2, None, last)


def experts_stage(nc, g, f):
    B, L = g.B, g.L
    GROUPS = B * L // 512
    GPB = L // 512
    with ExitStack() as ctx:
        def sb(name, shape, dt=F32):
            return ctx.enter_context(nc.sbuf_tensor(name, shape, dt))

        def sem(name):
            return ctx.enter_context(nc.semaphore(name))

        hTs = sb("e_hTs", [P, 2, 512])
        st3 = sb("e_st3", [P, 2, 4, 6])
        mv3 = sb("e_mv3", [P, 2, 4, 2])
        sd3 = sb("e_sd3", [P, 2, 4])
        rs3 = sb("e_rs3", [P, 2, 4])
        nb3 = sb("e_nb3", [P, 2, 4])
        hn = sb("e_hn", [P, 2, 4, 8, P])
        rT = sb("e_rT", [P, 2, 8, 512])
        o = sb("e_o", [P, 2, 4, P])
        st4 = sb("e_st4", [P, 4, 6])
        mv4 = sb("e_mv4", [P, 4, 2])
        sd4 = sb("e_sd4", [P, 4])
        rs4 = sb("e_rs4", [P, 4])
        c4 = sb("e_c4", [P, 4, P])
        n4 = sb("e_n4", [P, 4, P])
        t4 = sb("e_t4", [P, 4, P])
        t5 = sb("e_t5", [P, 4, P])
        res = sb("e_res", [P, 4, P])
        zero = sb("e_zero", [1, 1])
        spot = sb("e_spot", [1, 4, 4 * GROUPS])

        ps_h = ctx.enter_context(nc.psum_tensor("ps_h", [P, 2, 4, 256], F32))
        ps_t = ctx.enter_context(nc.psum_tensor("ps_t", [P, 2, 512], F32))
        ps_e = ctx.enter_context(nc.psum_tensor("ps_e", [P, 2, 4, P], F32))

        h_in = [sem("e_h_in0"), sem("e_h_in1")]
        hid, stat, aggr, root, inv, shift, normed = (sem("e_hid"), sem("e_stat"), sem("e_aggr"), sem("e_root"), sem("e_inv"),
                                                     sem("e_shift"), sem("e_normed"))
        turned, relu, outs, gated = sem("e_turned"), sem("e_relu"), sem("e_outs"), sem("e_gated")
        stat4, aggr4, root4, inv4, c4_done, n4_done, t4_done, t5_done, res_done = (
            sem("e_stat4"), sem("e_aggr4"), sem("e_root4"), sem("e_inv4"), sem("e_c4_done"), sem("e_n4_done"), sem("e_t4_done"),
            sem("e_t5_done"), sem("e_res_done"))
        stored, ready = sem("e_stored"), sem("e_ready")

        ov = g.out.rearrange("b l e -> (b l) e").rearrange("(t p) e -> p t e", p=P)

        def has(n):
            return not isinstance(n, int) or 0 <= n < GROUPS

        def run(eng, body):
            body(0, 0)
            body(1, 1)
            body(2, 0)
            body(3, 1)
            with eng.Fori(2, GROUPS // 2) as j:
                body(2 * j, 0)
                body(2 * j + 1, 1)
            body(GROUPS, 0)
            body(GROUPS + 1, 1)

        block = ctx.enter_context(nc.Block())

        @block.sync
        def _(sp):
            def load(n):
                if n >= 4:
                    sp.wait_ge(hid, 4 * n - 4)
                sp.dma_start(hTs[:, n % 2, :], f.hT2[:, 512 * n:512 * n + 512]).then_inc(h_in[n % 2], 16)

            def store(m):
                sp.wait_ge(res_done, m + 1)
                sp.dma_start(ov[:, 4 * m:4 * m + 4, :], res[:, :, :]).then_inc(stored, 16)

            for n in range(2, 6):
                load(n)
            for m in range(GROUPS):
                if m + 5 in (6, 7):
                    load(m + 5)
                store(m)
            sp.wait_ge(stored, 16 * GROUPS)

        @block.gpsimd
        def _(pool):
            G = nc.gpsimd

            def body(n, u):
                if has(n - 3):
                    finish(n - 3, 1 - u)

            def per_tile(ap):
                return ap.unsqueeze(2).to_broadcast([P, 4, P])

            def finish(m, u):
                b = m // GPB
                pool.wait_ge(inv4, m + 1)
                G.tensor_tensor(c4[:, :, :], o[:, u, :, :], per_tile(mv4[:, :, 0]), ALU.subtract).then_inc(c4_done, 1)
                pool.wait_ge(c4_done, m + 1)
                G.tensor_tensor(n4[:, :, :], c4[:, :, :], per_tile(rs4[:, :]), ALU.mult).then_inc(n4_done, 1)
                pool.wait_ge(n4_done, m + 1)
                G.tensor_tensor(t4[:, :, :], n4[:, :, :], g.mod_rep[:, 2, at(b, 1), :].to_broadcast([P, 4, P]), ALU.mult).then_inc(t4_done, 1)
                pool.wait_ge(t4_done, m + 1)
                G.tensor_tensor(t5[:, :, :], t4[:, :, :], g.mod_rep[:, 3, at(b, 1), :].to_broadcast([P, 4, P]), ALU.add).then_inc(t5_done, 1)
                pool.wait_ge(t5_done, m + 1)
                wait(pool, stored, 16 * m)
                G.tensor_tensor(res[:, :, :], t5[:, :, :], f.x2[:, at(4 * m, 4), :], ALU.add).then_inc(res_done, 1)

            run(pool, body)
            finish(GROUPS - 1, 1)

        @block.scalar
        def _(act):
            A = nc.scalar

            def relu_of(m, u, chunks):
                for c in chunks:
                    act.wait_ge(turned, 8 * m + c + 1)
                    wait(act, outs, 4 * m - 4)
                    A.activation(rT[:, u, c, :], ps_t[:, c % 2, :], ACT.Relu, bias=g.vecT[:, C_LNB + c:C_LNB + c + 1],
                                 scale=g.vecT[:, C_LNG + c:C_LNG + c + 1]).then_inc(relu, 1)

            def body(n, u):
                for i in range(4):
                    if i == 0 and has(n - 2):
                        relu_of(n - 2, u, (6, 7))
                    if i > 0 and has(n - 1):
                        relu_of(n - 1, 1 - u, (2 * i - 2, 2 * i - 1))
                    if i == 1 and has(n - 3):
                        root_of_output(n - 3)
                    if has(n):
                        k = 4 * n + i
                        act.wait_ge(aggr, k + 1)
                        wait(act, inv, k - 1)
                        A.activation(sd3[:, i % 2, :], mv3[:, i % 2, :, 1], ACT.Sqrt, bias=g.eps[:, 0:1]).then_inc(root, 1)
                        act.wait_ge(shift, k + 1)
                        wait(act, turned, 8 * n - 8)
                        for e in range(4):
                            last = A.activation(flat(hn[:, u, i, 2 * e:2 * e + 2, :]), ps_h[:, i % 2, e, :], ACT.Identity,
                                                scale=rs3[:, i % 2, e:e + 1], bias=nb3[:, i % 2, e:e + 1])
                        last.then_inc(normed, 1)

            def root_of_output(m):
                act.wait_ge(aggr4, m + 1)
                wait(act, inv4, m)
                A.activation(sd4[:, :], mv4[:, :, 1], ACT.Sqrt, bias=g.eps[:, 0:1]).then_inc(root4, 1)

            run(act, body)
            root_of_output(GROUPS - 1)

        @block.vector
        def _(dve):
            D = nc.vector

            def gated_sum(m, u, i, experts):
                for e in experts:
                    gate = f.gate[:, at(4 * m + i, 1), e]
                    if e == 0:
                        dve.wait_ge(outs, 4 * m + i + 1)
                        if i == 0:
                            wait(dve, c4_done, m - 1)
                        D.tensor_scalar(o[:, u, i, :], ps_e[:, i % 2, e, :], gate, None, ALU.mult).then_inc(gated, 1)
                    else:
                        dve.wait_ge(gated, 16 * m + 4 * i + e)
                        D.scalar_tensor_tensor(o[:, u, i, :], ps_e[:, i % 2, e, :], gate, o[:, u, i, :],
                                               op0=ALU.mult, op1=ALU.add).then_inc(gated, 1)

            def output_stats(m, u):
                dve.wait_ge(gated, 16 * (m + 1))
                carry(D, spot, zero, 2, m)
                for t in range(4):
                    last = D.bn_stats(st4[:, t, :], o[:, u, t, :])
                last.then_inc(stat4, 1)
                wait(dve, n4_done, m)
                dve.wait_ge(stat4, m + 1)
                carry(D, spot, zero, 3, m)
                for t in range(4):
                    last = D.bn_aggr(mv4[:, t, :], st4[:, t, :])
                last.then_inc(aggr4, 1)

            def output_rs(m):
                dve.wait_ge(root4, m + 1)
                D.reciprocal(rs4[:, :], sd4[:, :]).then_inc(inv4, 1)

            def body(n, u):
                for i in range(4):
                    k = 4 * n + i
                    if has(n):
                        dve.wait_ge(hid, k + 1)
                        carry(D, spot, zero, 0, k)
                        for e in range(4):
                            last = D.bn_stats(st3[:, i % 2, e, :], ps_h[:, i % 2, e, :])
                        last.then_inc(stat, 1)
                        dve.wait_ge(stat, k + 1)
                        carry(D, spot, zero, 1, k)
                        for e in range(4):
                            last = D.bn_aggr(mv3[:, i % 2, e, :], st3[:, i % 2, e, :])
                        last.then_inc(aggr, 1)
                    tile = (n - 3, 1 - u, 3) if i == 0 else (n - 2, u, i - 1)
                    if has(tile[0]):
                        gated_sum(*tile, (0, 1))
                    if has(n):
                        dve.wait_ge(root, k + 1)
                        wait(dve, normed, k - 1)
                        D.reciprocal(rs3[:, i % 2, :], sd3[:, i % 2, :]).then_inc(inv, 1)
                        dve.wait_ge(inv, k + 1)
                        D.scalar_tensor_tensor(nb3[:, i % 2, :], mv3[:, i % 2, :, 0], -1.0, rs3[:, i % 2, :],
                                               op0=ALU.mult, op1=ALU.mult).then_inc(shift, 1)
                    if has(tile[0]):
                        gated_sum(*tile, (2, 3))
                    if i == 0 and has(n - 3):
                        output_stats(n - 3, 1 - u)
                    if i == 2 and has(n - 3):
                        output_rs(n - 3)

            D.memset(zero[:, :], 0.0).then_inc(ready, 1)
            dve.wait_ge(ready, 1)
            run(dve, body)
            gated_sum(GROUPS - 1, 1, 3, range(4))
            output_stats(GROUPS - 1, 1)
            output_rs(GROUPS - 1)

        @block.tensor
        def _(pe):
            T = nc.tensor
            pe.wait_ge(f.s_w, 32)

            def body(n, u):
                for i in range(4):
                    if has(n):
                        if isinstance(n, int) and n < 2:
                            h = f.hT2[:, 512 * n + i * P:512 * n + (i + 1) * P]
                        else:
                            h = hTs[:, u, i * P:(i + 1) * P]
                            if i == 0:
                                pe.wait_ge(h_in[u], 16 * (n // 2))
                        wait(pe, normed, 4 * n + i - 1)
                        for a in range(2):
                            last = T.matmul(flat(ps_h[:, i % 2, 2 * a:2 * a + 2, :]), h,
                                            flat(f.w1[:, 2 * a:2 * a + 2, :]), start=True, stop=True)
                        last.then_inc(hid, 1)
                    if has(n - 2):
                        m = n - 2
                        if i == 0:
                            pe.wait_ge(relu, 8 * m + 8)
                        wait(pe, gated, 16 * m + 4 * i - 4)
                        for e in range(4):
                            for a in range(2):
                                last = T.matmul(ps_e[:, i % 2, e, :], rT[:, u, 2 * e + a, i * P:(i + 1) * P], f.w2[:, 2 * e + a, :],
                                                start=(a == 0), stop=(a == 1))
                        last.then_inc(outs, 1)
                    if has(n - 1):
                        m = n - 1
                        if i == 0:
                            pe.wait_ge(normed, 4 * m + 4)
                        for c in (2 * i, 2 * i + 1):
                            wait(pe, relu, 8 * m + c - 1)
                            for t in range(4):
                                last = T.transpose(ps_t[:, c % 2, t * P:(t + 1) * P], hn[:, 1 - u, t, c, :], g.ident[:, :])
                            last.then_inc(turned, 1)

            run(pe, body)


def ffn_stage(nc, g):
    B, L = g.B, g.L
    TILES = B * L // P
    with ExitStack() as ctx:
        f = Shared()

        def sb(name, shape):
            return ctx.enter_context(nc.sbuf_tensor(name, shape, F32))

        f.w1 = sb("w1s", [P, 4, 256])
        f.w2 = sb("w2s", [P, 8, P])
        f.x2 = sb("x2", [P, TILES, P])
        f.hT2 = sb("hT2", [P, B * L])
        f.gate = sb("gate", [P, TILES, 4])
        f.s_w = ctx.enter_context(nc.semaphore("w_in"))
        router_stage(nc, g, f)
        experts_stage(nc, g, f)


_INS = ['L0_attn_X', 'L0_attn_W_qkv', 'L0_attn_b_qkv', 'L0_attn_W_fc', 'L0_attn_b_fc', 'L0_ffn_router_w', 'L0_ffn_rn_g',
        'L0_ffn_rn_b', 'L0_ffn_w1', 'L0_ffn_ln_g', 'L0_ffn_ln_b', 'L0_ffn_w2', 'L0_ffn_on_g', 'L0_ffn_on_b', 'L0_c', 'L0_wmod']


def kernel(**inputs):
    import numpy as np
    import concourse.bacc as bacc
    from concourse.bass_utils import run_bass_kernel_spmd

    nc = bacc.Bacc("TRN2", target_bir_lowering=False, num_devices=1)
    arrays, args = {}, []
    for name in _INS:
        a = np.ascontiguousarray(inputs[name])
        arrays[f"in_{name}"] = a
        args.append(nc.dram_tensor(f"in_{name}", a.shape, mybir.dt.from_np(a.dtype), kind="ExternalInput").ap())
    args.append(nc.dram_tensor("out_0", inputs['L0_attn_X'].shape, F32, kind="ExternalOutput").ap())
    build(nc, *args)
    r = run_bass_kernel_spmd(nc, [arrays], core_ids=[0])
    return r.results[0]["out_0"]
```

```python
from contextlib import ExitStack

import concourse.bass as bass
from concourse import mybir

F32 = mybir.dt.float32
F32R = mybir.dt.float32r
ACT = mybir.ActivationFunctionType
ALU = mybir.AluOpType
AX = mybir.AxisListType.X

P = 128
EPS = 1e-5
EPS_GATE = 1e-8
GUARD = 0.25
ds = bass.ds


def flat(ap):
    return ap.rearrange("p a b -> p (a b)")


def wait(eng, sem, value):
    if not isinstance(value, int) or value > 0:
        eng.wait_ge(sem, value)


def run_pairs(eng, count, body, first=None, last=None):
    if first:
        first()
    body(0, 0)
    body(1, 1)
    with eng.Fori(1, count // 2 - 1) as j:
        body(2 * j, 0)
        body(2 * j + 1, 1)
    body(count - 2, 0)
    body(count - 1, 1)
    if last:
        last()


def at(index, size):
    return slice(index, index + size) if isinstance(index, int) else ds(index, size)


def carry(eng, spot, zero, kind, index):
    eng.tensor_tensor(spot[0:1, kind, at(index, 1)], zero[0:1, 0:1], zero[0:1, 0:1], ALU.mult)


class Shared:
    pass


def build(nc, X, W_qkv, b_qkv, W_fc, b_fc, router_w, rn_g, rn_b, w1, ln_g, ln_b, w2, on_g, on_b, c, wmod, out):
    B, L, E = X.shape
    HD = W_fc.shape[0]
    DK = 64
    H = HD // DK
    assert E == P and L == 1024 and H == 16 and B == 4
    with ExitStack() as ctx:
        g = Shared()
        g.X, g.W_qkv, g.W_fc, g.out = X, W_qkv, W_fc, out
        g.small = (b_qkv, b_fc, router_w, rn_g, rn_b, ln_g, ln_b, on_g, on_b, c, wmod)
        g.w1, g.w2 = w1, w2
        g.B, g.L, g.E, g.H = B, L, E, H

        def sb(name, shape, dt=F32):
            return ctx.enter_context(nc.sbuf_tensor(name, shape, dt))

        g.ident = sb("ident", [P, P])
        g.ones = sb("ones", [P, P])
        g.eps = sb("eps", [P, 1])
        g.attnT = sb("attnT", [P, B * L])
        g.vecT = sb("vecT", [P, 64])
        g.modT = sb("modT", [P, 6, B])
        g.gaT = sb("gaT", [P, B])
        g.gacT = sb("gacT", [P, B])
        g.mod_rep = sb("mod_rep", [P, 4, B, P])
        g.on_rep = sb("on_rep", [P, 2, P])
        g.rw = sb("rw", [P, 8])
        g.rw_sum = sb("rw_sum", [P, 4])
        g.hT = sb("hT", [P, B * L])
        g.x_in = ctx.enter_context(nc.semaphore("x_in"))
        with ExitStack() as two:
            g.hT_hi = two.enter_context(nc.sbuf_tensor("hT_hi", [P, B * L], F32R))
            g.hT_lo = two.enter_context(nc.sbuf_tensor("hT_lo", [P, B * L], F32R))
            setup_stage(nc, g)
            attention_stage(nc, g)
        ffn_stage(nc, g)


C_LNG, C_LNB, C_RNG, C_RNB, C_BFC, C_RW, C_C, C_BQ, C_BK, C_BV = 0, 8, 16, 17, 18, 19, 23, 27, 35, 43
N_VEC = 51


def setup_stage(nc, g):
    b_qkv, b_fc, router_w, rn_g, rn_b, ln_g, ln_b, on_g, on_b, c, wmod = g.small
    B, L = g.B, g.L
    GROUPS = B * L // 512
    with ExitStack() as ctx:
        def sb(name, shape, dt=F32):
            return ctx.enter_context(nc.sbuf_tensor(name, shape, dt))

        def sem(name):
            return ctx.enter_context(nc.semaphore(name))

        rows = sb("rows", [64, P])
        on_row = sb("on_row", [1, 2 * P])
        wm = sb("wm", [P, 6 * P])
        wfc = sb("wfc_all", [P, 8, P])
        silu = sb("silu", [P, 4, B])
        silu_rep = sb("silu_rep", [P, B, P])
        tmpT = sb("tmpT", [P, 4, B])
        TILES = 4 * GROUPS
        x = sb("x", [P, TILES, P])
        xn = sb("xn", [P, 2, 4, P])
        st = sb("st", [P, TILES, 6])
        mv = sb("mv", [P, TILES, 2])
        sd = sb("sd", [P, TILES])
        rs = sb("rs", [P, TILES])
        ps_a = ctx.enter_context(nc.psum_tensor("ps_a", [P, 512], F32))
        ps_m = ctx.enter_context(nc.psum_tensor("ps_m", [P, B, 512], F32))
        ps_x = ctx.enter_context(nc.psum_tensor("ps_x", [P, 2, 512], F32))
        ps_b = ctx.enter_context(nc.psum_tensor("ps_b", [P, 512], F32))

        s_rows, s_wm, s_wfc = sem("s_rows"), sem("s_wm"), sem("s_wfc")
        s_x = [sem(f"s_x{b}") for b in range(B)]
        s_id, s_const = sem("s_id"), sem("s_const")
        s_vec, s_vecT, s_exp = sem("s_vec"), sem("s_vecT"), sem("s_exp")
        s_v = sem("s_v")
        s_mod, s_modrep, s_onrep, s_bv, s_silu, s_modT = (sem("s_mod"), sem("s_modrep"), sem("s_onrep"), sem("s_bv"),
                                                          sem("s_silu"), sem("s_modT"))
        s_st, s_mv, s_sd, s_rs, s_xn, s_xt = sem("s_st"), sem("s_mv"), sem("s_sd"), sem("s_rs"), sem("s_xn"), sem("s_xt")
        s_h, s_hi, s_lo = sem("s_h"), sem("s_hi"), sem("s_lo")

        xv = g.X.rearrange("b l e -> (b l) e").rearrange("(t p) e -> p t e", p=P)
        N_ROW_DMAS = 15

        block = ctx.enter_context(nc.Block())

        @block.sync
        def _(sp):
            for b in range(B):
                sp.dma_start(x[:, 8 * b:8 * b + 8, :], xv[:, 8 * b:8 * b + 8, :]).then_inc(s_x[b], 16)
            sp.dma_start(wm[:, :], wmod).then_inc(s_wm, 16)
            sp.dma_start(wfc[:, :, :], g.W_fc.rearrange("(k p) e -> p k e", p=P)).then_inc(s_wfc, 16)

        @block.gpsimd
        def _(pool):
            nc.gpsimd.memset(g.ident[:, :], 0.0).then_inc(s_id, 1)
            nc.gpsimd.memset(g.ones[:, :], 1.0).then_inc(s_const, 1)
            nc.gpsimd.memset(g.eps[:, :], EPS).then_inc(s_const, 1)
            pool.wait_ge(s_id, 1)
            nc.gpsimd.affine_select(out=g.ident[:, :], in_=g.ident[:, :], compare_op=ALU.not_equal, fill=1.0,
                                    base=0, pattern=[[-1, P]], channel_multiplier=1).then_inc(s_id, 1)
            nc.gpsimd.memset(g.attnT[:, :], 0.0)

            def body(n, u):
                cols = at(n * 512, 512)
                pool.wait_ge(s_hi, n + 1)
                nc.gpsimd.tensor_tensor(g.hT_lo[:, cols], g.hT[:, cols], g.hT_hi[:, cols].bitcast(F32), ALU.subtract)

            run_pairs(pool, GROUPS, body)

        @block.scalar
        def _(act):
            A = nc.scalar
            act.dma_start(rows[C_LNG:C_LNG + 8, :], ln_g.rearrange("e (a h) -> (e a) h", h=P)).then_inc(s_rows, 16)
            act.dma_start(rows[C_LNB:C_LNB + 8, :], ln_b.rearrange("e (a h) -> (e a) h", h=P)).then_inc(s_rows, 16)
            act.dma_start(rows[C_RNG:C_RNG + 1, :], rn_g.rearrange("(a h) -> a h", a=1)).then_inc(s_rows, 16)
            act.dma_start(rows[C_RNB:C_RNB + 1, :], rn_b.rearrange("(a h) -> a h", a=1)).then_inc(s_rows, 16)
            act.dma_start(rows[C_BFC:C_BFC + 1, :], b_fc.rearrange("(a h) -> a h", a=1)).then_inc(s_rows, 16)
            act.dma_start(rows[C_RW:C_RW + 4, :], router_w).then_inc(s_rows, 16)
            act.dma_start(rows[C_C:C_C + 4, :], c).then_inc(s_rows, 16)
            bv = b_qkv.rearrange("(p h t d) -> t p h d", h=2, t=3, d=64)
            for col, t in ((C_BQ, 0), (C_BK, 1), (C_BV, 2)):
                for hh in range(2):
                    act.dma_start(rows[col:col + 8, 64 * hh:64 * hh + 64], bv[t, :, hh, :]).then_inc(s_rows, 16)
            act.dma_start(on_row[0:1, 0:P], on_g.rearrange("(a h) -> a h", a=1)).then_inc(s_rows, 16)
            act.dma_start(on_row[0:1, P:2 * P], on_b.rearrange("(a h) -> a h", a=1)).then_inc(s_rows, 16)

            act.wait_ge(s_vecT, 1)
            A.activation(silu[:, 0, :], g.vecT[:, C_C:C_C + 4], ACT.Exp, scale=-1.0).then_inc(s_exp, 1)
            A.activation(flat(g.on_rep[:, :, :]), ps_a[:, 256:512], ACT.Copy).then_inc(s_onrep, 1)
            act.wait_ge(s_const, 2)
            act.wait_ge(s_mv, 1)
            A.activation(sd[:, :], mv[:, :, 1], ACT.Sqrt, bias=g.eps[:, 0:1]).then_inc(s_sd, 1)
            act.wait_ge(s_modT, 1)
            for n in range(GROUPS):
                cols, b = slice(n * 512, n * 512 + 512), n * 512 // L
                act.wait_ge(s_xt, n + 1)
                A.activation(g.hT[:, cols], ps_x[:, n % 2, :], ACT.Identity, scale=g.modT[:, 1, b:b + 1],
                             bias=g.modT[:, 0, b:b + 1]).then_inc(s_h, 1)
                act.wait_ge(s_h, n + 1)
                A.activation(g.hT_hi[:, cols], g.hT[:, cols], ACT.Copy).then_inc(s_hi, 1)
            act.wait_ge(s_modrep, B)
            A.activation(g.mod_rep[:, 1, :, :], ps_m[:, :, 0:P], ACT.Copy)
            A.activation(g.mod_rep[:, 0, :, :], ps_m[:, :, P:2 * P], ACT.Identity, bias=g.ones[:, 0:1])
            A.activation(g.mod_rep[:, 2, :, :], ps_m[:, :, 2 * P:3 * P], ACT.Copy)

        @block.vector
        def _(dve):
            done = [0]

            def link(ins):
                done[0] += 1
                ins.then_inc(s_v, 1)
                dve.wait_ge(s_v, done[0])

            V = nc.vector

            def token_stats(b):
                dve.wait_ge(s_x[b], 16)
                for t in range(8 * b, 8 * b + 8):
                    last = V.bn_stats(st[:, t, :], x[:, t, :])
                last.then_inc(s_st, 1)

            token_stats(0)
            token_stats(1)
            dve.wait_ge(s_vec, 1)
            V.tensor_copy(g.vecT[:, 0:N_VEC], ps_a[:, 0:N_VEC]).then_inc(s_vecT, 1)
            token_stats(2)
            dve.wait_ge(s_vecT, 1)
            dve.wait_ge(s_exp, 1)
            link(V.tensor_scalar_add(silu[:, 1, :], silu[:, 0, :], 1.0))
            link(V.reciprocal(silu[:, 2, :], silu[:, 1, :]))
            link(V.tensor_tensor(silu[:, 3, :], silu[:, 2, :], g.vecT[:, C_C:C_C + 4], ALU.mult))
            V.tensor_copy(silu_rep[:, :, :], silu[:, 3, :].unsqueeze(2).to_broadcast([P, B, P])).then_inc(s_silu, 1)
            token_stats(3)
            dve.wait_ge(s_st, B)
            for t in range(TILES):
                last = V.bn_aggr(mv[:, t, :], st[:, t, :])
            last.then_inc(s_mv, 1)
            dve.wait_ge(s_mod, 1)
            link(V.tensor_copy(g.modT[:, :, :], ps_b[:, 0:24].rearrange("p (a b) -> p a b", a=6)))
            V.tensor_scalar_add(g.modT[:, 1, :], g.modT[:, 1, :], 1.0).then_inc(s_modT, 1)

            dve.wait_ge(s_sd, 1)
            V.reciprocal(rs[:, :], sd[:, :]).then_inc(s_rs, 1)
            dve.wait_ge(s_rs, 1)
            dve.wait_ge(s_mv, 1)

            def body(n, u):
                wait(dve, s_xt, n - 1)
                for i in range(4):
                    last = V.tensor_scalar(xn[:, u, i:i + 1, :], x[:, at(4 * n + i, 1), :], mv[:, at(4 * n + i, 1), 0],
                                           rs[:, at(4 * n + i, 1)], ALU.subtract, ALU.mult)
                last.then_inc(s_xn, 1)

            run_pairs(dve, GROUPS, body)

            link(V.tensor_scalar_add(g.modT[:, 4, :], g.modT[:, 4, :], 1.0))
            ga = g.modT[:, 2, :]
            link(V.scalar_tensor_tensor(tmpT[:, 0, :], ga, -1.0, ga, op0=ALU.mult, op1=ALU.max))
            link(V.tensor_scalar_max(tmpT[:, 1, :], tmpT[:, 0, :], GUARD))
            link(V.tensor_scalar(tmpT[:, 2, :], ga, 0.0, 2.0, ALU.is_ge, ALU.mult))
            link(V.scalar_tensor_tensor(g.gaT[:, :], tmpT[:, 2, :], 1.0, tmpT[:, 1, :], op0=ALU.subtract, op1=ALU.mult))
            dve.wait_ge(s_bv, 1)
            link(V.tensor_tensor(tmpT[:, 3, 0:1], ps_b[:, 64:65], g.vecT[:, C_BFC:C_BFC + 1], ALU.add))
            V.tensor_scalar(g.gacT[:, :], g.gaT[:, :], tmpT[:, 3, 0:1], None, ALU.mult)

        @block.tensor
        def _(pe):
            T = nc.tensor
            pe.wait_ge(s_id, 2)
            pe.wait_ge(s_const, 2)
            pe.wait_ge(s_rows, 16 * N_ROW_DMAS)
            T.matmul(ps_a[:, 256:512], g.ones[0:1, :], on_row[0:1, :], start=True, stop=True)
            T.transpose(ps_a[:, 0:N_VEC], rows[0:N_VEC, :], g.ident[0:N_VEC, 0:N_VEC]).then_inc(s_vec, 1)
            pe.wait_ge(s_wm, 16)
            pe.wait_ge(s_silu, 1)
            for k in range(6):
                last = T.matmul(ps_b[:, 4 * k:4 * k + 4], wm[:, k * P:(k + 1) * P], silu[:, 3, :], start=True, stop=True)
            last.then_inc(s_mod, 1)

            def body(n, u):
                pe.wait_ge(s_xn, n + 1)
                wait(pe, s_h, n - 1)
                for i in range(4):
                    last = T.transpose(ps_x[:, u, i * P:(i + 1) * P], xn[:, u, i, :], g.ident[:, :])
                last.then_inc(s_xt, 1)
                if isinstance(n, int):
                    b = n if n < 2 else n - GROUPS + B
                    T.matmul(ps_m[:, b, 0:3 * P], silu_rep[:, b, :], wm[:, 3 * P:6 * P], start=True, stop=True).then_inc(s_modrep, 1)

            run_pairs(pe, GROUPS, body)
            pe.wait_ge(s_wfc, 16)
            pe.wait_ge(s_modT, 1)
            for k in range(8):
                last = T.matmul(ps_b[:, 64:65], wfc[:, k, :], g.vecT[:, C_BV + k:C_BV + k + 1],
                                start=(k == 0), stop=(k == 7))
            last.then_inc(s_bv, 1)


def attention_stage(nc, g):
    B, L, H = g.B, g.L, g.H
    NP = B * H // 2
    PAIRS = H // 2
    SCALE = 0.125
    with ExitStack() as ctx:
        def sb(name, shape, dt=F32):
            return ctx.enter_context(nc.sbuf_tensor(name, shape, dt))

        def psum(name, shape):
            return ctx.enter_context(nc.psum_tensor(name, shape, F32))

        def sem(name):
            return ctx.enter_context(nc.semaphore(name))

        QA = sb("QA", [P, 2, 2, L], F32R)
        QB = sb("QB", [P, 2, 2, L], F32R)
        KA = sb("KA", [P, 2, 2, L], F32R)
        KB = sb("KB", [P, 2, 2, L], F32R)
        V = sb("V", [P, 2, 8, P])
        PR = sb("PR", [P, 8, 2, 512])
        ACC = sb("ACC", [P, 2, 2, 512])
        Wraw = sb("Wraw", [P, 2, 2, 3, 64])
        Whi = sb("Whi", [P, 2, 2, 64], F32R)
        Wlo = sb("Wlo", [P, 2, 2, 64], F32R)
        bias = sb("bias", [P, 2, 2])
        Wfc = sb("Wfc", [P, 2, P])
        hcur = sb("hcur", [P, L])
        raw = sb("raw", [P, 2, 512])
        SUM = sb("SUM", [P, 512])
        O = sb("O", [P, 512])
        NMH = sb("NMH", [P, 2, 2, 4, 2])
        NM = sb("NM", [P, 2, 2, 4])
        mask = sb("mask", [P, 4, P])

        ps_s = psum("ps_s", [P, 2, 512])
        ps_mx = psum("ps_mx", [P, 2, 512])
        ps_o = psum("ps_o", [P, 2, 512])
        ps_w2 = psum("ps_w2", [P, 2, 512])

        s_init = sem("a_init")
        s_gb = sem("a_gate_rows")
        s_mask = sem("a_mask")
        wraw_in, hcur_in, wfc_in = [sem("wraw_in0"), sem("wraw_in1")], sem("hcur_in"), [sem("wfc_in0"), sem("wfc_in1")]
        kdup, qdup = [sem("kdup0"), sem("kdup1")], [[sem(f"qdup{u}{ch}") for ch in range(2)] for u in range(2)]
        scored, pv_done, mx_done = sem("scored"), sem("pv_done"), sem("mx_done")
        k_proj, q_proj, v_proj = sem("k_proj"), sem("q_proj"), sem("v_proj")
        rows_t, sums_mm, fc_mm = sem("rows_t"), sem("sums_mm"), sem("fc_mm")
        exp_done, k_hi, q_hi, v_copied, o_copied, w_hi = (sem("exp_done"), sem("k_hi"), sem("q_hi"),
                                                          sem("v_copied"), sem("o_copied"), sem("w_hi"))
        mx_red, k_lo, q_lo, neg_rows, recip, o_norm, fc_added, w_lo = (
            sem("mx_red"), sem("k_lo"), sem("q_lo"), sem("neg_rows"), sem("recip"), sem("o_norm"),
            sem("fc_added"), sem("w_lo"))
        added, raw_in, sums_in, mx_both = sem("added"), sem("raw_in"), sem("sums_in"), sem("mx_both")

        wqkv = g.W_qkv.rearrange("e (p h t d) -> e p h t d", h=2, t=3, d=64)
        wfc_v = g.W_fc.rearrange("(k p) e -> p k e", p=P)

        def place(s):
            if s < 6:
                i = s + 2
                return 0, 1, i // 4, i % 4
            if s < 14:
                i = s - 6
                return 1, 0, i // 4, i % 4
            i = s - 14
            return 1, 1, i // 4, i % 4

        UNITS = {0: ("k", 1, 0), 1: ("k", 1, 1), 2: ("sums", -1, 1), 3: ("q", 1, 0),
                 6: ("rows", 0, 1), 7: ("v", 1, 0), 8: ("q", 1, 1), 9: ("fc", -1, 1),
                 10: ("sums", 0, 0), 11: ("v", 1, 1), 14: ("rows", 1, 0), 15: ("fc", 0, 0)}
        INVERT = {2: (-1, 1, (0,)), 4: (-1, 1, (1,)), 5: (-1, 1, (2,)), 7: (-1, 1, (3,)),
                  10: (0, 0, (0,)), 11: (0, 0, (1,)), 12: (0, 0, (2,)), 13: (0, 0, (3,))}
        LAST_ON_POOL = 6
        ORDER = sorted(UNITS)

        def unit_at(n, s):
            if s not in UNITS:
                return None
            kind, d, ch = UNITS[s]
            if isinstance(n, int) and not 0 <= n + d < NP:
                return None
            return kind, n + d, ch

        FIRST_UNITS = [("k", 0), ("k", 1), ("q", 0), ("v", 0), ("v", 1), ("q", 1), ("rows", 0)]

        def unit_u(s, u):
            return u if UNITS[s][1] == 0 else 1 - u

        def raw_count(kind, m, ch):
            return 4 * m + (2 if kind == "q" else 0) + ch + 1

        def has(n):
            return not isinstance(n, int) or 0 <= n < NP

        def batch_cols(m, ch):
            b = m // PAIRS
            return ds(b * L + ch * 512, 512) if not isinstance(b, int) else slice(b * L + ch * 512, b * L + ch * 512 + 512)

        def col(base, m):
            p = m % PAIRS
            return ds(p + base, 1) if not isinstance(p, int) else slice(base + p, base + p + 1)

        def half(h):
            return slice(64 * h, 64 * h + 64)

        def other(h):
            return slice(64 - 64 * h, 128 - 64 * h)

        def run(eng, pair, first, last=None):
            run_pairs(eng, NP, pair, first, last)

        block = ctx.enter_context(nc.Block())

        @block.sync
        def _(sp):
            def load_w(m, u):
                wait(sp, v_proj, 2 * m - 2)
                p = m % PAIRS
                src = wqkv[:, p:p + 1, :, :, :] if isinstance(p, int) else wqkv[:, ds(p, 1), :, :, :]
                sp.dma_start(Wraw[:, u, :, :, :], src).then_inc(wraw_in[u], 16)

            def load_h(m):
                wait(sp, v_proj, 2 * m)
                b = m // PAIRS
                src = g.hT[:, b * L:(b + 1) * L] if isinstance(b, int) else g.hT[:, ds(b * L, L)]
                sp.dma_start(hcur[:, :], src).then_inc(hcur_in, 16)

            def load_fc(m, u):
                wait(sp, fc_mm, 2 * m - 2)
                p = m % PAIRS
                src = wfc_v[:, p:p + 1, :] if isinstance(p, int) else wfc_v[:, ds(p, 1), :]
                sp.dma_start(Wfc[:, u:u + 1, :], src).then_inc(wfc_in[u], 16)

            def dup_k(m, u, ch):
                q = slice(ch * 512, ch * 512 + 512)
                sp.wait_ge(k_hi, 2 * m + ch + 1)
                for h in range(2):
                    sp.dma_start(KA[other(h), u, h, q].bitcast(F32), KA[half(h), u, h, q].bitcast(F32)).then_inc(kdup[u], 16)

            def dup_q(m, u, ch):
                q = slice(ch * 512, ch * 512 + 512)
                sp.wait_ge(q_hi, 2 * m + ch + 1)
                for h in range(2):
                    sp.dma_start(QB[half(h), u, h, q].bitcast(F32), QA[half(h), u, h, q].bitcast(F32)).then_inc(qdup[u][ch], 16)

            def first():
                load_w(0, 0)
                load_h(0)
                load_w(1, 1)
                load_fc(0, 0)
                dup_k(0, 0, 0)
                dup_k(0, 0, 1)
                dup_q(0, 0, 0)
                dup_q(0, 0, 1)
                load_h(1)

            def pair(n, u):
                if has(n + 1):
                    dup_k(n + 1, 1 - u, 0)
                    dup_k(n + 1, 1 - u, 1)
                    dup_q(n + 1, 1 - u, 0)
                    load_fc(n + 1, 1 - u)
                    dup_q(n + 1, 1 - u, 1)
                if has(n + 2):
                    load_w(n + 2, u)
                    load_h(n + 2)

            def last():
                sp.wait_ge(hcur_in, 16 * NP)
                xv = g.X.rearrange("b l e -> (b l) e").rearrange("(t p) e -> p t e", p=P)
                for b in range(B):
                    sp.dma_start(g.hT[:, b * L:(b + 1) * L].rearrange("p (t e) -> p t e", e=P), xv[:, 8 * b:8 * b + 8, :]).then_inc(g.x_in, 16)

            run(sp, pair, first, last)

        @block.gpsimd
        def _(pool):
            G = nc.gpsimd

            def first():
                for h in range(2):
                    rest = other(h)
                    G.memset(QB[rest, :, h, :].bitcast(F32), 0.0)
                    G.memset(KB[rest, :, h, :].bitcast(F32), 0.0).then_inc(s_init, 1)
                pool.wait_ge(s_init, 2)
                for h in range(2):
                    top = slice(64 - 64 * h, 68 - 64 * h)
                    G.memset(KB[top, :, h, :].bitcast(F32), 1.0).then_inc(s_init, 1)
                pool.wait_ge(s_init, 4)
                G.memset(mask[:, :, :], 1.0).then_inc(s_mask, 1)
                pool.wait_ge(s_mask, 1)
                G.affine_select(out=mask[0:64, :, :], in_=mask[0:64, :, :], compare_op=ALU.is_equal, fill=0.0,
                                base=0, pattern=[[-1, 4], [0, P]], channel_multiplier=1).then_inc(s_mask, 1)
                G.affine_select(out=mask[64:128, :, :], in_=mask[64:128, :, :], compare_op=ALU.is_equal, fill=0.0,
                                base=0, pattern=[[-1, 4], [0, P]], channel_multiplier=1).then_inc(s_mask, 1)

            def pair(n, u):
                for ch in range(2):
                    chunk = 2 * n + ch
                    wait(pool, sums_mm, chunk - 1)
                    for t in range(1, LAST_ON_POOL if isinstance(n, int) and chunk == 2 * NP - 1 else 8):
                        pool.wait_ge(exp_done, 2 * (16 * n + 8 * ch + t + 1))
                        a = PR[:, 0, :, :] if t == 1 else ACC[:, ch, :, :]
                        if t > 1:
                            pool.wait_ge(added, 7 * chunk + t - 1)
                        G.tensor_tensor(ACC[:, ch, :, :], a, PR[:, t, :, :], ALU.add).then_inc(added, 1)

            run(pool, pair, first)

        @block.scalar
        def _(act):
            A = nc.scalar

            def split_w(m, u):
                A.activation(bias[:, u, 0:1], g.vecT[:, col(C_BQ, m)], ACT.Copy)
                A.activation(bias[:, u, 1:2], g.vecT[:, col(C_BK, m)], ACT.Copy)
                wait(act, wraw_in[u], (m // 2 + 1) * 16)
                wait(act, q_proj, 2 * m)
                for h in range(2):
                    last = A.activation(Whi[:, :, h, :], Wraw[:, u, h, 0:2, :], ACT.Copy)
                last.then_inc(w_hi, 1)

            def unit(kind, m, u, ch, ps_w):
                q = slice(ch * 512, ch * 512 + 512)
                if kind in "qk":
                    X, proj, ty, hi, lo = (KA, k_proj, 1, k_hi, k_lo) if kind == "k" else (QA, q_proj, 0, q_hi, q_lo)
                    act.wait_ge(proj, 2 * m + ch + 1)
                    if kind == "k":
                        wait(act, q_lo, 2 * m + ch - 1)
                    else:
                        act.wait_ge(k_lo, 2 * m + ch + 1)
                    A.activation(raw[:, ch, :], ps_w, ACT.Identity, bias=bias[:, u, ty:ty + 1]).then_inc(raw_in, 1)
                    act.wait_ge(raw_in, raw_count(kind, m, ch))
                    for h in range(2):
                        last = A.activation(X[half(h), u, h, q], raw[half(h), ch, :], ACT.Copy)
                    last.then_inc(hi, 1)
                elif kind == "v":
                    act.wait_ge(v_proj, 2 * m + ch + 1)
                    A.activation(flat(V[:, u, 4 * ch:4 * ch + 4, :]), ps_w, ACT.Copy).then_inc(v_copied, 1)
                elif kind == "sums":
                    act.wait_ge(sums_mm, 2 * m + ch + 1)
                    wait(act, o_norm, 2 * m + ch)
                    A.activation(SUM[:, :], ps_w, ACT.Copy).then_inc(sums_in, 1)

            def first():
                split_w(0, 0)
                for k, (kind, ch) in enumerate(FIRST_UNITS):
                    if kind != "rows":
                        unit(kind, 0, 0, ch, ps_w2[:, k % 2, :])
                split_w(1, 1)

            def copy_o(n, ch):
                act.wait_ge(pv_done, 16 * n + 8 * ch + 8)
                wait(act, fc_mm, 2 * n + ch)
                A.activation(O[:, :], ps_o[:, ch, :], ACT.Copy).then_inc(o_copied, 1)

            def pair(n, u):
                for s in range(16):
                    ch, t = divmod(s, 8)
                    chunk = 2 * n + ch
                    wait(act, pv_done, 16 * n + s - 7)
                    wait(act, added, 7 * (chunk - 1) + max(t, 1))
                    for h in range(2):
                        act.wait_ge(scored, 32 * n + 2 * s + h + 1)
                        A.activation(PR[:, t, h, :], ps_s[:, h, :], ACT.Exp, scale=SCALE).then_inc(exp_done, 1)
                    x = unit_at(n, s)
                    if x and x[0] not in ("rows", "fc"):
                        unit(x[0], x[1], unit_u(s, u), x[2], ps_w2[:, ORDER.index(s) % 2, :])
                    if s == 10:
                        copy_o(n, 0)
                    if s == 0 and has(n - 1):
                        copy_o(n - 1, 1)
                    if s == 10 and has(n + 2):
                        split_w(n + 2, u)

            def last():
                copy_o(NP - 1, 1)
                unit("sums", NP - 1, 1, 1, ps_w2[:, 0, :])

            run(act, pair, first, last)

        @block.vector
        def _(dve):
            D = nc.vector

            def split_w(m, u):
                dve.wait_ge(w_hi, m + 1)
                for h in range(2):
                    last = D.tensor_tensor(Wlo[:, :, h, :], Wraw[:, u, h, 0:2, :], Whi[:, :, h, :].bitcast(F32), ALU.subtract)
                last.then_inc(w_lo, 1)

            def reduce_max(m, ch, h, i, count, banks=ps_mx):
                if h == 0 and i == 0:
                    wait(dve, mx_both, 2 * m + ch - 1)
                for kc in range(2):
                    dve.wait_ge(mx_done, 2 * count - 1 + kc)
                    D.tensor_reduce(NMH[:, ch, h, i, kc:kc + 1], banks[:, kc, :], AX, ALU.max, negate=True).then_inc(mx_red, 1)
                if h == 1 and i == 3:
                    dve.wait_ge(mx_red, 2 * count)
                    wait(dve, rows_t, 2 * m + ch - 1)
                    D.tensor_tensor(NM[:, ch, :, :], NMH[:, ch, :, :, 0], NMH[:, ch, :, :, 1], ALU.min).then_inc(mx_both, 1)

            def unit(kind, m, u, ch, ps_w):
                q = slice(ch * 512, ch * 512 + 512)
                if kind == "k":
                    dve.wait_ge(k_hi, 2 * m + ch + 1)
                    for h in range(2):
                        last = D.tensor_tensor(KB[half(h), u, h, q], raw[half(h), ch, :], KA[half(h), u, h, q].bitcast(F32), ALU.subtract)
                    last.then_inc(k_lo, 1)
                elif kind == "q":
                    dve.wait_ge(q_hi, 2 * m + ch + 1)
                    for h in range(2):
                        last = D.tensor_tensor(QA[other(h), u, h, q], raw[half(h), ch, :], QA[half(h), u, h, q].bitcast(F32), ALU.subtract)
                    last.then_inc(q_lo, 1)
                elif kind == "rows":
                    dve.wait_ge(rows_t, 2 * m + ch + 1)
                    for h in range(2):
                        top = slice(64 - 64 * h, 68 - 64 * h)
                        rows = ps_w[top, h * P:(h + 1) * P].unsqueeze(1).to_broadcast([4, 4, P])
                        last = D.tensor_tensor(QB[top, u, h, q].rearrange("p (i q) -> p i q", i=4), rows, mask[top, :, :], ALU.mult)
                    last.then_inc(neg_rows, 1)
                elif kind == "fc":
                    dve.wait_ge(fc_mm, 2 * m + ch + 1)
                    wait(dve, fc_added, 2 * m + ch)
                    cols = batch_cols(m, ch)
                    D.tensor_tensor(g.attnT[:, cols], g.attnT[:, cols], ps_w, ALU.add).then_inc(fc_added, 1)

            def invert(m, ch, part):
                q = slice(part * P, part * P + P)
                dve.wait_ge(sums_in, 2 * m + ch + 1)
                D.reciprocal(SUM[:, q], SUM[:, q]).then_inc(recip, 1)
                if part == 3:
                    dve.wait_ge(recip, 4 * (2 * m + ch + 1))
                    dve.wait_ge(o_copied, 2 * m + ch + 1)
                    D.tensor_tensor(O[:, :], O[:, :], SUM[:, :], ALU.mult).then_inc(o_norm, 1)

            def first():
                split_w(0, 0)
                for kind, ch in FIRST_UNITS:
                    if kind in "kq":
                        unit(kind, 0, 0, ch, None)
                for i in range(8):
                    reduce_max(0, 0, i // 4, i % 4, i + 1, (ps_mx, ps_s)[i % 2])
                dve.wait_ge(s_mask, 3)
                dve.wait_ge(s_init, 4)
                unit("rows", 0, 0, 0, ps_w2[:, 0, :])
                for i in range(2):
                    reduce_max(0, 1, i // 4, i % 4, i + 9)
                split_w(1, 1)

            def pair(n, u):
                for s in range(16):
                    d, ch, h, i = place(s)
                    if has(n + d):
                        reduce_max(n + d, ch, h, i, 16 * n + s + 11)
                    x = unit_at(n, s)
                    if x:
                        unit(x[0], x[1], unit_u(s, u), x[2], ps_w2[:, ORDER.index(s) % 2, :])
                    if s in INVERT and has(n + INVERT[s][0]):
                        for part in INVERT[s][2]:
                            invert(n + INVERT[s][0], INVERT[s][1], part)
                    if s == 10 and has(n + 2):
                        split_w(n + 2, u)
                    if isinstance(n, int) and n == 1 and s in range(3, 9):
                        gate_rows(s - 3)

            def gate_rows(step):
                gb, t = g.mod_rep[:, 2, :, :], g.mod_rep[:, 3, :, :]
                if step:
                    dve.wait_ge(s_gb, step)
                if step == 0:
                    ins = D.scalar_tensor_tensor(t, gb, -1.0, gb, op0=ALU.mult, op1=ALU.max)
                elif step == 1:
                    ins = D.tensor_scalar_max(t, t, GUARD)
                elif step == 2:
                    ins = D.tensor_scalar(gb, gb, 0.0, 2.0, ALU.is_ge, ALU.mult)
                elif step == 3:
                    ins = D.scalar_tensor_tensor(t, gb, 1.0, t, op0=ALU.subtract, op1=ALU.mult)
                elif step == 4:
                    ins = D.tensor_tensor(gb, t, g.on_rep[:, 0:1, :].to_broadcast([P, B, P]), ALU.mult)
                else:
                    ins = D.tensor_tensor(t, t, g.on_rep[:, 1:2, :].to_broadcast([P, B, P]), ALU.mult)
                ins.then_inc(s_gb, 1)

            def last():
                for t in range(LAST_ON_POOL, 8):
                    dve.wait_ge(exp_done, 2 * (16 * (NP - 1) + 8 + t + 1))
                    dve.wait_ge(added, 7 * (2 * NP - 1) + t - 1)
                    D.tensor_tensor(ACC[:, 1, :, :], ACC[:, 1, :, :], PR[:, t, :, :], ALU.add).then_inc(added, 1)
                for part in range(4):
                    invert(NP - 1, 1, part)
                unit("fc", NP - 1, 1, 1, ps_w2[:, 1, :])

            run(dve, pair, first, last)

        @block.tensor
        def _(pe):
            T = nc.tensor

            def unit(kind, m, u, ch, ps_w):
                q = slice(ch * 512, ch * 512 + 512)
                if kind in "qk":
                    ty = 0 if kind == "q" else 1
                    pe.wait_ge(w_lo, m + 1)
                    hi, lo = g.hT_hi[:, batch_cols(m, ch)], g.hT_lo[:, batch_cols(m, ch)]
                    wh, wl = flat(Whi[:, ty, :, :]), flat(Wlo[:, ty, :, :])
                    T.matmul(ps_w[:, :], wh, hi, start=True, stop=False)
                    T.matmul(ps_w[:, :], wl, hi, start=False, stop=False)
                    T.matmul(ps_w[:, :], wh, lo, start=False, stop=True).then_inc(q_proj if kind == "q" else k_proj, 1)
                elif kind == "v":
                    pe.wait_ge(hcur_in, 16 * (m + 1))
                    pe.wait_ge(wraw_in[u], 16 * (m // 2 + 1))
                    for i in range(4):
                        t = 4 * ch + i
                        last = T.matmul(ps_w[:, i * P:(i + 1) * P], hcur[:, t * P:(t + 1) * P], Wraw[:, u, :, 2, :],
                                        start=True, stop=True)
                    last.then_inc(v_proj, 1)
                elif kind == "rows":
                    for h in range(2):
                        last = T.matmul(ps_w[64 - 64 * h:68 - 64 * h, h * P:(h + 1) * P], NM[:, ch, h, :], g.ident[:, :],
                                        start=True, stop=True)
                    last.then_inc(rows_t, 1)
                elif kind == "sums":
                    pe.wait_ge(added, 14 * m + 7 * ch + 7)
                    for h in range(2):
                        last = T.matmul(ps_w[half(h), :], g.ones[:, 0:64], ACC[:, ch, h, :], start=True, stop=True)
                    last.then_inc(sums_mm, 1)
                elif kind == "fc":
                    pe.wait_ge(o_norm, 2 * m + ch + 1)
                    pe.wait_ge(wfc_in[u], 16 * (m // 2 + 1))
                    T.matmul(ps_w[:, :], Wfc[:, u, :], O[:, :], start=True, stop=True).then_inc(fc_mm, 1)

            def freed(kind, m, ch):
                if kind == "k" or kind == "q":
                    pe.wait_ge(raw_in, raw_count(kind, m, ch))
                else:
                    pe.wait_ge({"v": v_copied, "rows": neg_rows, "sums": sums_in, "fc": fc_added}[kind], 2 * m + ch + 1)

            def max_half(m, u, ch, h, i, kc, count, banks=ps_mx, ahead=0):
                if h == 0 and i == 0 and kc == 0:
                    pe.wait_ge(q_lo, 2 * m + ch + 1)
                    if ch == 0:
                        pe.wait_ge(k_hi, 2 * m + 2)
                        pe.wait_ge(kdup[u], 64 * (m // 2 + 1))
                wait(pe, mx_red, 2 * (count - ahead) - 1 + kc)
                q = ch * 512 + i * P
                T.matmul(banks[:, kc, :], QA[:, u, h, q:q + P], KA[:, u, h, kc * 512:(kc + 1) * 512],
                         start=True, stop=True).then_inc(mx_done, 1)

            def scores(n, u, s):
                ch, t = divmod(s, 8)
                q, k = slice(ch * 512, ch * 512 + 512), slice(t * P, (t + 1) * P)
                if t == 0:
                    pe.wait_ge(neg_rows, 2 * n + ch + 1)
                    pe.wait_ge(qdup[u][ch], 32 * (n // 2) + 32)
                    if ch == 0:
                        pe.wait_ge(k_lo, 2 * n + 2)
                for h in range(2):
                    wait(pe, exp_done, 32 * n + 2 * s + h - 1)
                    T.matmul(ps_s[:, h, :], KA[:, u, h, k], QA[:, u, h, q], start=True, stop=False)
                    T.matmul(ps_s[:, h, :], KB[:, u, h, k], QB[:, u, h, q], start=False, stop=True).then_inc(scored, 1)

            def times_v(n, u, s):
                ch, t = divmod(s, 8)
                pe.wait_ge(exp_done, 32 * n + 2 * s + 2)
                if t == 0:
                    wait(pe, o_copied, 2 * n + ch - 1)
                    pe.wait_ge(v_copied, 2 * n + 2)
                for h in range(2):
                    last = T.matmul(ps_o[half(h), ch, :], V[:, u, t, half(h)], PR[:, t, h, :], start=(t == 0), stop=(t == 7))
                last.then_inc(pv_done, 1)

            def first():
                for k, (kind, ch) in enumerate(FIRST_UNITS):
                    if k >= 2:
                        freed(FIRST_UNITS[k - 2][0], 0, FIRST_UNITS[k - 2][1])
                    if kind == "rows":
                        for i in range(8):
                            for kc in range(2):
                                max_half(0, 0, 0, i // 4, i % 4, kc, i, (ps_mx, ps_s)[i % 2], 1)
                        pe.wait_ge(mx_both, 1)
                    unit(kind, 0, 0, ch, ps_w2[:, k % 2, :])
                for i in range(2):
                    for kc in range(2):
                        max_half(0, 0, 1, i // 4, i % 4, kc, i + 8)
                freed("q", 0, 1)
                freed("rows", 0, 0)

            def v_of_last_step(n, u, s):
                if s > 0:
                    times_v(n, u, s - 1)
                elif has(n - 1):
                    times_v(n - 1, 1 - u, 15)

            def pair(n, u):
                for s in range(16):
                    d, ch, h, i = place(s)
                    grp = (n + d, u if d == 0 else 1 - u, ch, h, i)
                    scores(n, u, s)
                    if has(n + d):
                        max_half(*grp, 0, 16 * n + s + 10)
                    x = unit_at(n, s)
                    if not x or x[0] == "rows":
                        v_of_last_step(n, u, s)
                    if x:
                        k = ORDER.index(s) - 2
                        before = unit_at(n, ORDER[k]) if k >= 0 else has(n - 1) and unit_at(n - 1, ORDER[k])
                        if before:
                            freed(*before)
                        if x[0] == "rows":
                            pe.wait_ge(mx_both, 2 * x[1] + x[2] + 1)
                        unit(x[0], x[1], unit_u(s, u), x[2], ps_w2[:, ORDER.index(s) % 2, :])
                    if x and x[0] != "rows":
                        v_of_last_step(n, u, s)
                    if has(n + d):
                        max_half(*grp, 1, 16 * n + s + 10)

            def last():
                times_v(NP - 1, 1, 15)
                freed("sums", NP - 1, 0)
                unit("sums", NP - 1, 1, 1, ps_w2[:, 0, :])
                freed("fc", NP - 1, 0)
                unit("fc", NP - 1, 1, 1, ps_w2[:, 1, :])

            run(pe, pair, first, last)


def router_stage(nc, g, f):
    B, L = g.B, g.L
    GROUPS = B * L // 512
    TILES = 4 * GROUPS
    GPB = L // 512
    with ExitStack() as ctx:
        def sb(name, shape, dt=F32):
            return ctx.enter_context(nc.sbuf_tensor(name, shape, dt))

        def sem(name):
            return ctx.enter_context(nc.semaphore(name))

        yT = sb("r_yT", [P, 2, 512])
        st = sb("r_st", [P, TILES, 6])
        mv = sb("r_mv", [P, TILES, 2])
        sd = sb("r_sd", [P, TILES])
        rs = sb("r_rs", [P, TILES])
        n2 = sb("r_n2", [P, 2, 4, P])
        centre = sb("r_centre", [P, P])
        back = sb("r_back", [P, P + 4])
        st2 = sb("r_st2", [P, TILES, 6])
        mv2 = sb("r_mv2", [P, TILES, 2])
        hT = sb("r_hT", [P, 2, 512])
        sd2 = sb("r_sd2", [P, TILES])
        rs2 = sb("r_rs2", [P, TILES])
        zero = sb("r_zero", [1, 1])
        spot = sb("r_spot", [1, 2, GROUPS])
        ps_y = ctx.enter_context(nc.psum_tensor("ps_y", [P, 2, 512], F32))
        ps_n = ctx.enter_context(nc.psum_tensor("ps_n", [P, 2, 512], F32))
        ps_c = ctx.enter_context(nc.psum_tensor("ps_c", [P, 2, 4, 256], F32))

        s_y, s_yt, s_x2, s_st, s_mv, s_sd, s_rs = (sem("r_y"), sem("r_yt"), sem("r_x2"), sem("r_st_"),
                                                        sem("r_mv_"), sem("r_sd_"), sem("r_rs_"))
        s_n2, s_nt, s_hT, s_back, s_st2, s_mv2, s_sd2 = (sem("r_n2_"), sem("r_nt"), sem("r_hT_"), sem("r_back_mm"),
                                                         sem("r_st2_"), sem("r_mv2_"), sem("r_sd2_"))
        s_tri, s_ex, s_e, s_c, s_cen, s_rw, s_sum = (sem("r_tri_"), sem("r_exp_in"), sem("r_exp"), sem("r_chain"),
                                                     sem("r_cen"), sem("r_rw"), sem("r_sum"))
        s_hi, s_lo, s_w1hi = sem("r_hi"), sem("r_lo"), sem("r_w1_hi")

        block = ctx.enter_context(nc.Block())

        @block.sync
        def _(sp):
            sp.dma_start(f.w1[:, :, :], g.w1.rearrange("e d h -> d e h")).then_inc(f.s_w, 16)
            sp.dma_start(f.w2[:, :, :], g.w2.rearrange("e (a p) d -> p (e a) d", p=P)).then_inc(f.s_w, 16)

        @block.gpsimd
        def _(pool):
            G = nc.gpsimd
            G.memset(centre[:, :], -1.0 / P).then_inc(s_cen, 1)
            pool.wait_ge(s_cen, 1)
            G.affine_select(out=centre[:, :], in_=centre[:, :], compare_op=ALU.not_equal, fill=1.0 - 1.0 / P,
                            base=0, pattern=[[-1, P]], channel_multiplier=1).then_inc(s_cen, 1)
            G.memset(f.tri[:, :, :, :], 1.0).then_inc(s_tri, 1)
            pool.wait_ge(s_tri, 1)
            G.affine_select(out=f.tri[:, 0, :, :], in_=f.tri[:, 0, :, :], compare_op=ALU.is_gt, fill=0.0, base=0,
                            pattern=[[1, 4], [-1, 4]], channel_multiplier=0).then_inc(s_tri, 1)
            G.affine_select(out=f.tri[:, 1, :, :], in_=f.tri[:, 1, :, :], compare_op=ALU.is_gt, fill=0.0, base=0,
                            pattern=[[-1, 4], [1, 4]], channel_multiplier=0).then_inc(s_tri, 1)
            pool.wait_ge(s_w1hi, 1)
            G.tensor_tensor(f.w1_lo[:, :, :], f.w1[:, :, :], f.w1_hi[:, :, :].bitcast(F32), ALU.subtract)

            def body(n, u):
                cols = at(512 * n, 512)
                pool.wait_ge(s_hi, n + 1)
                G.tensor_tensor(f.hT2_lo[:, cols], hT[:, u, :], f.hT2_hi[:, cols].bitcast(F32), ALU.subtract).then_inc(s_lo, 1)

            run_pairs(pool, GROUPS, body)

        @block.scalar
        def _(act):
            A = nc.scalar
            act.wait_ge(f.s_w, 32)
            A.activation(f.w1_hi[:, :, :], f.w1[:, :, :], ACT.Copy).then_inc(s_w1hi, 1)
            act.wait_ge(s_mv, 1)
            A.activation(sd[:, :], mv[:, :, 1], ACT.Sqrt, bias=g.eps[:, 0:1]).then_inc(s_sd, 1)

            for n in range(GROUPS):
                act.wait_ge(s_nt, n + 1)
                if n >= 2:
                    act.wait_ge(s_back, n - 1)
                    act.wait_ge(s_lo, n - 1)
                A.activation(hT[:, n % 2, :], ps_n[:, n % 2, :], ACT.Identity, scale=g.modT[:, 4, n // GPB:n // GPB + 1],
                             bias=g.modT[:, 3, n // GPB:n // GPB + 1]).then_inc(s_hT, 1)
                act.wait_ge(s_hT, n + 1)
                A.activation(f.hT2_hi[:, 512 * n:512 * n + 512], hT[:, n % 2, :], ACT.Copy).then_inc(s_hi, 1)
            act.wait_ge(s_mv2, 1)
            A.activation(sd2[:, :], mv2[:, :, 1], ACT.Sqrt, bias=g.eps[:, 0:1]).then_inc(s_sd2, 1)
            act.wait_ge(s_ex, 1)
            A.activation(f.lg[:, 3, :, :], f.lg[:, 2, :, :], ACT.Exp).then_inc(s_e, 1)

        @block.vector
        def _(dve):
            D = nc.vector
            done = [0]

            def link(ins):
                done[0] += 1
                ins.then_inc(s_c, 1)
                dve.wait_ge(s_c, done[0])

            def one(ap):
                return ap.rearrange("p a b -> p (a b)")

            link(D.memset(zero[:, :], 0.0))
            D.tensor_scalar(g.rw[:, 0:4], g.vecT[:, C_RW:C_RW + 4], g.vecT[:, C_RNG:C_RNG + 1], None, ALU.mult)
            D.tensor_scalar(g.rw[:, 4:8], g.vecT[:, C_RW:C_RW + 4], g.vecT[:, C_RNB:C_RNB + 1], None, ALU.mult).then_inc(s_rw, 1)
            dve.wait_ge(s_sum, 1)
            D.tensor_copy(back[:, 0:P], g.ident[:, :])
            D.tensor_copy(back[:, P:P + 4], ps_n[:, 0, 0:4])
            link(D.tensor_copy(g.rw_sum[:, :], ps_n[:, 0, 8:12]))

            def gated(n, u):
                b = n // GPB
                wait(dve, s_yt, n - 1)
                D.tensor_scalar(yT[:, u, :], g.attnT[:, at(512 * n, 512)], g.gaT[:, at(b, 1)], g.gacT[:, at(b, 1)], ALU.mult, ALU.add).then_inc(s_y, 1)

            def add_x(n, u):
                dve.wait_ge(s_yt, n + 1)
                x2 = f.x2[:, at(4 * n, 4), :]
                D.tensor_tensor(x2, x2, ps_y[:, u, :].rearrange("p (a b) -> p a b", a=4), ALU.add).then_inc(s_x2, 1)

            def stats(n):
                dve.wait_ge(s_x2, n + 1)
                carry(D, spot, zero, 0, n)
                for i in range(4):
                    last = D.bn_stats(one(st[:, at(4 * n + i, 1), :]), one(f.x2[:, at(4 * n + i, 1), :]))
                last.then_inc(s_st, 1)

            def body(n, u):
                if isinstance(n, int) and n == GROUPS - 1:
                    pass
                else:
                    gated(n + 1, 1 - u)
                add_x(n, u)
                if not isinstance(n, int) or n > 0:
                    stats(n - 1)

            def first():
                gated(0, 0)
                dve.wait_ge(g.x_in, 16 * B)

            run_pairs(dve, GROUPS, body, first, lambda: stats(GROUPS - 1))
            dve.wait_ge(s_st, GROUPS)
            for t in range(TILES):
                last = D.bn_aggr(mv[:, t, :], st[:, t, :])
            last.then_inc(s_mv, 1)
            dve.wait_ge(s_sd, 1)
            dve.wait_ge(s_mv, 1)
            D.reciprocal(rs[:, :], sd[:, :]).then_inc(s_rs, 1)
            dve.wait_ge(s_rs, 1)

            def body2(n, u):
                wait(dve, s_nt, n - 1)
                for i in range(4):
                    last = D.tensor_scalar(n2[:, u, i:i + 1, :], f.x2[:, at(4 * n + i, 1), :], mv[:, at(4 * n + i, 1), 0],
                                           rs[:, at(4 * n + i, 1)], ALU.subtract, ALU.mult)
                last.then_inc(s_n2, 1)
                if not isinstance(n, int) or n > 1:
                    stats_of_h(n - 2, u)

            def stats_of_h(n, u):
                dve.wait_ge(s_back, n + 1)
                carry(D, spot, zero, 1, n)
                for i in range(4):
                    D.bn_stats(one(st2[:, at(4 * n + i, 1), :]), ps_c[:, u, i, 0:P])
                D.tensor_scalar(f.lg[:, 1, at(4 * n, 4), :], ps_c[:, u, :, P:P + 4], 1.0, None, ALU.mult).then_inc(s_st2, 1)

            def last_stats():
                stats_of_h(GROUPS - 2, 0)
                stats_of_h(GROUPS - 1, 1)

            run_pairs(dve, GROUPS, body2, None, last_stats)
            dve.wait_ge(s_st2, GROUPS)
            for t in range(TILES):
                last = D.bn_aggr(mv2[:, t, :], st2[:, t, :])
            last.then_inc(s_mv2, 1)

            def per_e(ap):
                return ap.unsqueeze(1).to_broadcast([P, TILES, 4])

            def per_t(ap):
                return ap.unsqueeze(2).to_broadcast([P, TILES, 4])

            dve.wait_ge(s_sd2, 1)
            link(D.reciprocal(rs2[:, :], sd2[:, :]))
            link(D.tensor_tensor(f.lg[:, 0, :, :], f.lg[:, 1, :, :], per_t(rs2[:, :]), ALU.mult))
            link(D.tensor_tensor(f.lg[:, 1, :, :], f.lg[:, 0, :, :], per_e(g.rw_sum[:, :]), ALU.add))
            link(D.tensor_reduce(f.lt[:, 0, :], f.lg[:, 1, :, :], AX, ALU.max))
            D.tensor_tensor(f.lg[:, 2, :, :], f.lg[:, 1, :, :], per_t(f.lt[:, 0, :]), ALU.subtract).then_inc(s_ex, 1)

        @block.tensor
        def _(pe):
            T = nc.tensor

            def body(n, u):
                pe.wait_ge(s_y, n + 1)
                wait(pe, s_x2, n - 1)
                for i in range(4):
                    last = T.transpose(ps_y[:, u, i * P:(i + 1) * P], yT[:, u, i * P:(i + 1) * P], g.ident[:, :])
                last.then_inc(s_yt, 1)

            pe.wait_ge(s_rw, 1)
            pe.wait_ge(s_cen, 2)
            T.matmul(ps_n[:, 0, 0:4], centre[:, :], g.rw[:, 0:4], start=True, stop=True)
            T.matmul(ps_n[:, 0, 8:12], g.ones[:, :], g.rw[:, 4:8], start=True, stop=True).then_inc(s_sum, 1)
            run_pairs(pe, GROUPS, body)

            def turn_back(n, u):
                pe.wait_ge(s_hT, n + 1)
                wait(pe, s_st2, n - 1)
                for i in range(4):
                    last = T.matmul(ps_c[:, u, i, 0:P + 4], hT[:, u, i * P:(i + 1) * P], back[:, :], start=True, stop=True)
                last.then_inc(s_back, 1)

            def body2(n, u):
                pe.wait_ge(s_n2, n + 1)
                wait(pe, s_hT, n - 1)
                for i in range(4):
                    last = T.transpose(ps_n[:, u, i * P:(i + 1) * P], n2[:, u, i, :], g.ident[:, :])
                last.then_inc(s_nt, 1)
                if not isinstance(n, int) or n > 0:
                    turn_back(n - 1, 1 - u)

            run_pairs(pe, GROUPS, body2, None, lambda: turn_back(GROUPS - 1, 1))


def experts_stage(nc, g, f):
    B, L = g.B, g.L
    GROUPS = B * L // 512
    GPB = L // 512
    TILES = 4 * GROUPS
    lg, lt, cmp_ = f.lg, f.lt, f.cmp
    with ExitStack() as ctx:
        def sb(name, shape, dt=F32):
            return ctx.enter_context(nc.sbuf_tensor(name, shape, dt))

        def sem(name):
            return ctx.enter_context(nc.semaphore(name))

        gate_chain = sem("e_gate_chain")
        hTs = sb("e_hTs", [P, 2, 2, 512], F32R)
        st3 = sb("e_st3", [P, 2, 4, 6])
        mv3 = sb("e_mv3", [P, 2, 4, 2])
        sd3 = sb("e_sd3", [P, 2, 4])
        rs3 = sb("e_rs3", [P, 2, 4])
        nb3 = sb("e_nb3", [P, 2, 4])
        hn = sb("e_hn", [P, 2, 4, 8, P])
        rT = sb("e_rT", [P, 2, 8, 512])
        o = sb("e_o", [P, 2, 4, P])
        st4 = sb("e_st4", [P, 4, 6])
        mv4 = sb("e_mv4", [P, 4, 2])
        sd4 = sb("e_sd4", [P, 4])
        rs4 = sb("e_rs4", [P, 4])
        c4 = sb("e_c4", [P, 4, P])
        n4 = sb("e_n4", [P, 4, P])
        t4 = sb("e_t4", [P, 4, P])
        t5 = sb("e_t5", [P, 4, P])
        res = sb("e_res", [P, 4, P])
        zero = sb("e_zero", [1, 1])
        spot = sb("e_spot", [1, 4, 4 * GROUPS])

        ps_h = ctx.enter_context(nc.psum_tensor("ps_h", [P, 2, 4, 256], F32))
        ps_t = ctx.enter_context(nc.psum_tensor("ps_t", [P, 2, 512], F32))
        ps_e = ctx.enter_context(nc.psum_tensor("ps_e", [P, 2, 4, P], F32))

        h_in = [sem("e_h_in0"), sem("e_h_in1")]
        hid, stat, aggr, root, inv, shift, normed = (sem("e_hid"), sem("e_stat"), sem("e_aggr"), sem("e_root"), sem("e_inv"),
                                                     sem("e_shift"), sem("e_normed"))
        turned, relu, outs, gated = sem("e_turned"), sem("e_relu"), sem("e_outs"), sem("e_gated")
        stat4, aggr4, root4, inv4, c4_done, n4_done, t4_done, t5_done, res_done = (
            sem("e_stat4"), sem("e_aggr4"), sem("e_root4"), sem("e_inv4"), sem("e_c4_done"), sem("e_n4_done"), sem("e_t4_done"),
            sem("e_t5_done"), sem("e_res_done"))
        stored, ready, last_done = sem("e_stored"), sem("e_ready"), sem("e_last_done")

        ov = g.out.rearrange("b l e -> (b l) e").rearrange("(t p) e -> p t e", p=P)

        def has(n):
            return not isinstance(n, int) or 0 <= n < GROUPS

        def run(eng, body):
            body(0, 0)
            body(1, 1)
            body(2, 0)
            body(3, 1)
            with eng.Fori(2, GROUPS // 2) as j:
                body(2 * j, 0)
                body(2 * j + 1, 1)
            body(GROUPS, 0)
            body(GROUPS + 1, 1)

        block = ctx.enter_context(nc.Block())

        @block.sync
        def _(sp):
            def load(n):
                if n >= 4:
                    sp.wait_ge(hid, 4 * n - 4)
                for part, h in enumerate((f.hT2_hi, f.hT2_lo)):
                    sp.dma_start(hTs[:, n % 2, part, :].bitcast(F32), h[:, 512 * n:512 * n + 512].bitcast(F32)).then_inc(h_in[n % 2], 16)

            def store(m):
                sp.wait_ge(res_done, m + 1)
                sp.dma_start(ov[:, 4 * m:4 * m + 4, :], res[:, :, :]).then_inc(stored, 16)

            for n in range(2, 6):
                load(n)
            for m in range(GROUPS):
                if m + 5 in (6, 7):
                    load(m + 5)
                if m < GROUPS - 1:
                    store(m)
            sp.wait_ge(last_done, 4)
            sp.dma_start(ov[:, 4 * GROUPS - 4:4 * GROUPS, :], o[:, 1, :, :]).then_inc(stored, 16)
            sp.wait_ge(stored, 16 * GROUPS)

        @block.gpsimd
        def _(pool):
            G = nc.gpsimd

            def body(n, u):
                if has(n - 3):
                    finish(n - 3, 1 - u)

            def per_tile(ap):
                return ap.unsqueeze(2).to_broadcast([P, 4, P])

            def finish(m, u):
                b = m // GPB
                pool.wait_ge(inv4, m + 1)
                G.tensor_tensor(c4[:, :, :], o[:, u, :, :], per_tile(mv4[:, :, 0]), ALU.subtract).then_inc(c4_done, 1)
                pool.wait_ge(c4_done, m + 1)
                G.tensor_tensor(n4[:, :, :], c4[:, :, :], per_tile(rs4[:, :]), ALU.mult).then_inc(n4_done, 1)
                pool.wait_ge(n4_done, m + 1)
                G.tensor_tensor(t4[:, :, :], n4[:, :, :], g.mod_rep[:, 2, at(b, 1), :].to_broadcast([P, 4, P]), ALU.mult).then_inc(t4_done, 1)
                pool.wait_ge(t4_done, m + 1)
                G.tensor_tensor(t5[:, :, :], t4[:, :, :], g.mod_rep[:, 3, at(b, 1), :].to_broadcast([P, 4, P]), ALU.add).then_inc(t5_done, 1)
                pool.wait_ge(t5_done, m + 1)
                wait(pool, stored, 16 * m)
                G.tensor_tensor(res[:, :, :], t5[:, :, :], f.x2[:, at(4 * m, 4), :], ALU.add).then_inc(res_done, 1)

            run(pool, body)

        @block.scalar
        def _(act):
            A = nc.scalar

            def relu_of(m, u, chunks):
                for c in chunks:
                    act.wait_ge(turned, 8 * m + c + 1)
                    wait(act, outs, 4 * m - 4)
                    A.activation(rT[:, u, c, :], ps_t[:, c % 2, :], ACT.Relu, bias=g.vecT[:, C_LNB + c:C_LNB + c + 1],
                                 scale=g.vecT[:, C_LNG + c:C_LNG + c + 1]).then_inc(relu, 1)

            def normalise(n, u, i):
                act.wait_ge(shift, 4 * n + i + 1)
                wait(act, turned, 8 * n - 8)
                for e in range(4):
                    last = A.activation(flat(hn[:, u, i, 2 * e:2 * e + 2, :]), ps_h[:, i % 2, e, :], ACT.Identity,
                                        scale=rs3[:, i % 2, e:e + 1], bias=nb3[:, i % 2, e:e + 1])
                last.then_inc(normed, 1)

            def body(n, u):
                for i in range(4):
                    m, v, c = (n - 2, u, 6) if i == 0 else (n - 1, 1 - u, 2 * i - 2)
                    if has(m):
                        relu_of(m, v, (c, c + 1))
                    if i == 2 and has(n - 3):
                        root_of_output(n - 3)
                    m, v, t = (n - 1, 1 - u, 3) if i == 0 else (n, u, i - 1)
                    if has(m):
                        normalise(m, v, t)
                    if has(n):
                        k = 4 * n + i
                        act.wait_ge(aggr, k + 1)
                        wait(act, inv, k - 1)
                        A.activation(sd3[:, i % 2, :], mv3[:, i % 2, :, 1], ACT.Sqrt, bias=g.eps[:, 0:1]).then_inc(root, 1)

            def root_of_output(m):
                act.wait_ge(aggr4, m + 1)
                wait(act, inv4, m)
                A.activation(sd4[:, :], mv4[:, :, 1], ACT.Sqrt, bias=g.eps[:, 0:1]).then_inc(root4, 1)

            run(act, body)
            root_of_output(GROUPS - 1)

        @block.vector
        def _(dve):
            D = nc.vector

            pr = lg[:, 1, :, :]
            c0, c1 = (cmp_[:, k, :, :, :].rearrange("p t e j -> p (t e j)") for k in range(2))
            links = [0]

            def link(ins):
                links[0] += 1
                ins.then_inc(gate_chain, 1)
                dve.wait_ge(gate_chain, links[0])

            def per_t(ap):
                return ap.unsqueeze(2).to_broadcast([P, TILES, 4])

            def gates(part):
                if part == 0:
                    link(D.tensor_reduce(lt[:, 1, :], lg[:, 3, :, :], AX, ALU.add))
                    link(D.reciprocal(lt[:, 2, :], lt[:, 1, :]))
                    link(D.tensor_tensor(pr, lg[:, 3, :, :], per_t(lt[:, 2, :]), ALU.mult))
                elif part in (1, 2):
                    for e in (0, 1) if part == 1 else (2, 3):
                        one = lg[:, 1, :, e:e + 1].to_broadcast([P, TILES, 4])
                        D.tensor_tensor(cmp_[:, 0, :, e, :], pr, one, ALU.is_ge)
                        last = D.tensor_tensor(cmp_[:, 1, :, e, :], pr, one, ALU.is_gt)
                    link(last)
                elif part == 3:
                    for k in range(2):
                        t = f.tri[:, k:k + 1, :, :].rearrange("p a e j -> p a (e j)").to_broadcast([P, TILES, 16])
                        ck = cmp_[:, k, :, :, :].rearrange("p t e j -> p t (e j)")
                        last = D.tensor_tensor(ck, ck, t, ALU.mult)
                    link(last)
                elif part == 4:
                    link(D.tensor_tensor(c0, c0, c1, ALU.add))
                    link(D.tensor_reduce(lg[:, 0, :, :], cmp_[:, 0, :, :, :], AX, ALU.add))
                elif part == 5:
                    link(D.scalar_tensor_tensor(flat(lg[:, 2, :, :]), flat(lg[:, 0, :, :]), 2.0, flat(pr), op0=ALU.is_lt, op1=ALU.mult))
                    link(D.tensor_reduce(lt[:, 3, :], lg[:, 2, :, :], AX, ALU.add))
                elif part == 6:
                    link(D.tensor_scalar_add(lt[:, 0, :], lt[:, 3, :], EPS_GATE))
                    link(D.reciprocal(lt[:, 1, :], lt[:, 0, :]))
                    link(D.tensor_tensor(f.gate[:, :, :], lg[:, 2, :, :], per_t(lt[:, 1, :]), ALU.mult))

            def gated_sum(m, u, i, experts):
                for e in experts:
                    gate = f.gate[:, at(4 * m + i, 1), e]
                    if e == 0:
                        dve.wait_ge(outs, 4 * m + i + 1)
                        if i == 0:
                            wait(dve, c4_done, m - 1)
                        D.tensor_scalar(o[:, u, i, :], ps_e[:, i % 2, e, :], gate, None, ALU.mult).then_inc(gated, 1)
                    else:
                        dve.wait_ge(gated, 16 * m + 4 * i + e)
                        D.scalar_tensor_tensor(o[:, u, i, :], ps_e[:, i % 2, e, :], gate, o[:, u, i, :],
                                               op0=ALU.mult, op1=ALU.add).then_inc(gated, 1)

            def output_stats(m, u):
                dve.wait_ge(gated, 16 * (m + 1))
                carry(D, spot, zero, 2, m)
                for t in range(4):
                    last = D.bn_stats(st4[:, t, :], o[:, u, t, :])
                last.then_inc(stat4, 1)

            def output_aggr(m):
                wait(dve, n4_done, m)
                dve.wait_ge(stat4, m + 1)
                carry(D, spot, zero, 3, m)
                for t in range(4):
                    last = D.bn_aggr(mv4[:, t, :], st4[:, t, :])
                last.then_inc(aggr4, 1)

            def finish_last(m):
                last_o, b = o[:, 1, :, :], m // GPB
                dve.wait_ge(inv4, m + 1)
                for t in range(4):
                    ins = D.tensor_scalar(o[:, 1, t, :], o[:, 1, t, :], mv4[:, t, 0:1], rs4[:, t:t + 1], ALU.subtract, ALU.mult)
                ins.then_inc(last_done, 1)
                dve.wait_ge(last_done, 1)
                D.tensor_tensor(last_o, last_o, g.mod_rep[:, 2, b:b + 1, :].to_broadcast([P, 4, P]), ALU.mult).then_inc(last_done, 1)
                dve.wait_ge(last_done, 2)
                D.tensor_tensor(last_o, last_o, g.mod_rep[:, 3, b:b + 1, :].to_broadcast([P, 4, P]), ALU.add).then_inc(last_done, 1)
                dve.wait_ge(last_done, 3)
                D.tensor_tensor(last_o, last_o, f.x2[:, 4 * m:4 * m + 4, :], ALU.add).then_inc(last_done, 1)

            def output_rs(m):
                dve.wait_ge(root4, m + 1)
                D.reciprocal(rs4[:, :], sd4[:, :]).then_inc(inv4, 1)

            def body(n, u):
                for i in range(4):
                    k = 4 * n + i
                    tile = (n - 3, 1 - u, 3) if i == 0 else (n - 2, u, i - 1)
                    if has(n):
                        dve.wait_ge(hid, k + 1)
                        carry(D, spot, zero, 0, k)
                        for e in range(4):
                            last = D.bn_stats(st3[:, i % 2, e, :], ps_h[:, i % 2, e, :])
                        last.then_inc(stat, 1)
                    if has(tile[0]):
                        gated_sum(*tile, (0,))
                    if has(n):
                        dve.wait_ge(stat, k + 1)
                        carry(D, spot, zero, 1, k)
                        for e in range(4):
                            last = D.bn_aggr(mv3[:, i % 2, e, :], st3[:, i % 2, e, :])
                        last.then_inc(aggr, 1)
                    if has(tile[0]):
                        gated_sum(*tile, (1, 2))
                    if has(n):
                        dve.wait_ge(root, k + 1)
                        wait(dve, normed, k - 1)
                        D.reciprocal(rs3[:, i % 2, :], sd3[:, i % 2, :]).then_inc(inv, 1)
                    if has(tile[0]):
                        gated_sum(*tile, (3,))
                    if has(n):
                        dve.wait_ge(inv, k + 1)
                        D.scalar_tensor_tensor(nb3[:, i % 2, :], mv3[:, i % 2, :, 0], -1.0, rs3[:, i % 2, :],
                                               op0=ALU.mult, op1=ALU.mult).then_inc(shift, 1)
                    if i == 0 and has(n - 3):
                        output_stats(n - 3, 1 - u)
                    if i == 1 and has(n - 3):
                        output_aggr(n - 3)
                    if i == 3 and has(n - 3):
                        output_rs(n - 3)
                    if isinstance(n, int) and n < 2:
                        gates(4 * n + i)

            D.memset(zero[:, :], 0.0).then_inc(ready, 1)
            dve.wait_ge(ready, 1)
            run(dve, body)
            gated_sum(GROUPS - 1, 1, 3, range(4))
            output_stats(GROUPS - 1, 1)
            output_aggr(GROUPS - 1)
            output_rs(GROUPS - 1)
            finish_last(GROUPS - 1)

        @block.tensor
        def _(pe):
            T = nc.tensor
            pe.wait_ge(f.s_w, 32)

            def outputs(m, u, i):
                if i == 0:
                    pe.wait_ge(relu, 8 * m + 8)
                wait(pe, gated, 16 * m + 4 * i - 4)
                for e in range(4):
                    for a in range(2):
                        last = T.matmul(ps_e[:, i % 2, e, :], rT[:, u, 2 * e + a, i * P:(i + 1) * P], f.w2[:, 2 * e + a, :],
                                        start=(a == 0), stop=(a == 1))
                last.then_inc(outs, 1)

            def turns(m, u, i):
                if i == 0:
                    pe.wait_ge(normed, 4 * m + 4)
                for c in (2 * i, 2 * i + 1):
                    wait(pe, relu, 8 * m + c - 1)
                    for t in range(4):
                        last = T.transpose(ps_t[:, c % 2, t * P:(t + 1) * P], hn[:, u, t, c, :], g.ident[:, :])
                    last.then_inc(turned, 1)

            def body(n, u):
                for i in range(4):
                    if has(n):
                        if isinstance(n, int) and n < 2:
                            h_hi, h_lo = (h[:, 512 * n + i * P:512 * n + (i + 1) * P] for h in (f.hT2_hi, f.hT2_lo))
                        else:
                            h_hi, h_lo = (hTs[:, u, part, i * P:(i + 1) * P] for part in range(2))
                            if i == 0:
                                pe.wait_ge(h_in[u], 32 * (n // 2))
                        wait(pe, normed, 4 * n + i - 1)
                        for a in range(2):
                            bank = flat(ps_h[:, i % 2, 2 * a:2 * a + 2, :])
                            w_hi, w_lo = flat(f.w1_hi[:, 2 * a:2 * a + 2, :]), flat(f.w1_lo[:, 2 * a:2 * a + 2, :])
                            T.matmul(bank, h_hi, w_hi, start=True, stop=False)
                            T.matmul(bank, h_hi, w_lo, start=False, stop=False)
                            last = T.matmul(bank, h_lo, w_hi, start=False, stop=True)
                        last.then_inc(hid, 1)
                    if has(n - 2):
                        outputs(n - 2, u, i)
                    if has(n - 1):
                        turns(n - 1, 1 - u, i)

            run(pe, body)


def ffn_stage(nc, g):
    B, L = g.B, g.L
    TILES = B * L // P
    with ExitStack() as ctx:
        f = Shared()

        def sb(name, shape, dt=F32):
            return ctx.enter_context(nc.sbuf_tensor(name, shape, dt))

        f.w1 = sb("w1s", [P, 4, 256])
        f.w1_hi = sb("w1_hi", [P, 4, 256], F32R)
        f.w1_lo = sb("w1_lo", [P, 4, 256], F32R)
        f.w2 = sb("w2s", [P, 8, P])
        f.x2 = g.hT[:, :].rearrange("p (t e) -> p t e", e=P)
        f.hT2_hi = sb("hT2_hi", [P, B * L], F32R)
        f.hT2_lo = sb("hT2_lo", [P, B * L], F32R)
        f.gate = sb("gate", [P, TILES, 4])
        f.lg = sb("f_lg", [P, 4, TILES, 4])
        f.lt = sb("f_lt", [P, 4, TILES])
        f.cmp = sb("f_cmp", [P, 2, TILES, 4, 4])
        f.tri = sb("f_tri", [P, 2, 4, 4])
        f.s_w = ctx.enter_context(nc.semaphore("w_in"))
        router_stage(nc, g, f)
        experts_stage(nc, g, f)


_INS = ['L0_attn_X', 'L0_attn_W_qkv', 'L0_attn_b_qkv', 'L0_attn_W_fc', 'L0_attn_b_fc', 'L0_ffn_router_w', 'L0_ffn_rn_g',
        'L0_ffn_rn_b', 'L0_ffn_w1', 'L0_ffn_ln_g', 'L0_ffn_ln_b', 'L0_ffn_w2', 'L0_ffn_on_g', 'L0_ffn_on_b', 'L0_c', 'L0_wmod']


def kernel(**inputs):
    import numpy as np
    import concourse.bacc as bacc
    from concourse.bass_utils import run_bass_kernel_spmd

    nc = bacc.Bacc("TRN2", target_bir_lowering=False, num_devices=1)
    arrays, args = {}, []
    for name in _INS:
        a = np.ascontiguousarray(inputs[name])
        arrays[f"in_{name}"] = a
        args.append(nc.dram_tensor(f"in_{name}", a.shape, mybir.dt.from_np(a.dtype), kind="ExternalInput").ap())
    args.append(nc.dram_tensor("out_0", inputs['L0_attn_X'].shape, F32, kind="ExternalOutput").ap())
    build(nc, *args)
    r = run_bass_kernel_spmd(nc, [arrays], core_ids=[0])
    return r.results[0]["out_0"]
```
